# Optimizing a Trainium2 kernel written in Bass

```python
import numpy as np
import jax
import jax.numpy as jnp

def _softmax(x, axis=-1):
    return jax.nn.softmax(x, axis=axis)

def _gelu(x):
    return jax.nn.gelu(x, approximate=True)

def _silu(x):
    return jax.nn.silu(x)

def _sigmoid(x):
    return jax.nn.sigmoid(x)

def _layernorm(x, axis=-1, eps=1e-05):
    m = jnp.mean(x, axis=axis, keepdims=True)
    v = jnp.var(x, axis=axis, keepdims=True)
    return (x - m) / jnp.sqrt(v + eps)

def _scatter_add(tgt, idx, src, axis=0):
    return tgt.at[idx].add(src)

def _segment_sum(src, seg, n):
    return jax.ops.segment_sum(src, seg, n)
kernel_name = 'mk_gnn_ffn_d2_gnn_r16_1f9b7b'

def setup_inputs(seed: int=0):
    np.random.seed(seed)
    _w = jnp.asarray

    def _rec_inputs():
        import jax
        import jax.numpy as jnp
        _gk = jax.random.key(seed)
        x = -0.000364 + 1 * jax.random.normal(jax.random.fold_in(_gk, 1), (625, 768), jnp.float32)
        src = jax.random.randint(jax.random.fold_in(_gk, 2), (10000,), 0, 625, jnp.int32)
        dst = jax.random.randint(jax.random.fold_in(_gk, 3), (10000,), 0, 625, jnp.int32)
        _o = jnp.argsort(dst, stable=True)
        src = src[_o]
        dst = dst[_o]
        edge_type_34 = jax.random.randint(jax.random.fold_in(_gk, 12), (10000,), 0, 34, jnp.int32)
        return (x, src, dst, edge_type_34)
    x, src, dst, edge_type_34 = _rec_inputs()

    def _L0_gnn_setup():
        import jax, jax.numpy as jnp
        import numpy as np
        N = 1250
        E_RAND = 20000
        NEG_SLOPE = 0.2

        def gat_layer(x, W, a_src, a_dst, bias, src, dst, heads, out_c, concat):
            n = x.shape[0]
            h = (x @ W).reshape(n, heads, out_c)
            al_s = jnp.einsum('nhc,hc->nh', h, a_src)
            al_d = jnp.einsum('nhc,hc->nh', h, a_dst)
            e = jax.nn.leaky_relu(al_s[src] + al_d[dst], NEG_SLOPE)
            m = jax.ops.segment_max(e, dst, num_segments=n)
            ex = jnp.exp(e - m[dst])
            z = jax.ops.segment_sum(ex, dst, num_segments=n)
            alpha = ex / (z[dst] + 1e-16)
            msg = h[src] * alpha[:, :, None]
            out = jax.ops.segment_sum(msg, dst, num_segments=n)
            out = out.reshape(n, heads * out_c) if concat else out.mean(axis=1)
            return out + bias
        key = jax.random.key(seed)
        ks = jax.random.split(key, 10)
        x = jax.random.normal(ks[0], (N, 768), dtype=jnp.float32)
        src = jax.random.randint(ks[1], (E_RAND,), 0, N)
        dst = jax.random.randint(ks[2], (E_RAND,), 0, N)
        loop = jnp.arange(N)
        edge_index = jnp.stack([jnp.concatenate([src, loop]), jnp.concatenate([dst, loop])])
        s = 1.0 / np.sqrt(768.0)
        W1 = jax.random.normal(ks[3], (768, 768), dtype=jnp.float32) * s
        a_src1 = jax.random.normal(ks[4], (8, 96), dtype=jnp.float32) * 0.1
        a_dst1 = jax.random.normal(ks[5], (8, 96), dtype=jnp.float32) * 0.1
        b1 = jnp.zeros((768,), dtype=jnp.float32)
        W2 = jax.random.normal(ks[6], (768, 768), dtype=jnp.float32) * s
        a_src2 = jax.random.normal(ks[7], (1, 768), dtype=jnp.float32) * 0.1
        a_dst2 = jax.random.normal(ks[8], (1, 768), dtype=jnp.float32) * 0.1
        b2 = jnp.zeros((768,), dtype=jnp.float32)
        return {'x': x, 'edge_index': edge_index, 'W1': W1, 'a_src1': a_src1, 'a_dst1': a_dst1, 'b1': b1, 'W2': W2, 'a_src2': a_src2, 'a_dst2': a_dst2, 'b2': b2}
    _L0_gnn_all = _L0_gnn_setup()
    _L0_gnn_in = {k: v for k, v in _L0_gnn_all.items() if k in ('W1', 'a_src1', 'a_dst1', 'b1', 'W2', 'a_src2', 'a_dst2', 'b2')}
    del _L0_gnn_all

    def _L0_ffn_setup():
        import jax, jax.numpy as jnp
        import numpy as np
        E, C, F, K = (8, 768, 192, 2)
        key = jax.random.key(seed)
        k0, k1, k2, k3 = jax.random.split(key, 4)
        B, T = (8, 128)
        return {'x': jax.random.normal(k0, (B, T, C), jnp.float32), 'router_w': jax.random.normal(k1, (E, C), jnp.float32) * 0.02, 'w1': jax.random.normal(k2, (E, C, F), jnp.float32) * 0.02, 'b1': jnp.zeros((E, F), jnp.float32), 'w2': jax.random.normal(k3, (E, F, C), jnp.float32) * 0.02, 'b2': jnp.zeros((E, C), jnp.float32)}
    _L0_ffn_all = _L0_ffn_setup()
    _L0_ffn_in = {k: v for k, v in _L0_ffn_all.items() if k in ('router_w', 'w1', 'b1', 'w2', 'b2')}
    del _L0_ffn_all

    def _L1_gnn_setup():
        import jax, jax.numpy as jnp
        import numpy as np
        N_NODES = 625
        N_EDGES = 6250
        N_REL = 34
        DIM = 768

        def _graph_encoder(x, edge_index, edge_type, W_rel, W_root, b_rgcn, W_gcn, b_gcn):
            n = x.shape[0]
            src, dst = (edge_index[0], edge_index[1])
            ones = jnp.ones((src.shape[0],), dtype=x.dtype)
            seg = edge_type * n + dst
            agg = jax.ops.segment_sum(x[src], seg, num_segments=N_REL * n)
            cnt = jax.ops.segment_sum(ones, seg, num_segments=N_REL * n)
            mean = agg.reshape(N_REL, n, -1) / jnp.maximum(cnt, 1.0).reshape(N_REL, n, 1)
            h1 = jnp.einsum('rni,rio->no', mean, W_rel) + x @ W_root + b_rgcn
            xw = h1 @ W_gcn
            deg = jax.ops.segment_sum(ones, dst, num_segments=n) + 1.0
            dinv = jax.lax.rsqrt(deg)
            norm = dinv[src] * dinv[dst]
            out = jax.ops.segment_sum(xw[src] * norm[:, None], dst, num_segments=n)
            out = out + xw * (dinv * dinv)[:, None]
            return out + b_gcn
        key = jax.random.key(seed)
        ks = jax.random.split(key, 6)
        scale = 1.0 / np.sqrt(DIM)
        x = jax.random.normal(ks[0], (N_NODES, DIM), dtype=jnp.float32)
        edge_index = jax.random.randint(ks[1], (2, N_EDGES), 0, N_NODES, dtype=jnp.int32)
        edge_type = jax.random.randint(ks[2], (N_EDGES,), 0, N_REL, dtype=jnp.int32)
        W_rel = jax.random.normal(ks[3], (N_REL, DIM, DIM), dtype=jnp.float32) * scale
        W_root = jax.random.normal(ks[4], (DIM, DIM), dtype=jnp.float32) * scale
        b_rgcn = jnp.zeros((DIM,), dtype=jnp.float32)
        W_gcn = jax.random.normal(ks[5], (DIM, DIM), dtype=jnp.float32) * scale
        b_gcn = jnp.zeros((DIM,), dtype=jnp.float32)
        return {'x': x, 'edge_index': edge_index, 'edge_type': edge_type, 'W_rel': W_rel, 'W_root': W_root, 'b_rgcn': b_rgcn, 'W_gcn': W_gcn, 'b_gcn': b_gcn}
    _L1_gnn_all = _L1_gnn_setup()
    _L1_gnn_in = {k: v for k, v in _L1_gnn_all.items() if k in ('W_rel', 'W_root', 'b_rgcn', 'W_gcn', 'b_gcn')}
    del _L1_gnn_all

    def _L1_ffn_setup():
        import jax, jax.numpy as jnp
        import numpy as np
        B, T, C, H, E, TOPK, DR = (2, 128, 768, 192, 8, 2, 24)

        def _normalize(v, axis=-1, eps=1e-12):
            return v / jnp.maximum(jnp.linalg.norm(v, axis=axis, keepdims=True), eps)
        key = jax.random.key(seed)
        ks = jax.random.split(key, 16)
        std = 0.02
        n = lambda k, shape, s=std: (s * jax.random.normal(k, shape)).astype(jnp.float32)
        emb = jax.random.normal(ks[3], (E, DR), dtype=jnp.float32)
        emb = emb / (jnp.linalg.norm(emb, axis=-1, keepdims=True) + 1e-08)
        return {'x': jax.random.normal(ks[0], (B, T, C), dtype=jnp.float32), 'router_w': n(ks[1], (E, C)), 'probe_w': n(ks[2], (DR, C)), 'router_emb': emb, 'fatigue': jnp.zeros((E,), jnp.float32), 'energy': jnp.ones((E,), jnp.float32), 'w_fast1': n(ks[4], (E, C, H)), 'w_slow1': n(ks[5], (E, C, H)), 'h_fast1': n(ks[6], (E, C, H), 0.005), 'm_gate1': jax.random.uniform(ks[7], (E,), dtype=jnp.float32), 'b1': jnp.zeros((E, H), jnp.float32), 'w_fast2': n(ks[8], (E, H, C)), 'w_slow2': n(ks[9], (E, H, C)), 'h_fast2': n(ks[10], (E, H, C), 0.005), 'm_gate2': jax.random.uniform(ks[11], (E,), dtype=jnp.float32), 'b2': jnp.zeros((E, C), jnp.float32)}
    _L1_ffn_all = _L1_ffn_setup()
    _L1_ffn_in = {k: v for k, v in _L1_ffn_all.items() if k in ('router_w', 'probe_w', 'router_emb', 'fatigue', 'energy', 'w_fast1', 'w_slow1', 'h_fast1', 'm_gate1', 'b1', 'w_fast2', 'w_slow2', 'h_fast2', 'm_gate2', 'b2')}
    del _L1_ffn_all
    return {'x': x, 'src': src, 'dst': dst, 'edge_type_34': edge_type_34, 'L0_gnn_W1': _L0_gnn_in['W1'], 'L0_gnn_a_src1': _L0_gnn_in['a_src1'], 'L0_gnn_a_dst1': _L0_gnn_in['a_dst1'], 'L0_gnn_b1': _L0_gnn_in['b1'], 'L0_gnn_W2': _L0_gnn_in['W2'], 'L0_gnn_a_src2': _L0_gnn_in['a_src2'], 'L0_gnn_a_dst2': _L0_gnn_in['a_dst2'], 'L0_gnn_b2': _L0_gnn_in['b2'], 'L0_ffn_router_w': _L0_ffn_in['router_w'], 'L0_ffn_w1': _L0_ffn_in['w1'], 'L0_ffn_b1': _L0_ffn_in['b1'], 'L0_ffn_w2': _L0_ffn_in['w2'], 'L0_ffn_b2': _L0_ffn_in['b2'], 'L1_gnn_W_rel': _L1_gnn_in['W_rel'], 'L1_gnn_W_root': _L1_gnn_in['W_root'], 'L1_gnn_b_rgcn': _L1_gnn_in['b_rgcn'], 'L1_gnn_W_gcn': _L1_gnn_in['W_gcn'], 'L1_gnn_b_gcn': _L1_gnn_in['b_gcn'], 'L1_ffn_router_w': _L1_ffn_in['router_w'], 'L1_ffn_probe_w': _L1_ffn_in['probe_w'], 'L1_ffn_router_emb': _L1_ffn_in['router_emb'], 'L1_ffn_fatigue': _L1_ffn_in['fatigue'], 'L1_ffn_energy': _L1_ffn_in['energy'], 'L1_ffn_w_fast1': _L1_ffn_in['w_fast1'], 'L1_ffn_w_slow1': _L1_ffn_in['w_slow1'], 'L1_ffn_h_fast1': _L1_ffn_in['h_fast1'], 'L1_ffn_m_gate1': _L1_ffn_in['m_gate1'], 'L1_ffn_b1': _L1_ffn_in['b1'], 'L1_ffn_w_fast2': _L1_ffn_in['w_fast2'], 'L1_ffn_w_slow2': _L1_ffn_in['w_slow2'], 'L1_ffn_h_fast2': _L1_ffn_in['h_fast2'], 'L1_ffn_m_gate2': _L1_ffn_in['m_gate2'], 'L1_ffn_b2': _L1_ffn_in['b2']}

def reference(x, src, dst, edge_type_34, L0_gnn_W1, L0_gnn_a_src1, L0_gnn_a_dst1, L0_gnn_b1, L0_gnn_W2, L0_gnn_a_src2, L0_gnn_a_dst2, L0_gnn_b2, L0_ffn_router_w, L0_ffn_w1, L0_ffn_b1, L0_ffn_w2, L0_ffn_b2, L1_gnn_W_rel, L1_gnn_W_root, L1_gnn_b_rgcn, L1_gnn_W_gcn, L1_gnn_b_gcn, L1_ffn_router_w, L1_ffn_probe_w, L1_ffn_router_emb, L1_ffn_fatigue, L1_ffn_energy, L1_ffn_w_fast1, L1_ffn_w_slow1, L1_ffn_h_fast1, L1_ffn_m_gate1, L1_ffn_b1, L1_ffn_w_fast2, L1_ffn_w_slow2, L1_ffn_h_fast2, L1_ffn_m_gate2, L1_ffn_b2):
    import jax
    import jax.numpy as jnp

    def _L0_gnn_ref(x, edge_index, W1, a_src1, a_dst1, b1, W2, a_src2, a_dst2, b2):
        import jax, jax.numpy as jnp
        import numpy as np
        N = 1250
        E_RAND = 20000
        NEG_SLOPE = 0.2

        def gat_layer(x, W, a_src, a_dst, bias, src, dst, heads, out_c, concat):
            n = x.shape[0]
            h = (x @ W).reshape(n, heads, out_c)
            al_s = jnp.einsum('nhc,hc->nh', h, a_src)
            al_d = jnp.einsum('nhc,hc->nh', h, a_dst)
            e = jax.nn.leaky_relu(al_s[src] + al_d[dst], NEG_SLOPE)
            m = jax.ops.segment_max(e, dst, num_segments=n)
            ex = jnp.exp(e - m[dst])
            z = jax.ops.segment_sum(ex, dst, num_segments=n)
            alpha = ex / (z[dst] + 1e-16)
            msg = h[src] * alpha[:, :, None]
            out = jax.ops.segment_sum(msg, dst, num_segments=n)
            out = out.reshape(n, heads * out_c) if concat else out.mean(axis=1)
            return out + bias
        src, dst = (edge_index[0], edge_index[1])
        h = gat_layer(x, W1, a_src1, a_dst1, b1, src, dst, heads=8, out_c=96, concat=True)
        h = jax.nn.elu(h)
        out = gat_layer(h, W2, a_src2, a_dst2, b2, src, dst, heads=1, out_c=768, concat=False)
        return out

    def _L0_ffn_ref(x, router_w, w1, b1, w2, b2):
        import jax, jax.numpy as jnp
        import numpy as np
        E, C, F, K = (8, 768, 192, 2)
        B, T, Cc = x.shape
        flat = x.reshape(-1, Cc)
        logits = flat @ router_w.T
        probs = jax.nn.softmax(logits.astype(jnp.float32), axis=-1)
        top_w, top_i = jax.lax.top_k(probs, K)
        top_w = (top_w / top_w.sum(-1, keepdims=True)).astype(x.dtype)
        out = jnp.zeros_like(flat)
        for e in range(E):
            w_e = jnp.sum(top_w * (top_i == e), axis=-1)[:, None]
            h = jax.nn.gelu(flat @ w1[e] + b1[e], approximate=False)
            out = out + w_e * (h @ w2[e] + b2[e])
        return out.reshape(B, T, Cc)

    def _L1_gnn_ref(x, edge_index, edge_type, W_rel, W_root, b_rgcn, W_gcn, b_gcn):
        import jax, jax.numpy as jnp
        import numpy as np
        N_NODES = 625
        N_EDGES = 6250
        N_REL = 34
        DIM = 768

        def _graph_encoder(x, edge_index, edge_type, W_rel, W_root, b_rgcn, W_gcn, b_gcn):
            n = x.shape[0]
            src, dst = (edge_index[0], edge_index[1])
            ones = jnp.ones((src.shape[0],), dtype=x.dtype)
            seg = edge_type * n + dst
            agg = jax.ops.segment_sum(x[src], seg, num_segments=N_REL * n)
            cnt = jax.ops.segment_sum(ones, seg, num_segments=N_REL * n)
            mean = agg.reshape(N_REL, n, -1) / jnp.maximum(cnt, 1.0).reshape(N_REL, n, 1)
            h1 = jnp.einsum('rni,rio->no', mean, W_rel) + x @ W_root + b_rgcn
            xw = h1 @ W_gcn
            deg = jax.ops.segment_sum(ones, dst, num_segments=n) + 1.0
            dinv = jax.lax.rsqrt(deg)
            norm = dinv[src] * dinv[dst]
            out = jax.ops.segment_sum(xw[src] * norm[:, None], dst, num_segments=n)
            out = out + xw * (dinv * dinv)[:, None]
            return out + b_gcn
        return _graph_encoder(x, edge_index, edge_type, W_rel, W_root, b_rgcn, W_gcn, b_gcn)

    def _L1_ffn_ref(x, router_w, probe_w, router_emb, fatigue, energy, w_fast1, w_slow1, h_fast1, m_gate1, b1, w_fast2, w_slow2, h_fast2, m_gate2, b2):
        import jax, jax.numpy as jnp
        import numpy as np
        B, T, C, H, E, TOPK, DR = (2, 128, 768, 192, 8, 2, 24)

        def _normalize(v, axis=-1, eps=1e-12):
            return v / jnp.maximum(jnp.linalg.norm(v, axis=axis, keepdims=True), eps)
        Bd, Td, Cd = x.shape
        logits = jnp.einsum('btc,ec->bte', x, router_w)
        tok_proxy = x.mean(axis=-1, keepdims=True)
        router_gain = jnp.linalg.norm(router_emb, axis=-1)
        base_bias = 0.02 * tok_proxy
        gain_bias = 0.02 * tok_proxy * router_gain
        tok_unit = _normalize(jnp.einsum('btc,dc->btd', x, probe_w))
        align_bias = 0.02 * jnp.einsum('btd,ed->bte', tok_unit, _normalize(router_emb))
        logits = logits + base_bias + gain_bias + align_bias + 0.1 * energy - 0.1 * fatigue
        g, idx = jax.lax.top_k(logits, TOPK)
        gates = jax.nn.softmax(g, axis=-1)
        N = Bd * Td
        gates_full = jnp.zeros((N, E), x.dtype).at[jnp.arange(N)[:, None], idx.reshape(N, TOPK)].set(gates.reshape(N, TOPK))
        flat_x = x.reshape(N, Cd)

        def body(acc, p):
            wf1, ws1, hf1, mg1, bb1, wf2, ws2, hf2, mg2, bb2, ge = p
            W1 = wf1 + mg1 * ws1 + hf1
            h = jnp.square(jnp.maximum(flat_x @ W1 + bb1, 0.0))
            W2 = wf2 + mg2 * ws2 + hf2
            y = h @ W2 + bb2
            return (acc + ge[:, None] * y, None)
        out, _ = jax.lax.scan(body, jnp.zeros((N, Cd), x.dtype), (w_fast1, w_slow1, h_fast1, m_gate1, b1, w_fast2, w_slow2, h_fast2, m_gate2, b2, gates_full.T))
        return out.reshape(Bd, Td, Cd)
    edge_index = jnp.stack([src, dst])
    x = x + _L0_gnn_ref(_layernorm(x, axis=-1), edge_index, L0_gnn_W1, L0_gnn_a_src1, L0_gnn_a_dst1, L0_gnn_b1, L0_gnn_W2, L0_gnn_a_src2, L0_gnn_a_dst2, L0_gnn_b2)
    x = x + _L0_ffn_ref(_layernorm(x, axis=-1)[None], L0_ffn_router_w, L0_ffn_w1, L0_ffn_b1, L0_ffn_w2, L0_ffn_b2)[0]
    x = x + _L1_gnn_ref(_layernorm(x, axis=-1), edge_index, edge_type_34, L1_gnn_W_rel, L1_gnn_W_root, L1_gnn_b_rgcn, L1_gnn_W_gcn, L1_gnn_b_gcn)
    x = x + _L1_ffn_ref(_layernorm(x, axis=-1)[None], L1_ffn_router_w, L1_ffn_probe_w, L1_ffn_router_emb, L1_ffn_fatigue, L1_ffn_energy, L1_ffn_w_fast1, L1_ffn_w_slow1, L1_ffn_h_fast1, L1_ffn_m_gate1, L1_ffn_b1, L1_ffn_w_fast2, L1_ffn_w_slow2, L1_ffn_h_fast2, L1_ffn_m_gate2, L1_ffn_b2)[0]
    return x

_drawn_inputs = setup_inputs


def setup_inputs(seed=0):
    import zlib

    import numpy as np

    out = dict(_drawn_inputs(seed))
    spreads = {'L0_gnn_b1': (0.0, 0.1),
     'L0_gnn_b2': (0.0, 0.1),
     'L0_ffn_b1': (0.0, 0.498),
     'L0_ffn_b2': (0.0, 0.1),
     'L1_gnn_b_rgcn': (0.0, 0.1),
     'L1_gnn_b_gcn': (0.0, 0.1),
     'L1_ffn_fatigue': (0.0, 0.8),
     'L1_ffn_energy': (1.0, 0.6),
     'L1_ffn_b1': (0.0, 0.542),
     'L1_ffn_b2': (0.0, 0.1)}
    factors = {'L1_ffn_probe_w': 8.0,
     'L1_ffn_router_emb': 8.0,
     'L1_ffn_h_fast1': 2.769,
     'L1_ffn_h_fast2': 3.358,
     'L1_ffn_m_gate2': 2.778}
    for name, (base, spread) in spreads.items():
        noise = np.random.default_rng([zlib.crc32(name.encode()), seed]).standard_normal(out[name].shape)
        drawn = base * np.exp(spread * noise) if base else spread * noise
        out[name] = jnp.asarray(drawn.astype(out[name].dtype))
    for name, factor in factors.items():
        out[name] = (out[name] * factor).astype(out[name].dtype)
    return out
```

```python
import concourse.bass as bass
from concourse import mybir
from contextlib import ExitStack, contextmanager

FP32, FP16, BF16, I32 = (mybir.dt.float32, mybir.dt.float16, mybir.dt.bfloat16, mybir.dt.int32)
ALU = mybir.AluOpType
ACT = mybir.ActivationFunctionType
AX = mybir.AxisListType

N, C = 625, 768
E_EDGES = 10000
P, NT = 125, 5
PP = P + 1
KC = C // 128
HC = C // 2
EP, EJ = 125, 80
REL = 34
W_SCALE = 64.0
T1 = REL + E_EDGES // 128
T1 += T1 % 2
T2 = (E_EDGES + NT * 127) // 128
T2 += -T2 % 4
MAXT = (E_EDGES + 127) // 128
NEG = -1.0e30
HALF = 313
XW = 2 * HALF
HEADS, HD = 8, 96
T_EARLY = T1 // 3 // 4 * 4
IDX_BUFS = 4
AHEAD = 3
EXP, F, FT = 8, 192, 12


class Tally:

    def __init__(self, sem):
        self.sem, self.base, self.n = sem, 0, 0

    def value(self):
        return self.base + self.n

    def up(self, ins, k=1):
        ins.then_inc(self.sem, k)
        self.n += k
        return ins

    @contextmanager
    def loop(self, i, per, times, first=0):
        start = self.n - first * per
        self.base, self.n = i * per + start, 0
        yield
        assert self.n == per, (self.n, per)
        self.base, self.n = 0, start + per * times


def chain(eng, tally):
    def link(ins):
        tally.up(ins)
        eng.wait_ge(tally.sem, tally.value())
    return link


def bc(ap, shape):
    return ap.to_broadcast(shape)


class Core:

    def __init__(self, nc, ctx, ins, out):
        self.nc, self.ctx, self.ins, self.out = nc, ctx, ins, out
        self.sems = []
        self.dve_chain = Tally(self.sem("dve_chain"))
        self.act_chain = Tally(self.sem("act_chain"))
        self.pool_chain = Tally(self.sem("pool_chain"))
        self.sems = []

    def sem(self, name):
        handle = self.nc.alloc_semaphore(name)
        self.sems.append(handle)
        return handle

    def end_phase(self):
        self.nc.clear_and_free_semaphores(self.sems)
        self.nc.all_engine_barrier()
        self.sems = []

    def sb(self, name, shape, dt, ctx=None):
        return (ctx or self.ctx).enter_context(self.nc.sbuf_tensor(name, shape, dt))

    def pb(self, name, shape, dt=FP32, ctx=None):
        return (ctx or self.ctx).enter_context(self.nc.psum_tensor(name, shape, dt))


def edge_phase(K):
    nc, ins = K.nc, K.ins
    with ExitStack() as ctx:
        sb = lambda n, s, d: K.sb(n, s, d, ctx)
        edges_in = sb("edges_in", [EP, 3, EJ], I32)
        srcf, dstf, etf = (sb(n, [EP, EJ], FP32) for n in ("srcf", "dstf", "etf"))
        bucket = sb("bucket", [EP, EJ], FP32)
        bstep = sb("bstep", [EP, EJ], FP32)
        src1 = sb("src1", [EP, EJ], FP32)
        zero = sb("zero", [128, 1], FP32)
        zero16 = sb("zero16", [EP, 512], FP16)
        iota_n = sb("iota_n", [EP, N], FP16)
        iota_lo = sb("iota_lo", [EP, 128], FP16)
        iota_t = sb("iota_t", [128, T1], FP32)
        iota_t16 = sb("iota_t16", [128, T1], FP16)
        iota_g = sb("iota_g", [128, REL], FP32)
        iota_k = sb("iota_k", [128, MAXT], FP32)
        tri = sb("tri", [EP, EP], FP32)
        ones = sb("ones", [EP, 128], FP32)
        R = sb("R", [EP, REL, EJ], FP16)
        B = sb("B", [EP, NT, EJ], FP16)
        S = sb("S", [EP, REL, EJ], FP32)
        cmp_ = sb("cmp_", [128, T1 * REL], FP32)
        rowcnt = sb("rowcnt", [EP, REL], FP32)
        rowcntb = sb("rowcntb", [EP, NT], FP32)
        small = {g: {n: sb(f"{n}{g}", [128, g], FP32) for n in ("nt", "tiles", "tin", "tex", "ninc", "start", "k", "k2", "d")}
                 for g in (REL, NT)}
        pos1, pos2, pos2p = (sb(n, [EP, EJ], FP32) for n in ("pos1", "pos2", "pos2p"))
        posi = sb("posi", [EP, EJ], I32)
        parti = sb("parti", [EP, EJ], I32)
        lo1, hi1, plo1, phi = (sb(n, [EP, EJ], FP32) for n in ("lo1", "hi1", "plo1", "phi"))
        pool_edges = sb("pool_edges", [EP, 3, EJ], FP32)
        pool_col = sb("pool_col", [EP, 2, 3], FP32)
        lo2, hi2, dstl1 = (pool_edges[:, n, :] for n in range(3))
        oh_s = sb("oh_s", [EP, 2, N], FP16)
        oh_d = sb("oh_d", [EP, 2, N], FP16)
        oh_lo1 = sb("oh_lo1", [EP, 2, 128], FP16)
        oh_lo2 = sb("oh_lo2", [EP, 2, 128], FP16)
        val1 = sb("val1", [EP, 2, 4, T1], FP16)
        val2 = sb("val2", [EP, 2, T2], FP16)
        relf = sb("relf", [128, T1], FP32)
        firstf = sb("firstf", [128, T1], FP32)
        buckf = sb("buckf", [128, T2], FP32)
        startf = sb("startf", [128, T2], FP32)
        slot = sb("slot", [128, 4, T1], FP32)
        tmp = sb("tmp", [128, T1], FP32)
        qinv = sb("qinv", [P, NT, REL], FP32)
        CT = sb("CT", [P, NT, N], FP32)
        reli = sb("reli", [128, T1], I32)

        s = {n: K.sem("e_" + n) for n in (
            "edges_loaded", "x_loaded", "consts_ready", "rowcnt_ready", "prefix_ready", "ranks_ready", "prefix_used",
            "products_done", "counts_stored", "rest_stored", "slots_ready", "pool_col_ready", "pool_slots_ready", "slots_free", "transposed",
            "ct_stored", "qinv_ready", "qinv_stored")}

        with ExitStack() as pctx:
            acc = K.pb("acc", [128, 8, 512], FP32, pctx)
            REST = N - 512

            def count_piece(i, piece):
                if piece == 0:
                    return acc[0:P, i, :], slice(0, 512)
                b, o = (5, i * REST) if i < 4 else (6, 0)
                return acc[0:P, b, o:o + REST], slice(512, N)

            block = ctx.enter_context(nc.Block())

            @block.sync
            def _(eng):
                for a, name in enumerate(("src", "dst", "edge_type_34")):
                    eng.dma_start(edges_in[:, a, :], ins[name].rearrange("(p j) -> p j", j=EJ)).then_inc(s["edges_loaded"], 16)
                eng.dma_start(K.x[:, :, :], ins["x"].rearrange("(i p) c -> p i c", p=P)).then_inc(s["x_loaded"], 16)
                eng.wait_ge(s["x_loaded"], 16)
                eng.wait_ge(s["qinv_ready"], 1)
                eng.dma_start(K.qinv_dram.rearrange("(i p r) a -> p i (r a)", p=P, r=REL), qinv[:, :, :]).then_inc(s["qinv_stored"], 16)
                eng.wait_ge(s["consts_ready"], 12)
                eng.dma_start(K.msg_dram[E_EDGES:E_EDGES + 128, :].rearrange("p (a b) -> p a b", a=3),
                              bc(K.zrow[:, :].unsqueeze(1), [128, 3, 512])).then_inc(s["qinv_stored"], 16)
                eng.wait_ge(s["qinv_stored"], 32)

            @block.gpsimd
            def _(eng):
                ready = s["consts_ready"]
                eng.sem_inc(s["slots_free"], 2)
                eng.memset(zero[:, :], 0.0).then_inc(ready, 1)
                eng.memset(zero16[:, :], 0.0).then_inc(ready, 1)
                eng.iota(iota_g[:, :], pattern=[[1, REL]], base=0, channel_multiplier=0, allow_small_or_imprecise_dtypes=True).then_inc(ready, 1)
                eng.iota(iota_n[:, :], pattern=[[1, N]], base=0, channel_multiplier=0, allow_small_or_imprecise_dtypes=True).then_inc(ready, 1)
                eng.iota(iota_k[:, :], pattern=[[128, MAXT]], base=0, channel_multiplier=0, allow_small_or_imprecise_dtypes=True).then_inc(ready, 1)
                eng.iota(iota_lo[:, :], pattern=[[1, 128]], base=0, channel_multiplier=0, allow_small_or_imprecise_dtypes=True).then_inc(ready, 1)
                eng.iota(iota_t[:, :], pattern=[[1, T1]], base=0, channel_multiplier=0, allow_small_or_imprecise_dtypes=True).then_inc(ready, 1)
                eng.iota(iota_t16[:, :], pattern=[[1, T1]], base=0, channel_multiplier=0, allow_small_or_imprecise_dtypes=True).then_inc(ready, 1)
                eng.memset(ones[:, :], 1.0).then_inc(ready, 1)
                eng.memset(K.zrow[:, :], 0.0).then_inc(ready, 1)
                link = chain(eng, K.pool_chain)
                link(eng.memset(tri[:, :], 1.0))
                link(eng.memset(K.ident[:, :], 0.0))
                eng.affine_select(out=tri[:, :], in_=tri[:, :], compare_op=ALU.is_gt, fill=0.0, base=0,
                                  pattern=[[1, EP]], channel_multiplier=-1).then_inc(ready, 1)
                eng.affine_select(out=K.ident[:, :], in_=K.ident[:, :], compare_op=ALU.not_equal, fill=1.0, base=0,
                                  pattern=[[1, 128]], channel_multiplier=-1).then_inc(ready, 1)
                eng.wait_ge(s["ranks_ready"], 1)
                with eng.Fori(0, EJ // 2) as i:
                    for u in range(2):
                        j = i * 2 + u
                        eng.wait_ge(s["slots_free"], j + 1)
                        eng.tensor_copy(pool_col[:, u, :], pool_edges[:, :, bass.ds(j, 1)].rearrange("p n a -> p (n a)")
                                        ).then_inc(s["pool_col_ready"], 1)
                        eng.wait_ge(s["pool_col_ready"], j + 1)
                        eng.nop(nofuse=True)
                        eng.tensor_scalar(oh_lo2[:, u, :], iota_lo[:, :], pool_col[:, u, 0:1], None, ALU.is_equal)
                        eng.tensor_scalar(val2[:, u, :], iota_t16[0:EP, 0:T2], pool_col[:, u, 1:2], pool_col[:, u, 2:3], ALU.is_equal, ALU.mult
                                          ).then_inc(s["pool_slots_ready"], 1)

            @block.vector
            def _(eng):
                link = chain(eng, K.dve_chain)
                tal = K.dve_chain

                def ranks(G, onehot, rows, d, ready_at, floor, positions):
                    sc = S[:, 0:G, :]
                    flat = lambda a: a.rearrange("p g j -> p (g j)")
                    link(eng.tensor_tensor_scan(flat(sc), flat(onehot[:, :, :]), bc(zero[0:EP, :], [EP, G * EJ]), 0.0, ALU.add, ALU.add))
                    last = S[:, 0:G, EJ - 1]
                    link(eng.tensor_copy(rows[:, 0:1], last[:, 0:1]))
                    eng.tensor_tensor(rows[:, 1:G], last[:, 1:G], last[:, 0:G - 1], ALU.subtract).then_inc(s["rowcnt_ready"], 1)
                    eng.wait_ge(s["prefix_ready"], ready_at)
                    link(eng.tensor_copy(d["nt"][:, :], acc[:, 7, 64:64 + G]))
                    c3 = cmp_[:, 0:G * MAXT].rearrange("p (g k) -> p g k", k=MAXT)
                    link(eng.tensor_tensor(c3, bc(d["nt"][:, :].unsqueeze(2), [128, G, MAXT]),
                                           bc(iota_k[:, :].unsqueeze(1), [128, G, MAXT]), ALU.is_gt))
                    link(eng.tensor_reduce(d["tiles"][:, :], c3, AX.X, ALU.add))
                    link(eng.tensor_scalar(d["tiles"][:, :], d["tiles"][:, :], floor, None, ALU.max))
                    link(eng.tensor_tensor_scan(d["tin"][:, :], d["tiles"][:, :], bc(zero[:, :], [128, G]), 0.0, ALU.add, ALU.add))
                    link(eng.tensor_tensor(d["tex"][:, :], d["tin"][:, :], d["tiles"][:, :], ALU.subtract))
                    link(eng.tensor_tensor_scan(d["ninc"][:, :], d["nt"][:, :], bc(zero[:, :], [128, G]), 0.0, ALU.add, ALU.add))
                    link(eng.tensor_tensor(d["start"][:, :], d["ninc"][:, :], d["nt"][:, :], ALU.subtract))
                    for base, scale, k, pos in ((d["tex"], 128.0, d["k"], positions[0]), (d["start"], 1.0, d["k2"], positions[1])):
                        if pos is None:
                            continue
                        link(eng.scalar_tensor_tensor(k[0:EP, :], base[0:EP, :], scale, acc[0:EP, 7, 0:G], ALU.mult, ALU.add))
                        link(eng.tensor_tensor(k[0:EP, 1:G], k[0:EP, 1:G], last[:, 0:G - 1], ALU.subtract))
                        m = cmp_[0:EP, 0:G * EJ].rearrange("p (g j) -> p g j", j=EJ)
                        link(eng.tensor_tensor(m, sc, bc(k[0:EP, :].unsqueeze(2), [EP, G, EJ]), ALU.add))
                        link(eng.tensor_tensor(m, m, onehot[:, :, :], ALU.mult))
                        link(eng.tensor_reduce(pos[:, :], m.rearrange("p g j -> p j g"), AX.X, ALU.add))
                        link(eng.tensor_scalar(pos[:, :], pos[:, :], 1.0, None, ALU.subtract))

                def split(pos, lo, hi, lo_plus):
                    link(eng.tensor_copy(posi[:, :], pos[:, :]))
                    link(eng.tensor_scalar(parti[:, :], posi[:, :], 127, None, ALU.bitwise_and))
                    link(eng.tensor_copy(lo[:, :], parti[:, :]))
                    if lo_plus:
                        link(eng.tensor_scalar(lo[:, :], lo[:, :], float(lo_plus), None, ALU.add))
                    link(eng.tensor_scalar(parti[:, :], posi[:, :], 7, None, ALU.logical_shift_right))
                    link(eng.tensor_copy(hi[:, :], parti[:, :]))

                eng.wait_ge(s["edges_loaded"], 48)
                eng.wait_ge(s["consts_ready"], 12)
                link(eng.tensor_copy(srcf[:, :], edges_in[:, 0, :]))
                link(eng.tensor_copy(dstf[:, :], edges_in[:, 1, :]))
                link(eng.tensor_copy(etf[:, :], edges_in[:, 2, :]))
                link(eng.tensor_copy(K.ident16[:, :], K.ident[:, :]))

                eb = lambda a, g: bc(a[:, :].unsqueeze(1), [EP, g, EJ])
                ib = lambda g: bc(iota_g[0:EP, 0:g].unsqueeze(2), [EP, g, EJ])
                link(eng.tensor_tensor(R[:, :, :], eb(etf, REL), ib(REL), ALU.is_equal))
                link(eng.tensor_scalar(bucket[:, :], dstf[:, :], float(P), None, ALU.is_ge))
                for k in range(2, NT):
                    link(eng.tensor_scalar(bstep[:, :], dstf[:, :], float(P * k), None, ALU.is_ge))
                    link(eng.tensor_tensor(bucket[:, :], bucket[:, :], bstep[:, :], ALU.add))
                link(eng.tensor_tensor(B[:, :, :], eb(bucket, NT), ib(NT), ALU.is_equal))
                link(eng.tensor_scalar(bstep[:, :], bucket[:, :], -float(P), 1.0, ALU.mult, ALU.add))
                link(eng.tensor_tensor(dstl1[:, :], bstep[:, :], dstf[:, :], ALU.add))
                link(eng.tensor_scalar(src1[:, :], srcf[:, :], 1.0, None, ALU.add))
                ranks(REL, R, rowcnt, small[REL], 1, 1.0, (pos1, None))
                ranks(NT, B, rowcntb, small[NT], 2, 0.0, (pos2p, pos2))
                split(pos1, lo1, hi1, 0)
                split(pos2p, lo2, hi2, 0)
                split(pos2, plo1, phi, 0)
                eng.sem_inc(s["prefix_used"], 1)
                eng.sem_inc(s["ranks_ready"], 1)

                with eng.Fori(0, EJ // 2) as i:
                    for u in range(2):
                        j = i * 2 + u
                        col = lambda a: a[:, bass.ds(j, 1)]
                        eng.wait_ge(s["slots_free"], j + 1)
                        eng.tensor_scalar(oh_s[:, u, :], iota_n[:, :], col(srcf), None, ALU.is_equal)
                        eng.tensor_scalar(oh_d[:, u, :], iota_n[:, :], col(dstf), None, ALU.is_equal)
                        eng.tensor_scalar(oh_lo1[:, u, :], iota_lo[:, :], col(lo1), None, ALU.is_equal)
                        for a, v in enumerate((src1, dstf, phi, plo1)):
                            last = eng.tensor_scalar(val1[:, u, a, :], iota_t16[0:EP, :], col(hi1), col(v), ALU.is_equal, ALU.mult)
                        last.then_inc(s["slots_ready"], 1)
                eng.wait_ge(s["products_done"], 1)
                a, cols = count_piece(NT - 1, 1)
                eng.tensor_copy(K.counts[:, NT - 1, cols], a).then_inc(s["rest_stored"], 1)
                link(eng.tensor_scalar(qinv[:, :, :], acc[0:P, 6, REST + T2:REST + T2 + NT * REL].rearrange("p (i r) -> p i r", r=REL), 1.0, W_SCALE,
                                       ALU.max, ALU.mult))
                eng.reciprocal(qinv[:, :, :], qinv[:, :, :]).then_inc(s["qinv_ready"], 1)
                link(eng.tensor_copy(slot[:, :, :].rearrange("p a t -> p (a t)"), acc[:, 7, 0:4 * T1]))
                link(eng.memset(K.slot_dst[:, T2:T2 + 1], -1.0))
                link(eng.tensor_scalar(K.slot_dst[:, 0:T2], acc[:, 6, REST:REST + T2], 1.0, None, ALU.subtract))
                d = small[REL]
                c3 = cmp_[:, :].rearrange("p (t g) -> p t g", g=REL)
                link(eng.tensor_tensor(c3, bc(iota_t[:, :].unsqueeze(2), [128, T1, REL]), bc(d["tin"][:, :].unsqueeze(1), [128, T1, REL]), ALU.is_ge))
                link(eng.tensor_reduce(relf[:, :], c3, AX.X, ALU.add))
                link(eng.tensor_scalar(relf[:, :], relf[:, :], float(REL - 1), None, ALU.min))
                link(eng.memset(firstf[:, 0:1], 1.0))
                link(eng.tensor_tensor(firstf[:, 1:T1], relf[:, 1:T1], relf[:, 0:T1 - 1], ALU.not_equal))
                link(eng.tensor_copy(K.rel_row[:, :], relf[0:1, :]))
                link(eng.scalar_tensor_tensor(firstf[:, :], relf[:, :], float(REL - 1), firstf[:, :], ALU.is_lt, ALU.mult))
                link(eng.tensor_copy(reli[:, :], relf[:, :]))
                link(eng.tensor_scalar(reli[:, :], reli[:, :], 1, None, ALU.bitwise_and))
                link(eng.tensor_copy(tmp[:, :], reli[:, :]))
                link(eng.tensor_scalar(tmp[:, :], tmp[:, :], -1.0, 2.0, ALU.mult, ALU.add))
                link(eng.tensor_tensor(firstf[:, :], firstf[:, :], tmp[:, :], ALU.mult))
                link(eng.tensor_copy(K.first_row[:, :], firstf[0:1, :]))
                d = small[NT]
                c3 = cmp_[:, 0:T2 * NT].rearrange("p (t g) -> p t g", g=NT)
                tb = bc(iota_t[:, 0:T2].unsqueeze(2), [128, T2, NT])
                link(eng.tensor_tensor(c3, tb, bc(d["tin"][:, :].unsqueeze(1), [128, T2, NT]), ALU.is_ge))
                link(eng.tensor_reduce(buckf[:, :], c3, AX.X, ALU.add))
                link(eng.tensor_scalar(buckf[:, :], buckf[:, :], float(NT - 1), None, ALU.min))
                link(eng.tensor_copy(K.bucket_row[:, :], buckf[0:1, :]))
                link(eng.scalar_tensor_tensor(d["d"][:, :], d["tex"][:, :], -128.0, d["start"][:, :], ALU.mult, ALU.add))
                link(eng.tensor_tensor(c3, bc(buckf[:, :].unsqueeze(2), [128, T2, NT]), bc(iota_g[:, 0:NT].unsqueeze(1), [128, T2, NT]), ALU.is_equal))
                link(eng.tensor_tensor(c3, c3, bc(d["d"][:, :].unsqueeze(1), [128, T2, NT]), ALU.mult))
                link(eng.tensor_reduce(startf[:, :], c3, AX.X, ALU.add))
                link(eng.scalar_tensor_tensor(startf[:, :], iota_t[:, 0:T2], 128.0, startf[:, :], ALU.mult, ALU.add))
                link(eng.tensor_scalar(startf[:, :], startf[:, :], float(E_EDGES), None, ALU.min))
                link(eng.tensor_copy(K.start_row[:, :], startf[0:1, :]))

                link(eng.tensor_scalar(tmp[:, :], slot[:, 0, :], 1.0, 0.0, ALU.subtract, ALU.max))
                link(eng.tensor_copy(K.slot_src[:, 0:T1], tmp[:, :]))
                link(eng.memset(K.slot_src[:, T1:T1 + AHEAD], 0))
                link(eng.scalar_tensor_tensor(tmp[:, :], slot[:, 2, :], 128.0, slot[:, 3, :], ALU.mult, ALU.add))
                link(eng.tensor_scalar(slot[:, 2, :], slot[:, 0, :], 0.0, 2.0 * E_EDGES, ALU.is_equal, ALU.mult))
                link(eng.tensor_tensor(tmp[:, :], tmp[:, :], slot[:, 2, :], ALU.add))
                link(eng.tensor_copy(K.slot_row[:, :], tmp[:, :]))
                link(eng.scalar_tensor_tensor(tmp[:, :], slot[:, 1, :], float(REL), relf[:, :], ALU.mult, ALU.add))
                link(eng.tensor_copy(K.slot_pair[:, :], tmp[:, :]))

                for i in range(NT):
                    eng.wait_ge(s["transposed"], i + 1)
                    eng.tensor_copy(CT[:, i, :], acc[0:P, 2 * (i % 2):2 + 2 * (i % 2), :].rearrange("p b n -> p (b n)")[:, 0:N]
                                    ).then_inc(s["ct_stored"], 1)
                eng.wait_ge(s["ct_stored"], NT)
                link(eng.tensor_scalar(K.maskT[:, :, :], CT[:, :, :], 0.0, NEG, ALU.is_equal, ALU.mult))
                link(eng.tensor_reduce(K.deg[:, :], CT[:, :, :], AX.X, ALU.add))

            @block.scalar
            def _(eng):
                eng.wait_ge(s["products_done"], 1)
                for i in range(NT):
                    for piece in range(2 if i < NT - 1 else 1):
                        a, cols = count_piece(i, piece)
                        eng.copy(K.counts[:, i, cols], a).then_inc(s["counts_stored"], 1)

            @block.tensor
            def _(eng):
                kw = dict(skip_group_check=True)
                eng.wait_ge(s["consts_ready"], 12)
                z, zr = zero16[:, 0:P], zero16[:, :]

                def zeros(banks, m, start, stop):
                    for b in banks:
                        last = eng.matmul(acc[0:m, b, :], zero16[:, 0:m], zr, start=start, stop=stop, **kw)
                    return last
                zeros(range(6), P, True, False)
                zeros((6,), 128, True, False)
                for n, (rows, G) in enumerate(((rowcnt, REL), (rowcntb, NT))):
                    eng.wait_ge(s["rowcnt_ready"], n + 1)
                    eng.matmul(acc[0:EP, 7, 0:G], tri[:, :], rows[:, :], start=True, stop=True)
                    eng.matmul(acc[:, 7, 64:64 + G], ones[:, :], rows[:, :], start=True, stop=True).then_inc(s["prefix_ready"], 1)
                eng.wait_ge(s["prefix_used"], 1)
                zeros((7,), 128, True, False)
                with eng.Fori(0, EJ // 2) as i:
                    for u in range(2):
                        eng.wait_ge(s["pool_slots_ready"], i * 2 + (u + 1))
                        eng.matmul(acc[:, 6, REST:REST + T2], oh_lo2[:, u, :], val2[:, u, :], start=False, stop=False, **kw)
                        eng.wait_ge(s["slots_ready"], i * 2 + (u + 1))
                        eng.matmul(acc[:, 7, 0:4 * T1], oh_lo1[:, u, :], val1[:, u, :, :].rearrange("p a t -> p (a t)"), start=False, stop=False, **kw)
                        onehot = R[:, :, bass.ds(i * 2 + u, 1)].rearrange("p g a -> p (g a)")
                        for t in range(NT):
                            tile = slice(t * P, (t + 1) * P)
                            at = REST + T2 + t * REL
                            eng.matmul(acc[0:P, 6, at:at + REL], oh_d[:, u, tile], onehot, start=False, stop=False, **kw)
                            for piece in range(2):
                                a, cols = count_piece(t, piece)
                                last = eng.matmul(a, oh_s[:, u, tile], oh_d[:, u, cols], start=False, stop=False, **kw)
                        last.then_inc(s["slots_free"], 1)
                zeros(range(6), P, False, True)
                zeros((6, 7), 128, False, True).then_inc(s["products_done"], 1)
                eng.wait_ge(s["counts_stored"], 2 * NT - 1)
                eng.wait_ge(s["rest_stored"], 1)
                for i in range(NT):
                    if i >= 2:
                        eng.wait_ge(s["ct_stored"], i - 1)
                    for k in range(NT):
                        flat = acc[0:P, 2 * (i % 2):2 + 2 * (i % 2), :].rearrange("p b n -> p (b n)")
                        lo, hi = k * P, (k + 1) * P
                        src = K.counts[:, k, i * P:(i + 1) * P]
                        if hi <= 512:
                            last = eng.transpose(flat[:, lo:hi], src, K.ident[0:P, 0:P])
                        else:
                            c = 512 - lo
                            eng.matmul(flat[:, lo:512], src, K.ident[0:P, 0:c], start=True, stop=True)
                            last = eng.matmul(flat[:, 512:hi], src, K.ident[0:P, c:P], start=True, stop=True)
                    last.then_inc(s["transposed"], 1)


def gather_inverse_counts(K, eng, s, start, end):
    pair, got = K.pair_col, K.inv_col

    def gather_inv(u):
        eng.indirect_dma_start(out=got[:, u:u + 1], out_offset=None, in_=K.qinv_dram,
                               in_offset=bass.IndirectOffsetOnAxis(ap=pair[:, u:u + 1], axis=0)).then_inc(s["gathered_%d" % u], 16)
    eng.tensor_copy(pair[:, :], K.slot_pair[:, start:start + IDX_BUFS]).then_inc(s["pair_ready"], 1)
    eng.wait_ge(s["pair_ready"], 1)
    for u in range(IDX_BUFS):
        gather_inv(u)
    times = (end - start) // IDX_BUFS
    with eng.Fori(1, times) as i:
        for u in range(IDX_BUFS):
            t = i * IDX_BUFS + (start + u)
            eng.wait_ge(s["gathered_%d" % u], i * 16)
            eng.tensor_copy(K.slot_inv[:, bass.ds(t, 1)], got[:, u:u + 1])
            eng.tensor_copy(pair[:, u:u + 1], K.slot_pair[:, bass.ds(t, 1)]).then_inc(s["pair_ready"], 1)
            eng.wait_ge(s["pair_ready"], i * IDX_BUFS + (u + 2 - IDX_BUFS))
            eng.nop(nofuse=True)
            gather_inv(u)
    for u in range(IDX_BUFS):
        eng.wait_ge(s["gathered_%d" % u], times * 16)
        eng.tensor_copy(K.slot_inv[:, end + u:end + u + 1], got[:, u:u + 1])


class Transposed:

    def __init__(self, K, name, src, xT, parts, psum, norm=None):
        self.K, self.src, self.xT, self.parts, self.psum, self.norm = K, src, xT, parts, psum, norm
        self.s = {n: K.sem(name + "_" + n) for n in ("var_ready", "sd_ready", "rows_ready", "hi_ready", "lo_ready", "transposed", "copied_even", "copied_odd")}
        if norm:
            self.stats, self.mv, self.sd = norm["stats"], norm["mv"], norm["sd"]

    def _view(self, i):
        p = self.psum[i % 2][:, :, 0:KC * PP].rearrange("p a (k n) -> p a k n", n=PP)[:, :, :, 0:P]
        return self.xT[:, :, :, i * P:(i + 1) * P], p

    def _copy(self, eng, i):
        self_s = self.s
        out, src = self._view(i)
        eng.wait_ge(self_s["transposed"], i + 1)
        for a in range(2):
            if i % 2:
                last = eng.tensor_copy(out[:, a], src[:, a])
            else:
                last = eng.copy(out[:, a], src[:, a])
        last.then_inc(self_s[("copied_even", "copied_odd")[i % 2]], 1)

    def vector(self, eng):
        K, s = self.K, self.s
        link = chain(eng, K.dve_chain)
        if self.norm:
            for i in range(NT):
                for h in range(2):
                    eng.bn_stats(self.stats[:, i, h, :], K.x[:, i, h * HC:(h + 1) * HC])
            link(eng.memset(self.xT[:, :, :, N:XW], 0.0))
            for i in range(NT):
                last = eng.bn_aggr(self.mv[:, i, :], self.stats[:, i, :, :].rearrange("p a b -> p (a b)"))
            link(last)
            eng.tensor_scalar(self.sd[:, :], self.mv[:, :, 1], 1e-5, None, ALU.add).then_inc(s["var_ready"], 1)
            eng.wait_ge(s["sd_ready"], 1)
            link(eng.reciprocal(self.sd[:, :], self.sd[:, :]))
        else:
            link(eng.memset(self.xT[:, :, :, N:XW], 0.0))
        for i in range(NT):
            if self.norm:
                eng.tensor_scalar(self.src[:, i, :], K.x[:, i, :], self.mv[:, i, 0:1], self.sd[:, i:i + 1], ALU.subtract, ALU.mult
                                  ).then_inc(s["rows_ready"], 1)
            eng.wait_ge(s["hi_ready"], i + 1)
            eng.tensor_tensor(self.parts[:, i, 1, :], self.src[:, i, :], self.parts[:, i, 0, :], ALU.subtract).then_inc(s["lo_ready"], 1)
            if i >= 2 and i % 2 == 0:
                self._copy(eng, i - 1)

    def scalar(self, eng):
        K, s = self.K, self.s
        if self.norm:
            eng.wait_ge(s["var_ready"], 1)
            eng.activation(self.sd[:, :], self.sd[:, :], ACT.Sqrt).then_inc(s["sd_ready"], 1)
        for i in range(NT):
            if self.norm:
                eng.wait_ge(s["rows_ready"], i + 1)
            eng.activation(self.parts[:, i, 0, :], self.src[:, i, :], ACT.Copy).then_inc(s["hi_ready"], 1)
            if i >= 1 and i % 2 == 1:
                self._copy(eng, i - 1)
        self._copy(eng, NT - 1)

    def tensor(self, eng):
        K, s = self.K, self.s
        for i in range(NT):
            eng.wait_ge(s["lo_ready"], i + 1)
            if i >= 2:
                eng.wait_ge(s[("copied_even", "copied_odd")[i % 2]], i // 2)
            for a in range(2):
                for k in range(KC):
                    last = eng.transpose(self.psum[i % 2][:, a, k * PP:k * PP + P], self.parts[:, i, a, k * 128:(k + 1) * 128],
                                         K.ident16[0:P, 0:P])
            last.then_inc(s["transposed"], 1)

    def wait_done(self, eng):
        eng.wait_ge(self.s["copied_even"], (NT + 1) // 2)
        eng.wait_ge(self.s["copied_odd"], NT // 2)


class Weights:

    def __init__(self, K, name, dram, stage, parts, group=2):
        self.K, self.dram, self.stage, self.parts = K, dram, stage, parts
        self.chunks, self.group = stage.shape[1], group
        self.loads = (self.chunks + group - 1) // group
        self.s_loaded = [K.sem(name + "_loaded%d" % n) for n in range(self.loads)]
        self.s_hi, self.s_lo = K.sem(name + "_hi_ready"), K.sem(name + "_lo_ready")

    def sync(self, eng):
        for n in range(self.loads):
            a, b = n * self.group, min((n + 1) * self.group, self.chunks)
            for dst, src in self.dram(self.stage, a, b):
                eng.dma_start(dst, src).then_inc(self.s_loaded[n], 16)

    def loaded(self, eng, k):
        n = k // self.group
        a, b = n * self.group, min((n + 1) * self.group, self.chunks)
        eng.wait_ge(self.s_loaded[n], 16 * len(self.dram(self.stage, a, b)))

    def scalar(self, eng):
        for k in range(self.chunks):
            self.loaded(eng, k)
            eng.activation(self.parts[:, 0, k, :], self.stage[:, k, :], ACT.Copy, scale=W_SCALE).then_inc(self.s_hi, 1)

    def vector(self, eng):
        for k in range(self.chunks):
            eng.wait_ge(self.s_hi, k + 1)
            eng.scalar_tensor_tensor(self.parts[:, 1, k, :], self.stage[:, k, :], W_SCALE, self.parts[:, 0, k, :],
                                     ALU.mult, ALU.subtract).then_inc(self.s_lo, 1)

    def ready(self, eng, k):
        eng.wait_ge(self.s_lo, k + 1)


def three_products(eng, out_halves, xh, xl, wh, wl, first, last, **kw):
    ins = None
    for x, ws in ((xh, (wh, wl)), (xl, (wh,))):
        for w in ws:
            for h, out in enumerate(out_halves):
                n = out.shape[-1]
                ins = eng.matmul(out, x, w[:, h * n:(h + 1) * n], start=first and x is xh and w is wh,
                                 stop=last and x is xl, **kw)
    return ins


def project_tiles(eng, psum, xT, W, waits, done, free=None, free_base=0):
    for i in range(NT):
        waits(i)
        if i >= 2:
            eng.wait_ge(free, free_base + i - 1)
        tok = slice(i * P, (i + 1) * P)
        for k in range(KC):
            if i == 0:
                W.ready(eng, k)
            ins = three_products(eng, [psum[i % 2][0:P, h, 0:HC] for h in range(2)], xT[:, 0, k, tok], xT[:, 1, k, tok],
                                 W.parts[:, 0, k, :], W.parts[:, 1, k, :], k == 0, k == KC - 1)
        ins.then_inc(done, 1)


def rows_view(w):
    v = w.rearrange("(k p) n -> p k n", p=128)
    return lambda stage, a, b: [(stage[:, a:b, :], v[:, a:b, :])]


def gat_project(K, name, B, src, norm, w, a_src, a_dst, heads, ch, h_sb):
    nc = K.nc
    with ExitStack() as ctx:
        psum = K.pb(name + "_ps", [128, 8, 512], FP32, ctx)
        pT = [psum[:, 4 + 2 * b:6 + 2 * b, :].bitcast(FP16) for b in range(2)]
        pO = [psum[:, 2 * b:2 * b + 2, :] for b in range(2)]
        T = Transposed(K, name + "_t", src, B["xT"], B["parts"], pT, norm)
        W = Weights(K, name + "_w", rows_view(w), B["stage"], B["wparts"])
        s = {n: K.sem(name + "_" + n) for n in ("a_loaded", "projected", "h_ready", "ones_ready", "pair_ready"
                                                ) + tuple("gathered_%d" % b for b in range(IDX_BUFS))}
        a_bc = B["a_bc"]
        block = ctx.enter_context(nc.Block())

        @block.sync
        def _(eng):
            W.sync(eng)
            for n, a in enumerate((a_src, a_dst)):
                eng.dma_start(a_bc[:, n, :], a.rearrange("h c -> (h c)").partition_broadcast(P)).then_inc(s["a_loaded"], 16)
            eng.wait_ge(s["a_loaded"], 32)

        @block.gpsimd
        def _(eng):
            for i in range(NT):
                last = eng.memset(h_sb[:, i, :, ch:ch + 1], 1.0)
            last.then_inc(s["ones_ready"], 1)
            eng.wait_ge(s["ones_ready"], 1)
            if heads > 1:
                gather_inverse_counts(K, eng, s, 0, T_EARLY)

        @block.vector
        def _(eng):
            link = chain(eng, K.dve_chain)
            T.vector(eng)
            W.vector(eng)
            eng.wait_ge(s["a_loaded"], 32)
            for i in range(NT):
                eng.wait_ge(s["h_ready"], i + 1)
                for n, al in enumerate((B["al_s"], B["al_d"])):
                    prod = B["prod"][:, n, :].rearrange("p (h c) -> p h c", c=ch)
                    link(eng.tensor_tensor(prod, h_sb[:, i, :, 0:ch], a_bc[:, n, :].rearrange("p (h c) -> p h c", c=ch), ALU.mult))
                    link(eng.tensor_reduce(al[:, 0:heads, i], prod, AX.X, ALU.add))

        @block.scalar
        def _(eng):
            T.scalar(eng)
            W.scalar(eng)
            for i in range(NT):
                eng.wait_ge(s["projected"], i + 1)
                for b in range(2):
                    if heads == 1:
                        out, ps = h_sb[:, i, 0, b * HC:(b + 1) * HC], pO[i % 2][0:P, b, 0:HC]
                    else:
                        hb = heads // 2
                        out = h_sb[:, i, b * hb:(b + 1) * hb, 0:ch]
                        ps = pO[i % 2][0:P, b, 0:HC].rearrange("p (h c) -> p h c", c=ch)
                    last = eng.activation(out, ps, ACT.Copy, scale=1.0 / W_SCALE)
                last.then_inc(s["h_ready"], 1)

        @block.tensor
        def _(eng):
            T.tensor(eng)
            T.wait_done(eng)
            project_tiles(eng, pO, B["xT"], W, lambda i: None, s["projected"], s["h_ready"])


def column_pieces(k):
    lo, hi = k * P, (k + 1) * P
    if hi <= 512:
        return [(lo, hi, 0)]
    return [(lo, 512, 0), (512, hi, 512 - lo)]


def gat_attend(K, name, B, heads, ch, h_sb, finish):
    nc = K.nc
    pair = min(heads, 2)
    with ExitStack() as ctx:
        psum = K.pb(name + "_ps", [128, 8, 512], FP32, ctx)
        flat = lambda b: psum[:, b:b + 2, :].rearrange("p b n -> p (b n)")
        row = lambda b: flat(b)[0:P, 0:N]
        s = {n: K.sem(name + "_" + n) for n in ("cs_ready", "als_ready", "max_done", "uv_made", "uv_ready", "bc_ready", "rows_copied", "t1_ready", "arg_ready",
                                                "e_ready", "p_ready", "pv_done", "out_free", "finish_a", "finish_b", "bias_loaded", "pair_ready"
                                                ) + tuple("gathered_%d" % b for b in range(IDX_BUFS))}
        mx, mm, u_all, v_all, s2_all = (B["small"][:, n, 0:heads, :] for n in range(5))
        junk = B["parts"][:, :, :, :].bitcast(BF16).rearrange("p i a c -> p (i a c)")[:, 0:NT * N].rearrange("p (i n) -> p i n", n=N)
        t1, arg, ex, rec = B["t1"], B["arg"], B["ex"], B["rec"]
        block = ctx.enter_context(nc.Block())
        rows = B["rows"]
        sums = [psum[0:P, 4 + b, 0:NT * (ch + 1)].rearrange("p (i c) -> p i c", c=ch + 1) for b in range(2)] if heads > 1 else None

        def of(a, h):
            return a[:, h, :] if isinstance(h, int) else a[:, bass.ds(h, 1), :].rearrange("p a i -> p (a i)")

        def column(a, h, k):
            return a[:, h, k:k + 1] if isinstance(h, int) else a[:, bass.ds(h, 1), k:k + 1].rearrange("p a i -> p (a i)")

        def turns(eng, step, tally=None, per=0):
            for b in range(pair):
                step(b, b)
            if heads > 2:
                with eng.Fori(1, heads // 2) as i:
                    if tally:
                        with tally.loop(i, per, heads // 2, 1):
                            for b in range(2):
                                step(i * 2 + b, b)
                    else:
                        for b in range(2):
                            step(i * 2 + b, b)

        def over(h, least):
            return not isinstance(h, int) or h >= least

        @block.sync
        def _(eng):
            eng.dma_start(B["bias"][:, :], finish["bias"].partition_broadcast(P)).then_inc(s["bias_loaded"], 16)
            eng.wait_ge(s["bias_loaded"], 16)

        @block.vector
        def _(eng):
            link = chain(eng, K.dve_chain)

            def maximum(h, b):
                eng.wait_ge(s["als_ready"], h + 1)
                eng.nop(nofuse=True)
                for i in range(NT):
                    last = eng.tensor_tensor_reduce(out=junk[:, i, :], in0=row(2 * b), in1=K.maskT[:, i, :], scale=1.0, scalar=-3.0e38,
                                                    op0=ALU.add, op1=ALU.max, accum_out=B["max_cur"][:, b, i:i + 1])
                link(last)
                eng.tensor_copy(of(mx, h), B["max_cur"][:, b, :]).then_inc(s["max_done"], 1)
            turns(eng, maximum, K.dve_chain, 2)
            eng.wait_ge(s["max_done"], heads)
            a_s, a_d = B["al_s"][:, 0:heads, :], B["al_d"][:, 0:heads, :]
            link(eng.tensor_scalar(s2_all, a_s, 0.2, None, ALU.mult))
            link(eng.tensor_tensor(mm, a_d, mx, ALU.add))
            link(eng.scalar_tensor_tensor(mm, mm, 0.2, mm, ALU.mult, ALU.max))
            link(eng.tensor_tensor(u_all, a_d, mm, ALU.subtract))
            eng.scalar_tensor_tensor(v_all, a_d, 0.2, mm, ALU.mult, ALU.subtract).then_inc(s["uv_made"], 1)

            def weights(h, b):
                prob = B["prob"][b]
                eng.wait_ge(s["rows_copied"], h + 1)

                def make_arg(k):
                    eng.wait_ge(s["t1_ready"], h * NT + (k + 1))
                    eng.scalar_tensor_tensor(arg[:, k % 2, :], rows[:, b, 1, :], column(s2_all, h, k), t1[:, k % 2, :], ALU.add, ALU.max
                                             ).then_inc(s["arg_ready"], 1)

                def make_prob(k):
                    eng.wait_ge(s["e_ready"], h * NT + (k + 1))
                    eng.scalar_tensor_tensor(prob[:, k, :], ex[:, k % 2, :], 1.0, K.counts[:, k, :], ALU.min, ALU.mult
                                             ).then_inc(s["p_ready"], 1)
                make_arg(0)
                for k in range(1, NT):
                    make_arg(k)
                    make_prob(k - 1)
                make_prob(NT - 1)

            def normalise(h, b):
                eng.wait_ge(s["out_free"], h + 2)
                eng.wait_ge(s["pv_done"], h + 1)
                link(eng.tensor_scalar(rec[:, :], sums[b][:, :, ch], 1e-16, None, ALU.add))
                link(eng.reciprocal(rec[:, :], rec[:, :]))
                cols = slice(h * ch, (h + 1) * ch) if isinstance(h, int) else bass.ds(h * ch, ch)
                eng.tensor_tensor(B["g"][:, :, cols], sums[b][:, :, 0:ch], bc(rec[:, :].unsqueeze(2), [P, NT, ch]), ALU.mult
                                  ).then_inc(s["out_free"], 1)

            def step(h, b):
                if over(h, 1):
                    weights(h - 1, 1 - b)
                if over(h, 2):
                    normalise(h - 2, b)
            turns(eng, step, K.dve_chain, 4)
            weights(heads - 1, pair - 1)
            if heads > 1:
                normalise(heads - 2, 0)
                normalise(heads - 1, 1)
                eng.wait_ge(s["out_free"], heads + 2)
                finish["vector"](eng, link, s)
            else:
                finish["vector"](eng, link, s, psum)

        @block.scalar
        def _(eng):
            def current(h, b):
                if over(h, 2):
                    eng.wait_ge(s["als_ready"], h - 1)
                eng.copy(B["cur"][:, b, 0, :], of(B["al_s"], h)).then_inc(s["cs_ready"], 1)
            turns(eng, current)

            def weights(h, b):
                def make_t1(k):
                    eng.activation(t1[:, k % 2, :], rows[:, b, 0, :], ACT.Identity, bias=column(B["al_s"], h, k)).then_inc(s["t1_ready"], 1)

                def make_ex(k):
                    eng.wait_ge(s["arg_ready"], h * NT + (k + 1))
                    if k >= 2:
                        eng.wait_ge(s["p_ready"], h * NT + (k - 1))
                    eng.activation(ex[:, k % 2, :], arg[:, k % 2, :], ACT.Exp).then_inc(s["e_ready"], 1)
                eng.wait_ge(s["rows_copied"], h + 1)
                make_t1(0)
                make_t1(1)
                for k in range(2, NT):
                    make_ex(k - 2)
                    make_t1(k)
                make_ex(NT - 2)
                make_ex(NT - 1)

            def step(h, b):
                if over(h, 2):
                    eng.wait_ge(s["bc_ready"], h - 1)
                eng.copy(B["cur"][:, b, 1, :], of(u_all, h))
                eng.copy(B["cur"][:, b, 2, :], of(v_all, h)).then_inc(s["uv_ready"], 1)
                if over(h, 1):
                    weights(h - 1, 1 - b)
                eng.wait_ge(s["bc_ready"], h + 1)
                eng.copy(rows[:, b, 0, :], row(0))
                eng.copy(rows[:, b, 1, :], row(2)).then_inc(s["rows_copied"], 1)
            eng.wait_ge(s["uv_made"], 1)
            turns(eng, step)
            weights(heads - 1, pair - 1)
            finish["scalar"](eng, s)

        @block.gpsimd
        def _(eng):
            if heads > 1:
                eng.sem_inc(s["out_free"], 2)
                gather_inverse_counts(K, eng, s, T_EARLY, T1)

        @block.tensor
        def _(eng):
            def spread(bank, col):
                for i in range(NT):
                    for lo, hi, off in column_pieces(i):
                        ins = eng.matmul(flat(bank)[:, lo:hi], bc(col[:, i:i + 1], [P, 128]), K.ident[0:P, off:off + hi - lo],
                                         start=True, stop=True)
                return ins

            def spread_sources(h, b):
                if over(h, 2):
                    eng.wait_ge(s["max_done"], h - 1)
                eng.wait_ge(s["cs_ready"], h + 1)
                spread(2 * b, B["cur"][:, b, 0, :]).then_inc(s["als_ready"], 1)
            turns(eng, spread_sources)

            def multiply(h, b):
                eng.wait_ge(s["p_ready"], h * NT + NT)
                if heads > 1:
                    eng.wait_ge(s["out_free"], h + 1)
                for i in range(NT):
                    if heads == 1 and i >= 2:
                        eng.wait_ge(s["out_free"], i - 1)
                    for k in range(NT):
                        w = B["prob"][b][:, k, i * P:(i + 1) * P]
                        if heads > 1:
                            v = h_sb[:, k, h, :] if isinstance(h, int) else h_sb[:, k, bass.ds(h, 1), :].rearrange("p a c -> p (a c)")
                            ins = eng.matmul(sums[b][:, i, :], w, v, start=k == 0, stop=k == NT - 1)
                        else:
                            a = (6, 4)[i % 2]
                            eng.matmul(psum[0:P, a, 0:HC], w, h_sb[:, k, 0, 0:HC], start=k == 0, stop=k == NT - 1)
                            ins = eng.matmul(psum[0:P, a + 1, 0:HC + 1], w, h_sb[:, k, 0, HC:C + 1], start=k == 0, stop=k == NT - 1)
                    if heads == 1:
                        ins.then_inc(s["pv_done"], 1)
                if heads > 1:
                    ins.then_inc(s["pv_done"], 1)

            def step(h, b):
                if over(h, 1):
                    eng.wait_ge(s["rows_copied"], h)
                eng.wait_ge(s["uv_ready"], h + 1)
                spread(0, B["cur"][:, b, 1, :])
                spread(2, B["cur"][:, b, 2, :]).then_inc(s["bc_ready"], 1)
                if over(h, 2):
                    multiply(h - 2, b)
            turns(eng, step)
            if heads > 1:
                multiply(heads - 2, 0)
            multiply(heads - 1, pair - 1)


def gat_phase(K):
    nc, ins = K.nc, K.ins
    with ExitStack() as ctx:
        sb = lambda n, s, d: K.sb(n, s, d, ctx)
        B = {
            "xT": sb("xT", [128, 2, KC, XW], FP16), "parts": sb("parts", [P, NT, 2, C], FP16),
            "stage": sb("stage", [128, KC, C], FP32), "wparts": sb("wparts", [128, 2, KC, C], FP16),
            "a_bc": sb("a_bc", [P, 2, C], FP32), "prod": sb("prod", [P, 2, C], FP32),
            "al_s": sb("al_s", [P, HEADS, NT], FP32), "al_d": sb("al_d", [P, HEADS, NT], FP32),
            "small": sb("small", [P, 5, HEADS, NT], FP32), "cur": sb("cur", [P, 2, 3, NT], FP32),
            "max_cur": sb("max_cur", [P, 2, NT], FP32), "rec": sb("rec", [P, NT], FP32), "rows": sb("spread", [P, 2, 2, N], FP32), "bias": sb("bias", [P, C], FP32), "g": sb("g", [P, NT, C], FP32),
            "t1": sb("t1", [P, 2, N], FP32), "arg": sb("arg", [P, 2, N], FP32), "ex": sb("ex", [P, 2, N], FP32),
        }
        norm = {"stats": sb("stats", [P, NT, 2, 6], FP32), "mv": sb("mv", [P, NT, 2], FP32), "sd": sb("sd", [P, NT], FP32)}
        h1 = sb("h1", [P, NT, HEADS, HD + 1], FP32)
        h2 = h1[:, :, :, :].rearrange("p i h c -> p i (h c)")[:, :, 0:C + 1].unsqueeze(2)
        B["prob"] = [a[:, 0:NT * N].rearrange("p (k n) -> p k n", n=N) for a in (
            B["stage"][0:P, :, :].rearrange("p k n -> p (k n)"), B["parts"][:, :, :, :].bitcast(FP32).rearrange("p i a c -> p (i a c)"))]

        gat_project(K, "g1", B, B["g"], norm, ins["L0_gnn_W1"], ins["L0_gnn_a_src1"], ins["L0_gnn_a_dst1"], HEADS, HD, h1)

        def elu_vector(eng, link, s):
            g, t = B["g"], h1[:, :, :, :].rearrange("p i h c -> p (i h c)")[:, 0:NT * C].rearrange("p (i c) -> p i c", c=C)
            eng.wait_ge(s["bias_loaded"], 16)
            link(eng.tensor_tensor(g[:, :, :], g[:, :, :], bc(B["bias"][:, :].unsqueeze(1), [P, NT, C]), ALU.add))
            eng.tensor_scalar(t, g[:, :, :], 0.0, None, ALU.min).then_inc(s["finish_a"], 1)
            eng.wait_ge(s["finish_b"], 1)
            link(eng.scalar_tensor_tensor(t, g[:, :, :], 0.0, t, ALU.max, ALU.add))
            link(eng.tensor_scalar(g[:, :, :], t, 1.0, None, ALU.subtract))

        def elu_scalar(eng, s):
            t = h1[:, :, :, :].rearrange("p i h c -> p (i h c)")[:, 0:NT * C]
            eng.wait_ge(s["finish_a"], 1)
            eng.activation(t, t, ACT.Exp).then_inc(s["finish_b"], 1)

        gat_attend(K, "a1", B, HEADS, HD, h1, {"bias": ins["L0_gnn_b1"], "vector": elu_vector, "scalar": elu_scalar})
        gat_project(K, "g2", B, B["g"], None, ins["L0_gnn_W2"], ins["L0_gnn_a_src2"], ins["L0_gnn_a_dst2"], 1, C, h2)

        def residual(eng, link, s, psum):
            rec = B["rec"]
            eng.wait_ge(s["bias_loaded"], 16)
            link(eng.tensor_tensor(K.x[:, :, :], K.x[:, :, :], bc(B["bias"][:, :].unsqueeze(1), [P, NT, C]), ALU.add))
            for i in range(NT):
                b = (6, 4)[i % 2]
                eng.wait_ge(s["pv_done"], i + 1)
                link(eng.tensor_scalar(rec[:, i:i + 1], psum[0:P, b + 1, HC:HC + 1], 1e-16, None, ALU.add))
                link(eng.reciprocal(rec[:, i:i + 1], rec[:, i:i + 1]))
                for h in range(2):
                    xs = K.x[:, i, h * HC:(h + 1) * HC]
                    last = eng.scalar_tensor_tensor(xs, psum[0:P, b + h, 0:HC], rec[:, i:i + 1], xs, ALU.mult, ALU.add)
                last.then_inc(s["out_free"], 1)

        gat_attend(K, "a2", B, 1, C, h2, {"bias": ins["L0_gnn_b2"], "vector": residual, "scalar": lambda eng, s: None})




def store_phase(K):
    with ExitStack() as ctx:
        stored = K.sem("stored")
        block = ctx.enter_context(K.nc.Block())

        @block.sync
        def _(eng):
            eng.dma_start(K.out.rearrange("(i p) c -> p i c", p=P), K.x[:, :, :]).then_inc(stored, 16)
            eng.wait_ge(stored, 16)


def ffn_phase(K, layer):
    nc, ins = K.nc, K.ins
    L = "L%d_ffn_" % layer
    CH, CW = KC, EXP * F
    NR = EXP if layer == 0 else EXP + 24 + 1
    PR = 24
    with ExitStack() as ctx:
        sb = lambda n, s, d: K.sb("f%d_%s" % (layer, n), s, d, ctx)
        xT = sb("xT", [128, 2, KC, XW], FP16)
        rows = sb("parts", [128, NT * 2 * C], FP16)
        parts = rows[0:P, :].rearrange("p (i a c) -> p i a c", i=NT, a=2)
        stage = sb("stage", [128, CH, CW], FP32)
        wparts = sb("wparts", [128, 2, 2 * CH, CW], FP16)
        xn = wparts[0:P, 1, 2 * CH - NT:2 * CH, :].bitcast(FP32)
        norm = {"stats": sb("stats", [P, NT, 2, 6], FP32), "mv": sb("mv", [P, NT, 2], FP32), "sd": sb("sd", [P, NT], FP32)}
        rw = sb("rw", [NR, C], FP32)
        rT = sb("rT", [128, 2, KC, NR], FP16)
        lg = sb("lg", [P, NT, NR], FP32)
        m8 = sb("m8", [P, NT, 8], FP32)
        i8 = sb("i8", [P, NT, 8], mybir.dt.uint32)
        fidx = sb("fidx", [P, NT, 8], FP32)
        wk = sb("wk", [P, NT, 2], FP32)
        wt = sb("wt", [P, 2, NT, EXP], FP32)
        iota8 = sb("iota8", [P, EXP], FP32)
        sel = sb("sel", [EXP, CW], FP16)
        wTf = sb("wTf", [EXP, N], FP32)
        wT = sb("wT", [EXP, 2, XW], FP16)
        b1 = sb("b1", [128, FT], FP32)
        b2 = sb("b2", [EXP, C], FP32)
        b2p = sb("b2p", [EXP, 2, C], FP16)
        if layer == 1:
            mg1 = sb("mg1", [128, EXP], FP32)
            mg2 = sb("mg2", [128, FT], FP32)
            emb = sb("emb", [P, EXP, PR], FP32)
            en = sb("en", [P, EXP, 4], FP32)
            pr = sb("pr", [P, EXP * PR], FP32)
            tok = sb("tok", [P, NT, 4], FP32)
            al = sb("al", [P, NT, EXP], FP32)

        psum_ctx = ExitStack()
        psum = K.pb("f%d_ps" % layer, [128, 8, 512], FP32, psum_ctx)
        pT = [psum[:, 4 + 2 * b:6 + 2 * b, :].bitcast(FP16) for b in range(2)]
        T = Transposed(K, "f%d_t" % layer, xn, xT, parts, pT, norm)
        s = {n: K.sem("f%d_%s" % (layer, n)) for n in (
            "router_loaded", "small_loaded", "pool_ready", "rt_ready", "rt_hi", "rt_lo", "logits_ready", "diff_ready", "exp_ready", "norm_ready",
            "root_ready", "gates_ready", "gates_transposed", "wt_hi", "wt_lo", "w_hi", "w_lo", "sel_done")}
        s_w = [K.sem("f%d_chunk%d" % (layer, c)) for c in range(CH)]
        w1 = lambda n: ins[L + n].rearrange("e (k p) f -> p k e f", p=128)
        w2 = lambda n: ins[L + n].rearrange("e f c -> (e f) c").rearrange("(k t p) c -> p k t c", p=128, t=2)
        names = (("w1",), ("w2",)) if layer == 0 else (("w_fast1", "w_slow1", "h_fast1"), ("w_fast2", "w_slow2", "h_fast2"))
        per = len(names[0])
        block = psum_ctx.enter_context(nc.Block())
        slots = CH // per

        def chunk_src(name, c):
            return (w1(name)[:, c, :, :] if c < CH else w2(name)[:, c - CH, :, :])

        def chunk_dst(a, c):
            st = stage[:, (c % slots) * per + a, :]
            return st.rearrange("p (e f) -> p e f", f=F if c < CH else C)

        @block.sync
        def _(eng):
            eng.dma_start(rw[0:EXP, :], ins[L + "router_w"]).then_inc(s["router_loaded"], 16)
            if layer == 1:
                eng.dma_start(rw[EXP:EXP + PR, :], ins[L + "probe_w"]).then_inc(s["router_loaded"], 16)
            with nc.allow_non_contiguous_dma("a bias to a column per hidden tile"):
                eng.dma_start(b1[:, :], ins[L + "b1"].rearrange("e f -> (e f)").rearrange("(t p) -> p t", p=128)).then_inc(s["small_loaded"], 16)
            eng.dma_start(b2[:, :], ins[L + "b2"]).then_inc(s["small_loaded"], 16)
            if layer == 1:
                even = ins[L + "m_gate2"].rearrange("(a b) -> a b", b=2)
                with nc.allow_non_contiguous_dma("a few gates"):
                    for p0, p1, first, which in ((0, 128, 0, 0), (0, 64, 1, 0), (64, 128, 1, 1), (0, 128, 2, 1)):
                        eng.dma_start(mg2[p0:p1, first::3], even[:, which].partition_broadcast(p1 - p0)).then_inc(s["small_loaded"], 16)
                    eng.dma_start(mg1[:, :], ins[L + "m_gate1"].partition_broadcast(128)).then_inc(s["small_loaded"], 16)
                    eng.dma_start(en[:, :, 0], ins[L + "energy"].partition_broadcast(P)).then_inc(s["small_loaded"], 16)
                    eng.dma_start(en[:, :, 1], ins[L + "fatigue"].partition_broadcast(P)).then_inc(s["small_loaded"], 16)
                eng.dma_start(emb[:, :, :], ins[L + "router_emb"].partition_broadcast(P)).then_inc(s["small_loaded"], 16)
            for c in range(2 * CH):
                if c >= slots:
                    eng.wait_ge(s["w_lo"], c - slots + 1)
                for a, name in enumerate(names[c // CH]):
                    eng.dma_start(chunk_dst(a, c), chunk_src(name, c)).then_inc(s_w[c % slots], 16)

        small_loads = 32 if layer == 0 else 16 * 10

        @block.gpsimd
        def _(eng):
            link = chain(eng, K.pool_chain)
            eng.iota(iota8[:, :], pattern=[[1, EXP]], base=0, channel_multiplier=0, allow_small_or_imprecise_dtypes=True
                     ).then_inc(s["pool_ready"], 1)
            if layer == 1:
                eng.wait_ge(s["pool_ready"], 1)
                eng.memset(rw[NR - 1:NR, :], 1.0).then_inc(s["pool_ready"], 1)
            eng.wait_ge(s["pool_ready"], 1 + layer)
            link(eng.memset(sel[:, :], 1.0))
            link(eng.affine_select(out=sel[:, :], in_=sel[:, :], compare_op=ALU.is_ge, fill=0.0, base=0,
                                   pattern=[[1, CW]], channel_multiplier=-F))
            eng.affine_select(out=sel[:, :], in_=sel[:, :], compare_op=ALU.is_ge, fill=0.0, base=F - 1,
                              pattern=[[-1, CW]], channel_multiplier=F).then_inc(s["pool_ready"], 1)

        pool_ready = 2 if layer == 0 else 3

        @block.vector
        def _(eng):
            link = chain(eng, K.dve_chain)

            def cut(c):
                st = stage[:, (c % slots) * per, :]
                if layer == 1:
                    eng.wait_ge(s_w[c % slots], 16 * per * (c // slots + 1))
                    a, b, h = (stage[:, (c % slots) * per + n, :] for n in range(3))
                    if c < CH:
                        e3 = lambda t: t.rearrange("p (e f) -> p e f", f=F)
                        link(eng.tensor_tensor(e3(b), e3(b), bc(mg1[:, :].unsqueeze(2), [128, EXP, F]), ALU.mult))
                        link(eng.tensor_tensor(a, a, b, ALU.add))
                    else:
                        for t in range(2):
                            cols = slice(t * C, (t + 1) * C)
                            f = 2 * (c - CH) + t
                            last = eng.scalar_tensor_tensor(a[:, cols], b[:, cols], mg2[:, f:f + 1], a[:, cols], ALU.mult, ALU.add)
                        link(last)
                    eng.tensor_tensor(a, a, h, ALU.add).then_inc(s["sel_done"], 1)
                eng.wait_ge(s["w_hi"], c + 1)
                eng.scalar_tensor_tensor(wparts[:, 1, c, :], st, W_SCALE, wparts[:, 0, c, :], ALU.mult, ALU.subtract).then_inc(s["w_lo"], 1)

            T.vector(eng)
            eng.wait_ge(s["rt_hi"], 1)
            rps = psum[:, 0, 0:KC * NR].rearrange("p (k r) -> p k r", r=NR)
            eng.scalar_tensor_tensor(rT[:, 1, :, :], rps, W_SCALE, rT[:, 0, :, :], ALU.mult, ALU.subtract).then_inc(s["rt_lo"], 1)
            eng.wait_ge(s["small_loaded"], small_loads)
            link(eng.tensor_scalar(b2p[:, 0, :], b2[:, :], W_SCALE, None, ALU.mult))
            link(eng.scalar_tensor_tensor(b2p[:, 1, :], b2[:, :], W_SCALE, b2p[:, 0, :], ALU.mult, ALU.subtract))
            if layer == 0:
                cut(0), cut(1)
            eng.wait_ge(s["logits_ready"], 1)
            link(eng.tensor_scalar(lg[:, :, :], psum[0:P, 1, 0:NT * NR].rearrange("p (i r) -> p i r", r=NR), 1.0 / W_SCALE, None, ALU.mult))
            eng.wait_ge(s["pool_ready"], pool_ready)
            logit = lg[:, :, 0:EXP]
            if layer == 1:
                b4 = lambda a, sh: bc(a, sh)
                link(eng.tensor_tensor(pr[:, :].rearrange("p (e d) -> p e d", d=PR), emb[:, :, :], emb[:, :, :], ALU.mult))
                eng.tensor_reduce(en[:, :, 2], pr[:, :].rearrange("p (e d) -> p e d", d=PR), AX.X, ALU.add).then_inc(s["norm_ready"], 1)
                eng.wait_ge(s["norm_ready"], 1)
                for i in range(NT):
                    link(eng.tensor_tensor(pr[:, 0:PR], lg[:, i, EXP:EXP + PR], lg[:, i, EXP:EXP + PR], ALU.mult))
                    link(eng.tensor_reduce(tok[:, i, 0:1], pr[:, 0:PR], AX.X, ALU.add))
                eng.tensor_copy(tok[:, :, 1], tok[:, :, 0]).then_inc(s["norm_ready"], 1)
                eng.wait_ge(s["root_ready"], 2)
                link(eng.tensor_scalar(en[:, :, 3], en[:, :, 2], 1e-12, None, ALU.max))
                link(eng.reciprocal(en[:, :, 3], en[:, :, 3]))
                link(eng.tensor_scalar(tok[:, :, 1], tok[:, :, 1], 1e-12, None, ALU.max))
                link(eng.reciprocal(tok[:, :, 1], tok[:, :, 1]))
                link(eng.tensor_tensor(emb[:, :, :], emb[:, :, :], bc(en[:, :, 3].unsqueeze(2), [P, EXP, PR]), ALU.mult))
                for i in range(NT):
                    pe = pr[:, :].rearrange("p (e d) -> p e d", d=PR)
                    link(eng.tensor_scalar(lg[:, i, EXP:EXP + PR], lg[:, i, EXP:EXP + PR], tok[:, i, 1:2], None, ALU.mult))
                    link(eng.tensor_tensor(pe, emb[:, :, :], bc(lg[:, i, EXP:EXP + PR].unsqueeze(1), [P, EXP, PR]), ALU.mult))
                    link(eng.tensor_reduce(al[:, i, :], pe, AX.X, ALU.add))
                link(eng.tensor_scalar(tok[:, :, 2], lg[:, :, NR - 1], 0.02 / C, None, ALU.mult))
                link(eng.tensor_tensor(logit, logit, bc(tok[:, :, 2:3], [P, NT, EXP]), ALU.add))
                for i in range(NT):
                    last = eng.scalar_tensor_tensor(logit[:, i, :], en[:, :, 2], tok[:, i, 2:3], logit[:, i, :], ALU.mult, ALU.add)
                link(last)
                link(eng.scalar_tensor_tensor(logit, al[:, :, :], 0.02, logit, ALU.mult, ALU.add))
                link(eng.tensor_scalar(en[:, :, 0:2], en[:, :, 0:2], 0.1, None, ALU.mult))
                link(eng.tensor_tensor(logit, logit, bc(en[:, :, 0].unsqueeze(1), [P, NT, EXP]), ALU.add))
                link(eng.tensor_tensor(logit, logit, bc(en[:, :, 1].unsqueeze(1), [P, NT, EXP]), ALU.subtract))
            for i in range(NT):
                last = eng.max(m8[:, i, :], logit[:, i, :])
            link(last)
            for i in range(NT):
                last = eng.max_index(i8[:, i, :], m8[:, i, :], logit[:, i, :])
            link(last)
            link(eng.tensor_copy(fidx[:, :, :], i8[:, :, :]))
            eng.tensor_tensor(wk[:, :, 1], m8[:, :, 1], m8[:, :, 0], ALU.subtract).then_inc(s["diff_ready"], 1)
            eng.wait_ge(s["exp_ready"], 1)
            link(eng.tensor_scalar(wk[:, :, 0], wk[:, :, 1], 1.0, None, ALU.add))
            link(eng.reciprocal(wk[:, :, 0], wk[:, :, 0]))
            link(eng.tensor_tensor(wk[:, :, 1], wk[:, :, 1], wk[:, :, 0], ALU.mult))
            for a in range(2):
                w = wt[:, a, :, :]
                link(eng.tensor_tensor(w, bc(iota8[:, :].unsqueeze(1), [P, NT, EXP]), bc(fidx[:, :, a:a + 1], [P, NT, EXP]), ALU.is_equal))
                link(eng.tensor_tensor(w, w, bc(wk[:, :, a:a + 1], [P, NT, EXP]), ALU.mult))
            eng.tensor_tensor(wt[:, 0, :, :], wt[:, 0, :, :], wt[:, 1, :, :], ALU.add).then_inc(s["gates_ready"], 1)
            eng.wait_ge(s["gates_transposed"], 1)
            link(eng.tensor_copy(wTf[:, :], psum[0:EXP, 2:4, :].rearrange("p b n -> p (b n)")[:, 0:N]))
            link(eng.memset(wT[:, :, N:XW], 0.0))
            link(eng.tensor_copy(wT[:, 0, 0:N], wTf[:, :]))
            link(eng.tensor_tensor(wT[:, 1, 0:N], wTf[:, :], wT[:, 0, 0:N], ALU.subtract))
            for c in range(2 if layer == 0 else 0, 2 * CH):
                cut(c)

        @block.scalar
        def _(eng):
            def cut(c):
                if layer == 0:
                    eng.wait_ge(s_w[c % slots], 16 * (c // slots + 1))
                else:
                    eng.wait_ge(s["sel_done"], c + 1)
                eng.activation(wparts[:, 0, c, :], stage[:, (c % slots) * per, :], ACT.Copy, scale=W_SCALE).then_inc(s["w_hi"], 1)

            T.scalar(eng)
            eng.wait_ge(s["rt_ready"], 1)
            rps = psum[:, 0, 0:KC * NR].rearrange("p (k r) -> p k r", r=NR)
            eng.activation(rT[:, 0, :, :], rps, ACT.Copy, scale=W_SCALE).then_inc(s["rt_hi"], 1)
            if layer == 0:
                cut(0), cut(1)
            else:
                eng.wait_ge(s["norm_ready"], 1)
                eng.activation(en[:, :, 2], en[:, :, 2], ACT.Sqrt).then_inc(s["root_ready"], 1)
                eng.wait_ge(s["norm_ready"], 2)
                eng.activation(tok[:, :, 1], tok[:, :, 1], ACT.Sqrt).then_inc(s["root_ready"], 1)
            eng.wait_ge(s["diff_ready"], 1)
            eng.activation(wk[:, :, 1], wk[:, :, 1], ACT.Exp).then_inc(s["exp_ready"], 1)
            for c in range(2 if layer == 0 else 0, 2 * CH):
                cut(c)

        @block.tensor
        def _(eng):
            eng.wait_ge(s["router_loaded"], 16 * (1 + layer))
            eng.wait_ge(s["pool_ready"], pool_ready)
            for k in range(KC):
                last = eng.transpose(psum[:, 0, k * NR:(k + 1) * NR], rw[:, k * 128:(k + 1) * 128], K.ident[0:NR, 0:NR])
            last.then_inc(s["rt_ready"], 1)
            T.tensor(eng)
            T.wait_done(eng)
            eng.wait_ge(s["rt_lo"], 1)
            for i in range(NT):
                tok_ = slice(i * P, (i + 1) * P)
                out = psum[0:P, 1, i * NR:(i + 1) * NR]
                for k in range(KC):
                    last = three_products(eng, [out], xT[:, 0, k, tok_], xT[:, 1, k, tok_], rT[:, 0, k, :], rT[:, 1, k, :], k == 0, k == KC - 1)
            last.then_inc(s["logits_ready"], 1)
            eng.wait_ge(s["gates_ready"], 1)
            flat = psum[0:EXP, 2:4, :].rearrange("p b n -> p (b n)")
            for i in range(NT):
                for lo, hi, off in column_pieces(i):
                    last = eng.matmul(flat[:, lo:hi], wt[:, 0, i, :], K.ident[0:P, off:off + hi - lo], start=True, stop=True)
            last.then_inc(s["gates_transposed"], 1)

        psum_ctx.close()

        with ExitStack() as main_ctx:
            psum = K.pb("f%d_mps" % layer, [128, 8, 512], FP32, main_ctx)
            yv = stage[:, :, :].bitcast(FP16).rearrange("p a b -> p (a b)")[:, 0:2 * FT * XW].rearrange("p (a f n) -> p a f n", a=2, f=FT)
            hy = rows[:, :].bitcast(FP32)[:, 0:4 * XW].rearrange("p (a u n) -> p a u n", a=2, u=2)
            h, y = hy[:, 0], hy[:, 1]
            s = {n: K.sem("f%dm_%s" % (layer, n)) for n in ("up_ready", "up_free", "h_ready", "y_ready", "y_hi", "down_ready", "down_free")}
            block = main_ctx.enter_context(nc.Block())
            up = [psum[:, 2 * b:2 * b + 2, 0:HALF] for b in range(2)]
            wbc = [psum[:, 4 + 2 * b:6 + 2 * b, 0:HALF] for b in range(2)]
            halves = lambda a: a.rearrange("p (b n) -> p b n", b=2)

            @block.sync
            def _(eng):
                pass

            @block.scalar
            def _(eng):
                with eng.Fori(0, FT // 2) as j:
                    for u in range(2):
                        f = j * 2 + u
                        eng.wait_ge(s["up_ready"], f + 1)
                        eng.activation(halves(h[:, u, :]), up[u], ACT.Gelu if layer == 0 else ACT.Relu,
                                       bias=b1[:, bass.ds(f, 1)], scale=1.0 / W_SCALE).then_inc(s["h_ready"], 1)
                        eng.wait_ge(s["y_ready"], f + 1)
                        eng.activation(yv[:, 0, bass.ds(f, 1), :].rearrange("p a n -> p (a n)"), y[:, u, :], ACT.Copy).then_inc(s["y_hi"], 1)

            @block.vector
            def _(eng):
                link = chain(eng, K.dve_chain)
                with eng.Fori(0, FT // 2) as j:
                    with K.dve_chain.loop(j, 2 if layer else 0, FT // 2):
                        for u in range(2):
                            f = j * 2 + u
                            eng.wait_ge(s["h_ready"], f + 1)
                            if layer == 1:
                                link(eng.tensor_tensor(h[:, u, :], h[:, u, :], h[:, u, :], ALU.mult))
                            eng.tensor_tensor(halves(y[:, u, :]), halves(h[:, u, :]), wbc[u], ALU.mult).then_inc(s["y_ready"], 1)
                            eng.wait_ge(s["y_hi"], f + 1)
                            eng.tensor_tensor(yv[:, 1, bass.ds(f, 1), :].rearrange("p a n -> p (a n)"), y[:, u, :],
                                              yv[:, 0, bass.ds(f, 1), :].rearrange("p a n -> p (a n)"), ALU.subtract).then_inc(s["up_free"], 1)
                for i in range(NT):
                    eng.wait_ge(s["down_ready"], i + 1)
                    for hh in range(2):
                        xs = K.x[:, i, hh * HC:(hh + 1) * HC]
                        last = eng.scalar_tensor_tensor(xs, psum[0:P, 2 * (i % 2) + hh, 0:HC], 1.0 / W_SCALE, xs, ALU.mult, ALU.add)
                    last.then_inc(s["down_free"], 1)

            @block.gpsimd
            def _(eng):
                eng.sem_inc(s["up_free"], 2)

            @block.tensor
            def _(eng):
                with eng.Fori(0, FT // 2) as j:
                    for u in range(2):
                        f = j * 2 + u
                        eng.wait_ge(s["up_free"], f + 1)
                        for a in range(2):
                            for hh in range(2):
                                eng.matmul(wbc[u][:, hh, :], sel[:, bass.ds(f * 128, 128)], wT[:, a, hh * HALF:(hh + 1) * HALF],
                                           start=a == 0, stop=a == 1)
                        for k in range(KC):
                            for wa, xs in ((0, (0, 1)), (1, (0,))):
                                w = wparts[:, wa, k, bass.ds(f * 128, 128)]
                                for xa in xs:
                                    for hh in range(2):
                                        last = eng.matmul(up[u][:, hh, :], w, xT[:, xa, k, hh * HALF:(hh + 1) * HALF],
                                                          start=k == 0 and wa == 0 and xa == 0, stop=k == KC - 1 and wa == 1)
                        last.then_inc(s["up_ready"], 1)
                eng.wait_ge(s["up_free"], FT + 2)
                for i in range(NT):
                    if i >= 2:
                        eng.wait_ge(s["down_free"], i - 1)
                    tok_ = slice(i * P, (i + 1) * P)
                    outs = [psum[0:P, 2 * (i % 2) + hh, 0:HC] for hh in range(2)]
                    three_products(eng, outs, wT[:, 0, tok_], wT[:, 1, tok_], b2p[:, 0, :], b2p[:, 1, :], True, False)
                    for f in range(FT):
                        c, o = CH + f // 2, (f % 2) * C
                        last = three_products(eng, outs, yv[:, 0, f, tok_], yv[:, 1, f, tok_], wparts[:, 0, c, o:o + C], wparts[:, 1, c, o:o + C],
                                              False, f == FT - 1)
                    last.then_inc(s["down_ready"], 1)


def ffn0_phase(K):
    ffn_phase(K, 0)


def ffn1_phase(K):
    ffn_phase(K, 1)


def project_block(K, name, src, norm, xT, parts, stage, wparts, w, out, sync=None, vector=None, psum_hook=None):
    with ExitStack() as ctx:
        psum = K.pb(name + "_ps", [128, 8, 512], FP32, ctx)
        pT = [psum[:, 4 + 2 * b:6 + 2 * b, :].bitcast(FP16) for b in range(2)]
        pO = [psum[:, 2 * b:2 * b + 2, :] for b in range(2)]
        T = Transposed(K, name + "_t", src, xT, parts, pT, norm)
        W = Weights(K, name + "_w", rows_view(w), stage, wparts)
        s = {n: K.sem(name + "_" + n) for n in ("projected", "out_ready", "extra")}
        block = ctx.enter_context(K.nc.Block())

        @block.sync
        def _(eng):
            W.sync(eng)
            if sync:
                sync(eng, T, s)

        @block.vector
        def _(eng):
            link = chain(eng, K.dve_chain)
            T.vector(eng)
            W.vector(eng)
            if vector:
                vector(eng, link, s)

        @block.scalar
        def _(eng):
            T.scalar(eng)
            W.scalar(eng)
            for i in range(NT):
                eng.wait_ge(s["projected"], i + 1)
                for b in range(2):
                    last = eng.activation(out[:, i, b * HC:(b + 1) * HC], pO[i % 2][0:P, b, 0:HC], ACT.Copy, scale=1.0 / W_SCALE)
                last.then_inc(s["out_ready"], 1)

        @block.tensor
        def _(eng):
            T.tensor(eng)
            T.wait_done(eng)
            project_tiles(eng, pO, xT, W, lambda i: None, s["projected"], s["out_ready"])


UN = 4


def relation_phase(K, wstage, wring):
    nc, ins = K.nc, K.ins
    w_rel = ins["L1_gnn_W_rel"]
    with ExitStack() as ctx:
        sb = lambda n, s, d: K.sb(n, s, d, ctx)
        rows = sb("r_rows", [128, UN, 2 * C], FP16)
        rowsT = sb("r_rowsT", [128, 2, 2, KC, 128], FP16)
        msg = sb("r_msg", [128, UN, 2, C], FP16)
        gcol = sb("r_gcol", [128, UN], I32)
        scol = sb("r_scol", [128, UN], I32)
        pT = [K.pb("r_pT%d" % b, [128, 2, 1024], FP16, ctx) for b in range(2)]
        pO = [K.pb("r_pO%d" % b, [128, 2, 512], FP32, ctx) for b in range(2)]
        s = {n: K.sem("r_" + n) for n in ("staged_0", "staged_1", "w_hi", "w_lo", "col_ready", "scol_ready", "transposed", "copied", "multiplied",
                                          "msg_hi", "msg_ready")}
        gathered = [K.sem("r_gathered%d" % u) for u in range(UN)]
        scattered = [K.sem("r_scattered%d" % u) for u in range(UN)]
        block = ctx.enter_context(nc.Block())

        def load_w(eng, r, u):
            eng.dma_start(wstage[:, u, :, :], w_rel[r].rearrange("(k p) n -> p k n", p=128) if isinstance(r, int) else
                          w_rel[bass.ds(r, 1), :, :].rearrange("a (k p) n -> p (a k) n", p=128)).then_inc(s["staged_%d" % u], 16)

        @block.sync
        def _(eng):
            load_w(eng, 0, 0)
            load_w(eng, 1, 1)
            with eng.Fori(1, REL // 2) as i:
                for u in range(2):
                    eng.wait_ge(s["w_lo"], i * 2 + (u - 1))
                    load_w(eng, i * 2 + u, u)

        def col(a, t):
            return a[:, t:t + 1] if isinstance(t, int) else a[:, bass.ds(t, 1)]

        @block.gpsimd
        def _(eng):
            def gather(t, b):
                eng.tensor_copy(gcol[:, b:b + 1], col(K.slot_src, t)).then_inc(s["col_ready"], 1)
                eng.wait_ge(s["col_ready"], t + 1)
                eng.nop(nofuse=True)
                eng.indirect_dma_start(out=rows[:, b, :], out_offset=None, in_=K.xn_dram,
                                       in_offset=bass.IndirectOffsetOnAxis(ap=gcol[:, b:b + 1], axis=0)).then_inc(gathered[b], 16)

            def step(t, u, first):
                b = (u + AHEAD) % UN
                if not (first and u < UN - AHEAD):
                    eng.wait_ge(s["transposed"], t + (AHEAD - UN + 1))
                gather(t + AHEAD, b)
                if not first:
                    eng.wait_ge(scattered[u], (t - u) * (16 // UN))
                eng.tensor_copy(scol[:, u:u + 1], col(K.slot_row, t)).then_inc(s["scol_ready"], 1)
                eng.wait_ge(s["scol_ready"], t + 1)
                eng.nop(nofuse=True)
                eng.wait_ge(s["msg_ready"], t + 1)
                eng.nop(nofuse=True)
                eng.indirect_dma_start(out=K.msg_dram, out_offset=bass.IndirectOffsetOnAxis(ap=scol[:, u:u + 1], axis=0),
                                       in_=msg[:, u, :, :].rearrange("p a c -> p (a c)"), in_offset=None,
                                       bounds_check=E_EDGES - 1, oob_is_err=False).then_inc(scattered[u], 16)
            for b in range(AHEAD):
                gather(b, b)
            for u in range(UN):
                step(u, u, True)
            with eng.Fori(1, T1 // UN) as i:
                for u in range(UN):
                    step(i * UN + u, u, False)
            for u in range(UN):
                eng.wait_ge(scattered[u], 16 * (T1 // UN))
            for u in range(AHEAD):
                eng.wait_ge(gathered[u], 16 * (T1 // UN + 1))

        def at(i, u):
            return (i * UN + u) if not isinstance(i, int) else i * UN + u

        @block.scalar
        def _(eng):
            def cut(r, base, slot):
                for k in range(KC):
                    eng.activation(wring[:, slot, 0, k, :], wstage[:, slot, k, :], ACT.Copy, scale=W_SCALE).then_inc(s["w_hi"], 1)

            eng.wait_ge(s["staged_0"], 16)
            cut(0, 0, 0)

            def step(t, u, first):
                flag = eng.value_load(K.first_row[0:1, t:t + 1] if isinstance(t, int) else K.first_row[0:1, bass.ds(t, 1)], min_val=0, max_val=2)
                for slot in range(2):
                    with eng.If(flag == slot + 1):
                        rel = eng.value_load(K.rel_row[0:1, t:t + 1] if isinstance(t, int) else K.rel_row[0:1, bass.ds(t, 1)], min_val=0, max_val=REL - 1)
                        eng.wait_ge(s["staged_%d" % slot], (rel + (3 - slot)) * 8)
                        eng.nop(nofuse=True)
                        if not (first and u == 0):
                            eng.wait_ge(s["multiplied"], t)
                            eng.nop(nofuse=True)
                        cut(None, None, slot)
                eng.wait_ge(s["multiplied"], t + 1)
                if not first:
                    eng.wait_ge(scattered[u], (t - u) * (16 // UN))
                for h in range(2):
                    last = eng.activation(msg[:, u, 0, h * HC:(h + 1) * HC], pO[u % 2][:, h, 0:HC], ACT.Copy,
                                          scale=col(K.slot_inv, t + IDX_BUFS))
                last.then_inc(s["msg_hi"], 1)
            for u in range(UN):
                step(u, u, True)
            with eng.Fori(1, T1 // UN) as i:
                for u in range(UN):
                    step(i * UN + u, u, False)

        @block.vector
        def _(eng):
            def cut(slot, hi_from):
                for k in range(KC):
                    eng.wait_ge(s["w_hi"], hi_from + (k + 1))
                    ins_ = eng.scalar_tensor_tensor(wring[:, slot, 1, k, :], wstage[:, slot, k, :], W_SCALE, wring[:, slot, 0, k, :],
                                                    ALU.mult, ALU.subtract)
                ins_.then_inc(s["w_lo"], 1)

            def copy_rows(t, b, free):
                eng.wait_ge(s["transposed"], t + 1)
                if free:
                    eng.wait_ge(s["multiplied"], t - 1)
                    eng.nop(nofuse=True)
                    eng.wait_ge(s["transposed"], t + 1)
                eng.tensor_copy(rowsT[:, b, :, :, :].rearrange("p a k n -> p a (k n)"), pT[b][:, :, 0:C]).then_inc(s["copied"], 1)

            cut(0, 0)
            copy_rows(0, 0, False)

            def step(t, u, first):
                copy_rows(t + 1, (u + 1) % 2, not (first and u == 0))
                flag = eng.value_load(K.first_row[0:1, t:t + 1] if isinstance(t, int) else K.first_row[0:1, bass.ds(t, 1)], min_val=0, max_val=2)
                for slot in range(2):
                    with eng.If(flag == slot + 1):
                        rel = eng.value_load(K.rel_row[0:1, t:t + 1] if isinstance(t, int) else K.rel_row[0:1, bass.ds(t, 1)], min_val=0, max_val=REL - 1)
                        cut(slot, rel * KC + KC)
                eng.wait_ge(s["msg_hi"], t + 1)
                for h in range(2):
                    last = eng.scalar_tensor_tensor(msg[:, u, 1, h * HC:(h + 1) * HC], pO[u % 2][:, h, 0:HC], col(K.slot_inv, t + IDX_BUFS),
                                                    msg[:, u, 0, h * HC:(h + 1) * HC], ALU.mult, ALU.subtract)
                last.then_inc(s["msg_ready"], 1)
            for u in range(UN):
                step(u, u, True)
            with eng.Fori(1, T1 // UN) as i:
                for u in range(UN):
                    step(i * UN + u, u, False)

        @block.tensor
        def _(eng):
            def transposes(t, b, turn, free):
                eng.wait_ge(gathered[b], turn)
                eng.nop(nofuse=True)
                if free:
                    eng.wait_ge(s["copied"], t - 1)
                for a in range(2):
                    for k in range(KC):
                        last = eng.transpose(pT[b % 2][:, a, k * 128:(k + 1) * 128], rows[:, b, a * C + k * 128:a * C + (k + 1) * 128], K.ident16[:, :])
                last.then_inc(s["transposed"], 1)

            transposes(0, 0, 16, False)

            def step(t, u, first):
                b = (u + 1) % UN
                turn = 16 * (t // UN + 1 + (u + 1) // UN) if first else (t - u) * (16 // UN) + 16 * (1 + (u + 1) // UN)
                transposes(t + 1, b, turn, not (first and u == 0))
                rel = eng.value_load(K.rel_row[0:1, t:t + 1] if isinstance(t, int) else K.rel_row[0:1, bass.ds(t, 1)], min_val=0, max_val=REL - 1)
                slot = rel % 2
                eng.wait_ge(s["w_lo"], rel + 1)
                eng.nop(nofuse=True)
                if not (first and u < 2):
                    eng.wait_ge(s["msg_ready"], t - 1)
                    eng.nop(nofuse=True)
                eng.wait_ge(s["copied"], t + 1)
                for k in range(KC):
                    w = [wring[:, bass.ds(slot, 1), a, k, :].rearrange("p s n -> p (s n)") for a in range(2)]
                    last = three_products(eng, [pO[u % 2][:, h, 0:HC] for h in range(2)], rowsT[:, u % 2, 0, k, :], rowsT[:, u % 2, 1, k, :],
                                          w[0], w[1], k == 0, k == KC - 1)
                last.then_inc(s["multiplied"], 1)
            for u in range(UN):
                step(u, u, True)
            with eng.Fori(1, T1 // UN) as i:
                for u in range(UN):
                    step(i * UN + u, u, False)


def collect_phase(K, h1):
    nc = K.nc
    with ExitStack() as ctx:
        sb = lambda n, s, d: K.sb(n, s, d, ctx)
        rows = sb("c_rows", [128, UN, 2, C], FP16)
        onehot = sb("c_onehot", [128, 2, P], FP16)
        iota_p = sb("c_iota", [128, P], FP16)
        pO = [K.pb("c_pO%d" % b, [128, 2, 512], FP32, ctx) for b in range(2)]
        s = {n: K.sem("c_" + n) for n in ("iota_ready", "onehot_ready", "multiplied", "added")}
        loaded = [K.sem("c_loaded%d" % u) for u in range(UN)]
        block = ctx.enter_context(nc.Block())

        def val(eng, table, t, top):
            return eng.value_load(table[0:1, t:t + 1] if isinstance(t, int) else table[0:1, bass.ds(t, 1)], min_val=0, max_val=top)

        @block.gpsimd
        def _(eng):
            eng.iota(iota_p[:, :], pattern=[[1, P]], base=0, channel_multiplier=0, allow_small_or_imprecise_dtypes=True).then_inc(s["iota_ready"], 1)

        @block.sync
        def _(eng):
            def step(t, u, first):
                at = val(eng, K.start_row, t, E_EDGES)
                if not first:
                    eng.wait_ge(s["multiplied"], t - (UN - 1))
                eng.dma_start(rows[:, u, :, :].rearrange("p a c -> p (a c)"), K.msg_dram[bass.ds(at, 128), :]).then_inc(loaded[u], 16)
            for u in range(UN):
                step(u, u, True)
            with eng.Fori(1, T2 // UN) as i:
                for u in range(UN):
                    step(i * UN + u, u, False)

        @block.vector
        def _(eng):
            eng.wait_ge(s["iota_ready"], 1)

            def make(t, b, first):
                if not first:
                    eng.wait_ge(s["multiplied"], t - 1)
                c = K.slot_dst[:, t:t + 1] if isinstance(t, int) else K.slot_dst[:, bass.ds(t, 1)]
                eng.tensor_scalar(onehot[:, b, :], iota_p[:, :], c, None, ALU.is_equal).then_inc(s["onehot_ready"], 1)

            def step(t, u, first):
                make(t + 1, (u + 1) % 2, first and u == 0)
                bucket = val(eng, K.bucket_row, t, NT - 1)
                if not (first and u == 0):
                    eng.wait_ge(s["added"], t)
                    eng.nop(nofuse=True)
                eng.wait_ge(s["multiplied"], t + 1)
                eng.nop(nofuse=True)
                acc = h1[:, bass.ds(bucket, 1), :].rearrange("p a c -> p (a c)").rearrange("p (b n) -> p b n", b=2)
                eng.tensor_tensor(acc, pO[u % 2][0:P, :, 0:HC], acc, ALU.add).then_inc(s["added"], 1)
            make(0, 0, True)
            for u in range(UN):
                step(u, u, True)
            with eng.Fori(1, T2 // UN) as i:
                for u in range(UN):
                    step(i * UN + u, u, False)

        @block.tensor
        def _(eng):
            def step(t, u, first):
                eng.wait_ge(loaded[u], 16 if first else (t - u) * (16 // UN) + 16)
                eng.nop(nofuse=True)
                if not (first and u < 2):
                    eng.wait_ge(s["added"], t - 1)
                    eng.nop(nofuse=True)
                eng.wait_ge(s["onehot_ready"], t + 1)
                for a in range(2):
                    for h in range(2):
                        last = eng.matmul(pO[u % 2][0:P, h, 0:HC], onehot[:, u % 2, :], rows[:, u, a, h * HC:(h + 1) * HC], start=a == 0, stop=a == 1)
                last.then_inc(s["multiplied"], 1)
            for u in range(UN):
                step(u, u, True)
            with eng.Fori(1, T2 // UN) as i:
                for u in range(UN):
                    step(i * UN + u, u, False)


def gcn_phase(K, z, dinv, bias):
    with ExitStack() as ctx:
        pO = [K.pb("n_pO%d" % b, [128, 2, 512], FP32, ctx) for b in range(2)]
        s = {n: K.sem("n_" + n) for n in ("bias_loaded", "multiplied", "added")}
        block = ctx.enter_context(K.nc.Block())

        @block.sync
        def _(eng):
            eng.dma_start(bias[:, :], K.ins["L1_gnn_b_gcn"].partition_broadcast(P)).then_inc(s["bias_loaded"], 16)

        @block.tensor
        def _(eng):
            for i in range(NT):
                if i >= 2:
                    eng.wait_ge(s["added"], i - 1)
                for k in range(NT):
                    for h in range(2):
                        last = eng.matmul(pO[i % 2][0:P, h, 0:HC], K.counts[:, k, i * P:(i + 1) * P], z[:, k, h * HC:(h + 1) * HC],
                                          start=k == 0, stop=k == NT - 1)
                last.then_inc(s["multiplied"], 1)

        @block.vector
        def _(eng):
            link = chain(eng, K.dve_chain)
            eng.wait_ge(s["bias_loaded"], 16)
            link(eng.tensor_tensor(K.x[:, :, :], K.x[:, :, :], bc(bias[:, :].unsqueeze(1), [P, NT, C]), ALU.add))
            for i in range(NT):
                link(eng.scalar_tensor_tensor(K.x[:, i, :], z[:, i, :], dinv[:, i:i + 1], K.x[:, i, :], ALU.mult, ALU.add))
                eng.wait_ge(s["multiplied"], i + 1)
                xs = K.x[:, i, :].rearrange("p (b n) -> p b n", b=2)
                eng.scalar_tensor_tensor(xs, pO[i % 2][0:P, :, 0:HC], dinv[:, i:i + 1], xs, ALU.mult, ALU.add).then_inc(s["added"], 1)


def rgcn_phase(K):
    nc, ins = K.nc, K.ins
    with ExitStack() as ctx:
        sb = lambda n, s, d: K.sb("q_" + n, s, d, ctx)
        xT = sb("xT", [128, 2, KC, XW], FP16)
        parts = sb("parts", [P, NT, 2, C], FP16)
        wstage = sb("wstage", [128, 2, KC, C], FP32)
        wring = sb("wring", [128, 2, 2, KC, C], FP16)
        xn = sb("xn", [P, NT, C], FP32)
        h1 = sb("h1", [P, NT, C], FP32)
        bias = sb("bias", [P, C], FP32)
        dinv = sb("dinv", [P, NT], FP32)
        norm = {"stats": sb("stats", [P, NT, 2, 6], FP32), "mv": sb("mv", [P, NT, 2], FP32), "sd": sb("sd", [P, NT], FP32)}

        def store_rows(eng, T, s):
            eng.dma_start(bias[:, :], ins["L1_gnn_b_rgcn"].partition_broadcast(P)).then_inc(s["extra"], 16)
            eng.wait_ge(T.s["lo_ready"], NT)
            eng.dma_start(K.xn_dram.rearrange("(i p) c -> p i c", p=P), parts[:, :, :, :].rearrange("p i a c -> p i (a c)")).then_inc(s["extra"], 16)
            eng.wait_ge(s["extra"], 32)

        def add_bias(eng, link, s):
            eng.wait_ge(s["extra"], 32)
            eng.wait_ge(s["out_ready"], NT)
            link(eng.tensor_tensor(h1[:, :, :], h1[:, :, :], bc(bias[:, :].unsqueeze(1), [P, NT, C]), ALU.add))

        project_block(K, "q1", xn, norm, xT, parts, wstage[:, 0], wring[:, 0], ins["L1_gnn_W_root"], h1, store_rows, add_bias)
        relation_phase(K, wstage, wring)
        collect_phase(K, h1)

        def degrees(eng, link, s):
            link(eng.tensor_scalar(dinv[:, :], K.deg[:, :], 1.0, None, ALU.add))
            eng.wait_ge(s["out_ready"], NT)

        project_block(K, "q2", h1, None, xT, parts, wstage[:, 0], wring[:, 0], ins["L1_gnn_W_gcn"], xn, None, degrees)
        scale_phase(K, xn, dinv)
        gcn_phase(K, xn, dinv, bias)


def scale_phase(K, z, dinv):
    with ExitStack() as ctx:
        s = {n: K.sem("z_" + n) for n in ("root",)}
        block = ctx.enter_context(K.nc.Block())

        @block.scalar
        def _(eng):
            eng.activation(dinv[:, :], dinv[:, :], ACT.Sqrt).then_inc(s["root"], 1)

        @block.vector
        def _(eng):
            link = chain(eng, K.dve_chain)
            eng.wait_ge(s["root"], 1)
            link(eng.reciprocal(dinv[:, :], dinv[:, :]))
            for i in range(NT):
                last = eng.tensor_scalar(z[:, i, :], z[:, i, :], dinv[:, i:i + 1], None, ALU.mult)
            link(last)


_OUTS = [((N, C), "float32")]
_INS = ["x", "src", "dst", "edge_type_34",
        "L0_gnn_W1", "L0_gnn_a_src1", "L0_gnn_a_dst1", "L0_gnn_b1", "L0_gnn_W2", "L0_gnn_a_src2", "L0_gnn_a_dst2", "L0_gnn_b2",
        "L0_ffn_router_w", "L0_ffn_w1", "L0_ffn_b1", "L0_ffn_w2", "L0_ffn_b2",
        "L1_gnn_W_rel", "L1_gnn_W_root", "L1_gnn_b_rgcn", "L1_gnn_W_gcn", "L1_gnn_b_gcn",
        "L1_ffn_router_w", "L1_ffn_probe_w", "L1_ffn_router_emb", "L1_ffn_fatigue", "L1_ffn_energy",
        "L1_ffn_w_fast1", "L1_ffn_w_slow1", "L1_ffn_h_fast1", "L1_ffn_m_gate1", "L1_ffn_b1",
        "L1_ffn_w_fast2", "L1_ffn_w_slow2", "L1_ffn_h_fast2", "L1_ffn_m_gate2", "L1_ffn_b2"]


def build(nc, ins, out):
    with ExitStack() as ctx:
        K = Core(nc, ctx, ins, out)
        K.x = K.sb("x", [P, NT, C], FP32)
        K.ident = K.sb("ident", [128, 128], FP32)
        K.ident16 = K.sb("ident16", [128, 128], FP16)
        K.zrow = K.sb("zrow", [128, 512], FP16)
        K.counts = K.sb("counts", [P, NT, N], FP32)
        K.maskT = K.sb("maskT", [P, NT, N], BF16)
        K.deg = K.sb("deg", [P, NT], FP32)
        K.slot_src = K.sb("slot_src", [128, T1 + AHEAD], I32)
        K.slot_row = K.sb("slot_row", [128, T1], I32)
        K.slot_inv = K.sb("slot_inv", [128, IDX_BUFS + T1], FP32)
        K.slot_pair = K.sb("slot_pair", [128, T1], I32)
        K.pair_col = K.sb("pair_col", [128, IDX_BUFS], I32)
        K.inv_col = K.sb("inv_col", [128, IDX_BUFS], FP32)
        K.slot_dst = K.sb("slot_dst", [128, T2 + 1], FP32)
        K.rel_row = K.sb("rel_row", [1, T1], I32)
        K.first_row = K.sb("first_row", [1, T1], I32)
        K.bucket_row = K.sb("bucket_row", [1, T2], I32)
        K.start_row = K.sb("start_row", [1, T2], I32)
        K.qinv_dram = nc.dram_tensor("qinv_dram", (REL * N, 1), FP32).ap()
        K.msg_dram = nc.dram_tensor("msg_dram", (E_EDGES + 128, 2 * C), FP16).ap()
        K.xn_dram = nc.dram_tensor("xn_dram", (N, 2 * C), FP16).ap()
        edge_phase(K)
        K.end_phase()
        gat_phase(K)
        K.end_phase()
        ffn0_phase(K)
        K.end_phase()
        rgcn_phase(K)
        K.end_phase()
        ffn1_phase(K)
        K.end_phase()
        store_phase(K)
        K.end_phase()


def kernel(**inputs):
    import numpy as _np
    import concourse.bacc as _bacc
    from concourse import mybir as _mybir
    from concourse.bass_utils import run_bass_kernel_spmd as _run

    nc = _bacc.Bacc("TRN2", target_bir_lowering=False, num_devices=1)
    arrays, ins = {}, {}
    for name in _INS:
        a = _np.ascontiguousarray(inputs[name])
        arrays[f"in_{name}_dram"] = a
        ins[name] = nc.dram_tensor(f"in_{name}_dram", a.shape, _mybir.dt.from_np(a.dtype), kind="ExternalInput").ap()
    outs = []
    for i, (shape, dtype) in enumerate(_OUTS):
        dt = _mybir.dt.from_np(_np.dtype(dtype))
        outs.append(nc.dram_tensor(f"out_{i}_dram", shape, dt, kind="ExternalOutput").ap())
    build(nc, ins, outs[0])
    r = _run(nc, [arrays], core_ids=[0])
    return r.results[0]["out_0_dram"]
```

```python
import concourse.bass as bass
from concourse import mybir
from contextlib import ExitStack, contextmanager

FP32, FP16, BF16, I32 = (mybir.dt.float32, mybir.dt.float16, mybir.dt.bfloat16, mybir.dt.int32)
ALU = mybir.AluOpType
ACT = mybir.ActivationFunctionType
AX = mybir.AxisListType

N, C = 625, 768
E_EDGES = 10000
P, NT = 125, 5
PP = P + 1
KC = C // 128
HC = C // 2
EP, EJ = 125, 80
REL = 34
W_SCALE = 64.0
T1 = REL + E_EDGES // 128
T1 += T1 % 2
T2 = (E_EDGES + NT * 127) // 128
T2 += -T2 % 6
UN = 4
TURNS = T1 // UN
HOTS = 4
UC = 6
MAXT = (E_EDGES + 127) // 128
NEG = -1.0e30
HALF = 313
XW = 2 * HALF
HEADS, HD = 8, 96
T_EARLY = T1 // 3 // 4 * 4
IDX_BUFS = 4
AHEAD = 3
EXP, F, FT = 8, 192, 12


class Tally:

    def __init__(self, sem):
        self.sem, self.base, self.n = sem, 0, 0

    def value(self):
        return self.base + self.n

    def up(self, ins, k=1):
        ins.then_inc(self.sem, k)
        self.n += k
        return ins

    @contextmanager
    def loop(self, i, per, times, first=0):
        start = self.n - first * per
        self.base, self.n = i * per + start, 0
        yield
        assert self.n == per, (self.n, per)
        self.base, self.n = 0, start + per * times


def chain(eng, tally):
    def link(ins):
        tally.up(ins)
        eng.wait_ge(tally.sem, tally.value())
    return link


def bc(ap, shape):
    return ap.to_broadcast(shape)


class Core:

    def __init__(self, nc, ctx, ins, out):
        self.nc, self.ctx, self.ins, self.out = nc, ctx, ins, out
        self.sems = []
        self.dve_chain = Tally(self.sem("dve_chain"))
        self.pool_chain = Tally(self.sem("pool_chain"))
        self.sems = []

    def sem(self, name):
        handle = self.nc.alloc_semaphore(name)
        self.sems.append(handle)
        return handle

    def end_phase(self):
        self.nc.clear_and_free_semaphores(self.sems)
        self.nc.all_engine_barrier()
        self.sems = []

    def sb(self, name, shape, dt, ctx=None):
        return (ctx or self.ctx).enter_context(self.nc.sbuf_tensor(name, shape, dt))

    def pb(self, name, shape, dt=FP32, ctx=None):
        return (ctx or self.ctx).enter_context(self.nc.psum_tensor(name, shape, dt))


def edge_phase(K):
    nc, ins = K.nc, K.ins
    with ExitStack() as ctx:
        sb = lambda n, s, d: K.sb(n, s, d, ctx)
        edges_in = sb("edges_in", [EP, 3, EJ], I32)
        srcf, dstf, etf = (sb(n, [EP, EJ], FP32) for n in ("srcf", "dstf", "etf"))
        bucket = sb("bucket", [EP, EJ], FP32)
        bstep = sb("bstep", [EP, EJ], FP32)
        src1 = sb("src1", [EP, EJ], FP32)
        zero = sb("zero", [128, 1], FP32)
        zero16 = sb("zero16", [EP, 512], FP16)
        iota_n = sb("iota_n", [EP, N], FP16)
        iota_lo = sb("iota_lo", [EP, 128], FP16)
        iota_t = sb("iota_t", [128, T1], FP32)
        iota_t16 = sb("iota_t16", [128, T1], FP16)
        iota_g = sb("iota_g", [128, REL], FP32)
        iota_k = sb("iota_k", [128, MAXT], FP32)
        tri = sb("tri", [EP, EP], FP32)
        ones = sb("ones", [EP, 128], FP32)
        R = sb("R", [EP, REL, EJ], FP16)
        B = sb("B", [EP, NT, EJ], FP16)
        S = sb("S", [EP, REL, EJ], FP32)
        cmp_ = sb("cmp_", [128, T1 * REL], FP32)
        rowcnt = sb("rowcnt", [EP, REL], FP32)
        rowcntb = sb("rowcntb", [EP, NT], FP32)
        small = {g: {n: sb(f"{n}{g}", [128, g], FP32) for n in ("nt", "tiles", "tin", "tex", "ninc", "start", "k", "k2", "d")}
                 for g in (REL, NT)}
        pos1, pos2, pos2p = (sb(n, [EP, EJ], FP32) for n in ("pos1", "pos2", "pos2p"))
        posi = sb("posi", [EP, EJ], I32)
        parti = sb("parti", [EP, EJ], I32)
        lo1, hi1, plo1, phi = (sb(n, [EP, EJ], FP32) for n in ("lo1", "hi1", "plo1", "phi"))
        pool_edges = sb("pool_edges", [EP, 2, EJ], FP32)
        pool_col = sb("pool_col", [EP, HOTS, 2], FP32)
        hi2, dstl1 = (pool_edges[:, n, :] for n in range(2))
        lo2 = sb("lo2", [EP, EJ], FP32)
        square = sb("square", [EP, HOTS, 128], FP32)
        oh_s = sb("oh_s", [EP, HOTS, N], FP16)
        oh_d = sb("oh_d", [EP, HOTS, N], FP16)
        oh_lo1 = sb("oh_lo1", [EP, HOTS, 128], FP16)
        oh_lo2 = sb("oh_lo2", [EP, HOTS, 128], FP16)
        val1 = sb("val1", [EP, HOTS, 4, T1], FP16)
        val2 = sb("val2", [EP, HOTS, T2], FP16)
        relf = sb("relf", [128, T1], FP32)
        livef = sb("livef", [1, TURNS + 1], FP32)
        firstf = sb("firstf", [128, T1], FP32)
        buckf = sb("buckf", [128, T2], FP32)
        startf = sb("startf", [128, T2], FP32)
        slot = sb("slot", [128, 4, T1], FP32)
        tmp = sb("tmp", [128, T1], FP32)
        qinv = sb("qinv", [P, NT, REL], FP32)
        CT = sb("CT", [P, NT, N], FP32)
        reli = sb("reli", [128, T1], I32)

        s = {n: K.sem("e_" + n) for n in (
            "edges_loaded", "x_loaded", "consts_ready", "rowcnt_ready", "prefix_ready", "ranks_ready", "prefix_used",
            "products_done", "counts_stored", "rest_stored", "slots_ready", "pool_col_ready", "pool_slots_ready", "squared", "act_slots_ready", "slots_free", "transposed",
            "ct_stored", "qinv_ready", "qinv_stored")}

        with ExitStack() as pctx:
            acc = K.pb("acc", [128, 8, 512], FP32, pctx)
            REST = N - 512

            def count_piece(i, piece):
                if piece == 0:
                    return acc[0:P, i, :], slice(0, 512)
                b, o = (5, i * REST) if i < 4 else (6, 0)
                return acc[0:P, b, o:o + REST], slice(512, N)

            block = ctx.enter_context(nc.Block())

            @block.sync
            def _(eng):
                for a, name in enumerate(("src", "dst", "edge_type_34")):
                    eng.dma_start(edges_in[:, a, :], ins[name].rearrange("(p j) -> p j", j=EJ)).then_inc(s["edges_loaded"], 16)
                eng.dma_start(K.x[:, :, :], ins["x"].rearrange("(i p) c -> p i c", p=P)).then_inc(s["x_loaded"], 16)
                eng.wait_ge(s["x_loaded"], 16)
                eng.wait_ge(s["qinv_ready"], 1)
                eng.dma_start(K.qinv_dram.rearrange("(i p r) a -> p i (r a)", p=P, r=REL), qinv[:, :, :]).then_inc(s["qinv_stored"], 16)
                eng.wait_ge(s["consts_ready"], 12)
                eng.dma_start(K.msg_dram[E_EDGES:E_EDGES + 128, :].rearrange("p (a b) -> p a b", a=3),
                              bc(K.zrow[:, :].unsqueeze(1), [128, 3, 512])).then_inc(s["qinv_stored"], 16)
                eng.wait_ge(s["qinv_stored"], 32)

            @block.gpsimd
            def _(eng):
                ready = s["consts_ready"]
                eng.sem_inc(s["slots_free"], HOTS)
                eng.memset(zero[:, :], 0.0).then_inc(ready, 1)
                eng.memset(zero16[:, :], 0.0).then_inc(ready, 1)
                eng.iota(iota_g[:, :], pattern=[[1, REL]], base=0, channel_multiplier=0, allow_small_or_imprecise_dtypes=True).then_inc(ready, 1)
                eng.iota(iota_n[:, :], pattern=[[1, N]], base=0, channel_multiplier=0, allow_small_or_imprecise_dtypes=True).then_inc(ready, 1)
                eng.iota(iota_k[:, :], pattern=[[128, MAXT]], base=0, channel_multiplier=0, allow_small_or_imprecise_dtypes=True).then_inc(ready, 1)
                eng.iota(iota_lo[:, :], pattern=[[1, 128]], base=0, channel_multiplier=0, allow_small_or_imprecise_dtypes=True).then_inc(ready, 1)
                eng.iota(iota_t[:, :], pattern=[[1, T1]], base=0, channel_multiplier=0, allow_small_or_imprecise_dtypes=True).then_inc(ready, 1)
                eng.iota(iota_t16[:, :], pattern=[[1, T1]], base=0, channel_multiplier=0, allow_small_or_imprecise_dtypes=True).then_inc(ready, 1)
                eng.memset(ones[:, :], 1.0).then_inc(ready, 1)
                eng.memset(K.zrow[:, :], 0.0).then_inc(ready, 1)
                link = chain(eng, K.pool_chain)
                link(eng.memset(tri[:, :], 1.0))
                link(eng.memset(K.ident[:, :], 0.0))
                eng.affine_select(out=tri[:, :], in_=tri[:, :], compare_op=ALU.is_gt, fill=0.0, base=0,
                                  pattern=[[1, EP]], channel_multiplier=-1).then_inc(ready, 1)
                eng.affine_select(out=K.ident[:, :], in_=K.ident[:, :], compare_op=ALU.not_equal, fill=1.0, base=0,
                                  pattern=[[1, 128]], channel_multiplier=-1).then_inc(ready, 1)
                eng.wait_ge(s["ranks_ready"], 1)
                with eng.Fori(0, EJ // HOTS) as i:
                    for u in range(HOTS):
                        j = i * HOTS + u
                        eng.wait_ge(s["slots_free"], j + 1)
                        eng.tensor_copy(pool_col[:, u, :], pool_edges[:, :, bass.ds(j, 1)].rearrange("p n a -> p (n a)")
                                        ).then_inc(s["pool_col_ready"], 1)
                        eng.wait_ge(s["pool_col_ready"], j + 1)
                        eng.nop(nofuse=True)
                        eng.tensor_scalar(val2[:, u, :], iota_t16[0:EP, 0:T2], pool_col[:, u, 0:1], pool_col[:, u, 1:2], ALU.is_equal, ALU.mult
                                          ).then_inc(s["pool_slots_ready"], 1)
                for i in range(NT):
                    eng.wait_ge(s["ct_stored"], i + 1)
                    eng.tensor_scalar(K.maskT[:, i, :], CT[:, i, :], 0.0, NEG, ALU.is_equal, ALU.mult)

            @block.vector
            def _(eng):
                link = chain(eng, K.dve_chain)

                def ranks(G, onehot, rows, d, ready_at, floor, positions):
                    sc = S[:, 0:G, :]
                    flat = lambda a: a.rearrange("p g j -> p (g j)")
                    link(eng.tensor_tensor_scan(flat(sc), flat(onehot[:, :, :]), bc(zero[0:EP, :], [EP, G * EJ]), 0.0, ALU.add, ALU.add))
                    last = S[:, 0:G, EJ - 1]
                    link(eng.tensor_copy(rows[:, 0:1], last[:, 0:1]))
                    eng.tensor_tensor(rows[:, 1:G], last[:, 1:G], last[:, 0:G - 1], ALU.subtract).then_inc(s["rowcnt_ready"], 1)
                    eng.wait_ge(s["prefix_ready"], ready_at)
                    link(eng.tensor_copy(d["nt"][:, :], acc[:, 7, 64:64 + G]))
                    c3 = cmp_[:, 0:G * MAXT].rearrange("p (g k) -> p g k", k=MAXT)
                    link(eng.tensor_tensor(c3, bc(d["nt"][:, :].unsqueeze(2), [128, G, MAXT]),
                                           bc(iota_k[:, :].unsqueeze(1), [128, G, MAXT]), ALU.is_gt))
                    link(eng.tensor_reduce(d["tiles"][:, :], c3, AX.X, ALU.add))
                    link(eng.tensor_scalar(d["tiles"][:, :], d["tiles"][:, :], floor, None, ALU.max))
                    link(eng.tensor_tensor_scan(d["tin"][:, :], d["tiles"][:, :], bc(zero[:, :], [128, G]), 0.0, ALU.add, ALU.add))
                    link(eng.tensor_tensor(d["tex"][:, :], d["tin"][:, :], d["tiles"][:, :], ALU.subtract))
                    link(eng.tensor_tensor_scan(d["ninc"][:, :], d["nt"][:, :], bc(zero[:, :], [128, G]), 0.0, ALU.add, ALU.add))
                    link(eng.tensor_tensor(d["start"][:, :], d["ninc"][:, :], d["nt"][:, :], ALU.subtract))
                    for base, scale, k, pos in ((d["tex"], 128.0, d["k"], positions[0]), (d["start"], 1.0, d["k2"], positions[1])):
                        if pos is None:
                            continue
                        link(eng.scalar_tensor_tensor(k[0:EP, :], base[0:EP, :], scale, acc[0:EP, 7, 0:G], ALU.mult, ALU.add))
                        link(eng.tensor_tensor(k[0:EP, 1:G], k[0:EP, 1:G], last[:, 0:G - 1], ALU.subtract))
                        m = cmp_[0:EP, 0:G * EJ].rearrange("p (g j) -> p g j", j=EJ)
                        link(eng.tensor_tensor(m, sc, bc(k[0:EP, :].unsqueeze(2), [EP, G, EJ]), ALU.add))
                        link(eng.tensor_tensor(m, m, onehot[:, :, :], ALU.mult))
                        link(eng.tensor_reduce(pos[:, :], m.rearrange("p g j -> p j g"), AX.X, ALU.add))
                        link(eng.tensor_scalar(pos[:, :], pos[:, :], 1.0, None, ALU.subtract))

                def split(pos, lo, hi, lo_plus):
                    link(eng.tensor_copy(posi[:, :], pos[:, :]))
                    link(eng.tensor_scalar(parti[:, :], posi[:, :], 127, None, ALU.bitwise_and))
                    link(eng.tensor_copy(lo[:, :], parti[:, :]))
                    if lo_plus:
                        link(eng.tensor_scalar(lo[:, :], lo[:, :], float(lo_plus), None, ALU.add))
                    link(eng.tensor_scalar(parti[:, :], posi[:, :], 7, None, ALU.logical_shift_right))
                    link(eng.tensor_copy(hi[:, :], parti[:, :]))

                eng.wait_ge(s["edges_loaded"], 48)
                eng.wait_ge(s["consts_ready"], 12)
                link(eng.tensor_copy(srcf[:, :], edges_in[:, 0, :]))
                link(eng.tensor_copy(dstf[:, :], edges_in[:, 1, :]))
                link(eng.tensor_copy(etf[:, :], edges_in[:, 2, :]))
                link(eng.tensor_copy(K.ident16[:, :], K.ident[:, :]))

                eb = lambda a, g: bc(a[:, :].unsqueeze(1), [EP, g, EJ])
                ib = lambda g: bc(iota_g[0:EP, 0:g].unsqueeze(2), [EP, g, EJ])
                link(eng.tensor_tensor(R[:, :, :], eb(etf, REL), ib(REL), ALU.is_equal))
                link(eng.tensor_scalar(bucket[:, :], dstf[:, :], float(P), None, ALU.is_ge))
                for k in range(2, NT):
                    link(eng.tensor_scalar(bstep[:, :], dstf[:, :], float(P * k), None, ALU.is_ge))
                    link(eng.tensor_tensor(bucket[:, :], bucket[:, :], bstep[:, :], ALU.add))
                link(eng.tensor_tensor(B[:, :, :], eb(bucket, NT), ib(NT), ALU.is_equal))
                link(eng.tensor_scalar(bstep[:, :], bucket[:, :], -float(P), 1.0, ALU.mult, ALU.add))
                link(eng.tensor_tensor(dstl1[:, :], bstep[:, :], dstf[:, :], ALU.add))
                link(eng.tensor_scalar(src1[:, :], srcf[:, :], 1.0, None, ALU.add))
                ranks(REL, R, rowcnt, small[REL], 1, 1.0, (pos1, None))
                ranks(NT, B, rowcntb, small[NT], 2, 0.0, (pos2p, pos2))
                split(pos1, lo1, hi1, 0)
                split(pos2p, lo2, hi2, 0)
                split(pos2, plo1, phi, 0)
                link(eng.tensor_scalar(lo2[:, :], lo2[:, :], -1.0, None, ALU.mult))
                eng.sem_inc(s["prefix_used"], 1)
                eng.sem_inc(s["ranks_ready"], 1)

                with eng.Fori(0, EJ // HOTS) as i:
                    for u in range(HOTS):
                        j = i * HOTS + u
                        col = lambda a: a[:, bass.ds(j, 1)]
                        if u % 2 == 0:
                            eng.wait_ge(s["slots_free"], j + 2)
                        eng.tensor_scalar(oh_s[:, u, :], iota_n[:, :], col(srcf), None, ALU.is_equal)
                        eng.tensor_scalar(oh_d[:, u, :], iota_n[:, :], col(dstf), None, ALU.is_equal)
                        eng.tensor_scalar(oh_lo1[:, u, :], iota_lo[:, :], col(lo1), None, ALU.is_equal)
                        for a, v in enumerate((src1, dstf, phi, plo1)):
                            last = eng.tensor_scalar(val1[:, u, a, :], iota_t16[0:EP, :], col(hi1), col(v), ALU.is_equal, ALU.mult)
                        last.then_inc(s["slots_ready"], 1)
                eng.wait_ge(s["products_done"], 1)
                a, cols = count_piece(NT - 1, 1)
                eng.tensor_copy(K.counts[:, NT - 1, cols], a).then_inc(s["rest_stored"], 1)
                link(eng.tensor_scalar(qinv[:, :, :], acc[0:P, 6, REST + T2:REST + T2 + NT * REL].rearrange("p (i r) -> p i r", r=REL), 1.0, W_SCALE,
                                       ALU.max, ALU.mult))
                eng.reciprocal(qinv[:, :, :], qinv[:, :, :]).then_inc(s["qinv_ready"], 1)
                link(eng.tensor_copy(slot[:, :, :].rearrange("p a t -> p (a t)"), acc[:, 7, 0:4 * T1]))
                link(eng.memset(K.slot_dst[:, T2:T2 + 1], -1.0))
                link(eng.tensor_scalar(K.slot_dst[:, 0:T2], acc[:, 6, REST:REST + T2], 1.0, None, ALU.subtract))
                d = small[REL]
                c3 = cmp_[:, :].rearrange("p (t g) -> p t g", g=REL)
                link(eng.tensor_tensor(c3, bc(iota_t[:, :].unsqueeze(2), [128, T1, REL]), bc(d["tin"][:, :].unsqueeze(1), [128, T1, REL]), ALU.is_ge))
                link(eng.tensor_reduce(relf[:, :], c3, AX.X, ALU.add))
                link(eng.tensor_scalar(relf[:, :], relf[:, :], float(REL - 1), None, ALU.min))
                link(eng.memset(firstf[:, 0:1], 1.0))
                link(eng.tensor_tensor(firstf[:, 1:T1], relf[:, 1:T1], relf[:, 0:T1 - 1], ALU.not_equal))
                link(eng.tensor_copy(K.rel_row[:, :], relf[0:1, :]))
                link(eng.scalar_tensor_tensor(firstf[:, :], relf[:, :], float(REL - 1), firstf[:, :], ALU.is_lt, ALU.mult))
                link(eng.tensor_scalar(livef[:, 0:TURNS], iota_t[0:1, 0:TURNS], float(UN), d["tin"][0:1, REL - 1:REL], ALU.mult, ALU.is_lt))
                link(eng.tensor_reduce(livef[:, TURNS:TURNS + 1], livef[:, 0:TURNS], AX.X, ALU.add))
                link(eng.tensor_copy(K.live_row[:, :], livef[:, :]))
                link(eng.tensor_copy(reli[:, :], relf[:, :]))
                link(eng.tensor_scalar(reli[:, :], reli[:, :], 1, None, ALU.bitwise_and))
                link(eng.tensor_copy(tmp[:, :], reli[:, :]))
                link(eng.tensor_scalar(tmp[:, :], tmp[:, :], -1.0, 2.0, ALU.mult, ALU.add))
                link(eng.tensor_tensor(firstf[:, :], firstf[:, :], tmp[:, :], ALU.mult))
                link(eng.tensor_copy(K.first_row[:, :], firstf[0:1, :]))
                d = small[NT]
                c3 = cmp_[:, 0:T2 * NT].rearrange("p (t g) -> p t g", g=NT)
                tb = bc(iota_t[:, 0:T2].unsqueeze(2), [128, T2, NT])
                link(eng.tensor_tensor(c3, tb, bc(d["tin"][:, :].unsqueeze(1), [128, T2, NT]), ALU.is_ge))
                link(eng.tensor_reduce(buckf[:, :], c3, AX.X, ALU.add))
                link(eng.tensor_scalar(buckf[:, :], buckf[:, :], float(NT - 1), None, ALU.min))
                link(eng.tensor_copy(K.bucket_row[:, :], buckf[0:1, :]))
                link(eng.scalar_tensor_tensor(d["d"][:, :], d["tex"][:, :], -128.0, d["start"][:, :], ALU.mult, ALU.add))
                link(eng.tensor_tensor(c3, bc(buckf[:, :].unsqueeze(2), [128, T2, NT]), bc(iota_g[:, 0:NT].unsqueeze(1), [128, T2, NT]), ALU.is_equal))
                link(eng.tensor_tensor(c3, c3, bc(d["d"][:, :].unsqueeze(1), [128, T2, NT]), ALU.mult))
                link(eng.tensor_reduce(startf[:, :], c3, AX.X, ALU.add))
                link(eng.scalar_tensor_tensor(startf[:, :], iota_t[:, 0:T2], 128.0, startf[:, :], ALU.mult, ALU.add))
                link(eng.tensor_scalar(startf[:, :], startf[:, :], float(E_EDGES), None, ALU.min))
                link(eng.tensor_copy(K.start_row[:, :], startf[0:1, :]))

                link(eng.tensor_scalar(tmp[:, :], slot[:, 0, :], 1.0, 0.0, ALU.subtract, ALU.max))
                link(eng.tensor_copy(K.slot_src[:, 0:T1], tmp[:, :]))
                link(eng.memset(K.slot_src[:, T1:T1 + AHEAD], 0))
                link(eng.scalar_tensor_tensor(tmp[:, :], slot[:, 2, :], 128.0, slot[:, 3, :], ALU.mult, ALU.add))
                link(eng.tensor_scalar(slot[:, 2, :], slot[:, 0, :], 0.0, 2.0 * E_EDGES, ALU.is_equal, ALU.mult))
                link(eng.tensor_tensor(tmp[:, :], tmp[:, :], slot[:, 2, :], ALU.add))
                link(eng.tensor_copy(K.slot_row[:, :], tmp[:, :]))
                link(eng.scalar_tensor_tensor(tmp[:, :], slot[:, 1, :], float(REL), relf[:, :], ALU.mult, ALU.add))
                link(eng.tensor_copy(K.slot_pair[:, :], tmp[:, :]))

                eng.wait_ge(s["ct_stored"], NT)
                eng.tensor_reduce(K.deg[:, :], CT[:, :, :], AX.X, ALU.add)

            @block.scalar
            def _(eng):
                eng.wait_ge(s["ranks_ready"], 1)
                with eng.Fori(0, EJ // HOTS) as i:
                    for u in range(HOTS):
                        j = i * HOTS + u
                        eng.wait_ge(s["slots_free"], j + 1)
                        eng.activation(square[:, u, :], iota_lo[:, :], ACT.Square, bias=lo2[:, bass.ds(j, 1)]).then_inc(s["squared"], 1)
                        eng.wait_ge(s["squared"], j + 1)
                        eng.activation(oh_lo2[:, u, :], square[:, u, :], ACT.Relu, bias=1.0, scale=-1.0).then_inc(s["act_slots_ready"], 1)
                eng.wait_ge(s["products_done"], 1)
                for i in range(NT):
                    for piece in range(2 if i < NT - 1 else 1):
                        a, cols = count_piece(i, piece)
                        eng.copy(K.counts[:, i, cols], a).then_inc(s["counts_stored"], 1)
                for i in range(NT):
                    eng.wait_ge(s["transposed"], i + 1)
                    eng.copy(CT[:, i, :], acc[0:P, 2 * (i % 2):2 + 2 * (i % 2), :].rearrange("p b n -> p (b n)")[:, 0:N]).then_inc(s["ct_stored"], 1)

            @block.tensor
            def _(eng):
                kw = dict(skip_group_check=True)
                eng.wait_ge(s["consts_ready"], 12)
                z, zr = zero16[:, 0:P], zero16[:, :]

                def zeros(banks, m, start, stop):
                    for b in banks:
                        last = eng.matmul(acc[0:m, b, :], zero16[:, 0:m], zr, start=start, stop=stop, **kw)
                    return last
                zeros(range(6), P, True, False)
                zeros((6,), 128, True, False)
                for n, (rows, G) in enumerate(((rowcnt, REL), (rowcntb, NT))):
                    eng.wait_ge(s["rowcnt_ready"], n + 1)
                    eng.matmul(acc[0:EP, 7, 0:G], tri[:, :], rows[:, :], start=True, stop=True)
                    eng.matmul(acc[:, 7, 64:64 + G], ones[:, :], rows[:, :], start=True, stop=True).then_inc(s["prefix_ready"], 1)
                eng.wait_ge(s["prefix_used"], 1)
                zeros((7,), 128, True, False)
                with eng.Fori(0, EJ // HOTS) as i:
                    for u in range(HOTS):
                        eng.wait_ge(s["pool_slots_ready"], i * HOTS + (u + 1))
                        eng.wait_ge(s["act_slots_ready"], i * HOTS + (u + 1))
                        eng.matmul(acc[:, 6, REST:REST + T2], oh_lo2[:, u, :], val2[:, u, :], start=False, stop=False, **kw)
                        eng.wait_ge(s["slots_ready"], i * HOTS + (u + 1))
                        eng.matmul(acc[:, 7, 0:4 * T1], oh_lo1[:, u, :], val1[:, u, :, :].rearrange("p a t -> p (a t)"), start=False, stop=False, **kw)
                        onehot = R[:, :, bass.ds(i * HOTS + u, 1)].rearrange("p g a -> p (g a)")
                        for t in range(NT):
                            tile = slice(t * P, (t + 1) * P)
                            at = REST + T2 + t * REL
                            eng.matmul(acc[0:P, 6, at:at + REL], oh_d[:, u, tile], onehot, start=False, stop=False, **kw)
                            for piece in range(2):
                                a, cols = count_piece(t, piece)
                                last = eng.matmul(a, oh_s[:, u, tile], oh_d[:, u, cols], start=False, stop=False, **kw)
                        last.then_inc(s["slots_free"], 1)
                zeros(range(6), P, False, True)
                zeros((6, 7), 128, False, True).then_inc(s["products_done"], 1)
                eng.wait_ge(s["counts_stored"], 2 * NT - 1)
                eng.wait_ge(s["rest_stored"], 1)
                for i in range(NT):
                    if i >= 2:
                        eng.wait_ge(s["ct_stored"], i - 1)
                    for k in range(NT):
                        flat = acc[0:P, 2 * (i % 2):2 + 2 * (i % 2), :].rearrange("p b n -> p (b n)")
                        lo, hi = k * P, (k + 1) * P
                        src = K.counts[:, k, i * P:(i + 1) * P]
                        if hi <= 512:
                            last = eng.transpose(flat[:, lo:hi], src, K.ident[0:P, 0:P])
                        else:
                            c = 512 - lo
                            eng.matmul(flat[:, lo:512], src, K.ident[0:P, 0:c], start=True, stop=True)
                            last = eng.matmul(flat[:, 512:hi], src, K.ident[0:P, c:P], start=True, stop=True)
                    last.then_inc(s["transposed"], 1)


def gather_inverse_counts(K, eng, s, start, end):
    pair, got = K.pair_col, K.inv_col

    def gather_inv(u):
        eng.indirect_dma_start(out=got[:, u:u + 1], out_offset=None, in_=K.qinv_dram,
                               in_offset=bass.IndirectOffsetOnAxis(ap=pair[:, u:u + 1], axis=0)).then_inc(s["gathered_%d" % u], 16)
    eng.tensor_copy(pair[:, :], K.slot_pair[:, start:start + IDX_BUFS]).then_inc(s["pair_ready"], 1)
    eng.wait_ge(s["pair_ready"], 1)
    for u in range(IDX_BUFS):
        gather_inv(u)
    times = (end - start) // IDX_BUFS
    with eng.Fori(1, times) as i:
        for u in range(IDX_BUFS):
            t = i * IDX_BUFS + (start + u)
            eng.wait_ge(s["gathered_%d" % u], i * 16)
            eng.tensor_copy(K.slot_inv[:, bass.ds(t, 1)], got[:, u:u + 1])
            eng.tensor_copy(pair[:, u:u + 1], K.slot_pair[:, bass.ds(t, 1)]).then_inc(s["pair_ready"], 1)
            eng.wait_ge(s["pair_ready"], i * IDX_BUFS + (u + 2 - IDX_BUFS))
            eng.nop(nofuse=True)
            gather_inv(u)
    for u in range(IDX_BUFS):
        eng.wait_ge(s["gathered_%d" % u], times * 16)
        eng.tensor_copy(K.slot_inv[:, end + u:end + u + 1], got[:, u:u + 1])


class Transposed:

    def __init__(self, K, name, src, xT, parts, psum, norm=None):
        self.K, self.src, self.xT, self.parts, self.psum, self.norm = K, src, xT, parts, psum, norm
        self.s = {n: K.sem(name + "_" + n) for n in ("var_ready", "sd_ready", "rows_ready", "hi_ready", "lo_ready", "transposed", "copied_even", "copied_odd")}
        if norm:
            self.stats, self.mv, self.sd = norm["stats"], norm["mv"], norm["sd"]

    def _view(self, i):
        p = self.psum[i % 2][:, :, 0:KC * PP].rearrange("p a (k n) -> p a k n", n=PP)[:, :, :, 0:P]
        return self.xT[:, :, :, i * P:(i + 1) * P], p

    def _copy(self, eng, i):
        self_s = self.s
        out, src = self._view(i)
        eng.wait_ge(self_s["transposed"], i + 1)
        for a in range(2):
            if i % 2:
                last = eng.tensor_copy(out[:, a], src[:, a])
            else:
                last = eng.copy(out[:, a], src[:, a])
        last.then_inc(self_s[("copied_even", "copied_odd")[i % 2]], 1)

    def vector(self, eng):
        K, s = self.K, self.s
        link = chain(eng, K.dve_chain)
        if self.norm:
            for i in range(NT):
                for h in range(2):
                    eng.bn_stats(self.stats[:, i, h, :], K.x[:, i, h * HC:(h + 1) * HC])
            link(eng.memset(self.xT[:, :, :, N:XW], 0.0))
            for i in range(NT):
                last = eng.bn_aggr(self.mv[:, i, :], self.stats[:, i, :, :].rearrange("p a b -> p (a b)"))
            link(last)
            eng.tensor_scalar(self.sd[:, :], self.mv[:, :, 1], 1e-5, None, ALU.add).then_inc(s["var_ready"], 1)
            eng.wait_ge(s["sd_ready"], 1)
            link(eng.reciprocal(self.sd[:, :], self.sd[:, :]))
        else:
            link(eng.memset(self.xT[:, :, :, N:XW], 0.0))
        for i in range(NT):
            if self.norm:
                eng.tensor_scalar(self.src[:, i, :], K.x[:, i, :], self.mv[:, i, 0:1], self.sd[:, i:i + 1], ALU.subtract, ALU.mult
                                  ).then_inc(s["rows_ready"], 1)
            eng.wait_ge(s["hi_ready"], i + 1)
            eng.tensor_tensor(self.parts[:, i, 1, :], self.src[:, i, :], self.parts[:, i, 0, :], ALU.subtract).then_inc(s["lo_ready"], 1)
            if i >= 2 and i % 2 == 0:
                self._copy(eng, i - 1)

    def scalar(self, eng):
        K, s = self.K, self.s
        if self.norm:
            eng.wait_ge(s["var_ready"], 1)
            eng.activation(self.sd[:, :], self.sd[:, :], ACT.Sqrt).then_inc(s["sd_ready"], 1)
        for i in range(NT):
            if self.norm:
                eng.wait_ge(s["rows_ready"], i + 1)
            eng.activation(self.parts[:, i, 0, :], self.src[:, i, :], ACT.Copy).then_inc(s["hi_ready"], 1)
            if i >= 1 and i % 2 == 1:
                self._copy(eng, i - 1)
        self._copy(eng, NT - 1)

    def tensor(self, eng):
        K, s = self.K, self.s
        for i in range(NT):
            eng.wait_ge(s["lo_ready"], i + 1)
            if i >= 2:
                eng.wait_ge(s[("copied_even", "copied_odd")[i % 2]], i // 2)
            for a in range(2):
                for k in range(KC):
                    last = eng.transpose(self.psum[i % 2][:, a, k * PP:k * PP + P], self.parts[:, i, a, k * 128:(k + 1) * 128],
                                         K.ident16[0:P, 0:P])
            last.then_inc(s["transposed"], 1)

    def wait_done(self, eng):
        eng.wait_ge(self.s["copied_even"], (NT + 1) // 2)
        eng.wait_ge(self.s["copied_odd"], NT // 2)


class Weights:

    def __init__(self, K, name, dram, stage, parts, group=2):
        self.K, self.dram, self.stage, self.parts = K, dram, stage, parts
        self.chunks, self.group = stage.shape[1], group
        self.loads = (self.chunks + group - 1) // group
        self.s_loaded = [K.sem(name + "_loaded%d" % n) for n in range(self.loads)]
        self.s_hi, self.s_lo = K.sem(name + "_hi_ready"), K.sem(name + "_lo_ready")

    def sync(self, eng):
        for n in range(self.loads):
            a, b = n * self.group, min((n + 1) * self.group, self.chunks)
            for dst, src in self.dram(self.stage, a, b):
                eng.dma_start(dst, src).then_inc(self.s_loaded[n], 16)

    def loaded(self, eng, k):
        n = k // self.group
        a, b = n * self.group, min((n + 1) * self.group, self.chunks)
        eng.wait_ge(self.s_loaded[n], 16 * len(self.dram(self.stage, a, b)))

    def scalar(self, eng):
        for k in range(self.chunks):
            self.loaded(eng, k)
            eng.activation(self.parts[:, 0, k, :], self.stage[:, k, :], ACT.Copy, scale=W_SCALE).then_inc(self.s_hi, 1)

    def vector(self, eng):
        for k in range(self.chunks):
            eng.wait_ge(self.s_hi, k + 1)
            eng.scalar_tensor_tensor(self.parts[:, 1, k, :], self.stage[:, k, :], W_SCALE, self.parts[:, 0, k, :],
                                     ALU.mult, ALU.subtract).then_inc(self.s_lo, 1)

    def ready(self, eng, k):
        eng.wait_ge(self.s_lo, k + 1)


def three_products(eng, out_halves, xh, xl, wh, wl, first, last, **kw):
    ins = None
    for x, ws in ((xh, (wh, wl)), (xl, (wh,))):
        for w in ws:
            for h, out in enumerate(out_halves):
                n = out.shape[-1]
                ins = eng.matmul(out, x, w[:, h * n:(h + 1) * n], start=first and x is xh and w is wh,
                                 stop=last and x is xl, **kw)
    return ins


def project_tiles(eng, psum, xT, W, waits, done, free=None, free_base=0):
    for i in range(NT):
        waits(i)
        if i >= 2:
            eng.wait_ge(free, free_base + i - 1)
        tok = slice(i * P, (i + 1) * P)
        for k in range(KC):
            if i == 0:
                W.ready(eng, k)
            ins = three_products(eng, [psum[i % 2][0:P, h, 0:HC] for h in range(2)], xT[:, 0, k, tok], xT[:, 1, k, tok],
                                 W.parts[:, 0, k, :], W.parts[:, 1, k, :], k == 0, k == KC - 1)
        ins.then_inc(done, 1)


def rows_view(w):
    v = w.rearrange("(k p) n -> p k n", p=128)
    return lambda stage, a, b: [(stage[:, a:b, :], v[:, a:b, :])]


def gat_project(K, name, B, src, norm, w, a_src, a_dst, heads, ch, h_sb):
    nc = K.nc
    with ExitStack() as ctx:
        psum = K.pb(name + "_ps", [128, 8, 512], FP32, ctx)
        pT = [psum[:, 4 + 2 * b:6 + 2 * b, :].bitcast(FP16) for b in range(2)]
        pO = [psum[:, 2 * b:2 * b + 2, :] for b in range(2)]
        T = Transposed(K, name + "_t", src, B["xT"], B["parts"], pT, norm)
        W = Weights(K, name + "_w", rows_view(w), B["stage"], B["wparts"])
        s = {n: K.sem(name + "_" + n) for n in ("a_loaded", "projected", "h_ready", "ones_ready", "pair_ready"
                                                ) + tuple("gathered_%d" % b for b in range(IDX_BUFS))}
        a_bc = B["a_bc"]
        block = ctx.enter_context(nc.Block())

        @block.sync
        def _(eng):
            W.sync(eng)
            for n, a in enumerate((a_src, a_dst)):
                eng.dma_start(a_bc[:, n, :], a.rearrange("h c -> (h c)").partition_broadcast(P)).then_inc(s["a_loaded"], 16)
            eng.wait_ge(s["a_loaded"], 32)

        @block.gpsimd
        def _(eng):
            for i in range(NT):
                last = eng.memset(h_sb[:, i, :, ch:ch + 1], 1.0)
            last.then_inc(s["ones_ready"], 1)
            eng.wait_ge(s["ones_ready"], 1)
            if heads > 1:
                gather_inverse_counts(K, eng, s, 0, T_EARLY)

        @block.vector
        def _(eng):
            link = chain(eng, K.dve_chain)
            T.vector(eng)
            W.vector(eng)
            eng.wait_ge(s["a_loaded"], 32)
            for i in range(NT):
                eng.wait_ge(s["h_ready"], i + 1)
                for n, al in enumerate((B["al_s"], B["al_d"])):
                    prod = B["prod"][:, n, :].rearrange("p (h c) -> p h c", c=ch)
                    link(eng.tensor_tensor(prod, h_sb[:, i, :, 0:ch], a_bc[:, n, :].rearrange("p (h c) -> p h c", c=ch), ALU.mult))
                    link(eng.tensor_reduce(al[:, 0:heads, i], prod, AX.X, ALU.add))

        @block.scalar
        def _(eng):
            T.scalar(eng)
            W.scalar(eng)
            for i in range(NT):
                eng.wait_ge(s["projected"], i + 1)
                for b in range(2):
                    if heads == 1:
                        out, ps = h_sb[:, i, 0, b * HC:(b + 1) * HC], pO[i % 2][0:P, b, 0:HC]
                    else:
                        hb = heads // 2
                        out = h_sb[:, i, b * hb:(b + 1) * hb, 0:ch]
                        ps = pO[i % 2][0:P, b, 0:HC].rearrange("p (h c) -> p h c", c=ch)
                    last = eng.activation(out, ps, ACT.Copy, scale=1.0 / W_SCALE)
                last.then_inc(s["h_ready"], 1)

        @block.tensor
        def _(eng):
            T.tensor(eng)
            T.wait_done(eng)
            project_tiles(eng, pO, B["xT"], W, lambda i: None, s["projected"], s["h_ready"])


def column_pieces(k):
    lo, hi = k * P, (k + 1) * P
    if hi <= 512:
        return [(lo, hi, 0)]
    return [(lo, 512, 0), (512, hi, 512 - lo)]


def gat_attend(K, name, B, heads, ch, h_sb, finish):
    nc = K.nc
    pair = min(heads, 2)
    with ExitStack() as ctx:
        psum = K.pb(name + "_ps", [128, 8, 512], FP32, ctx)
        flat = lambda b: psum[:, b:b + 2, :].rearrange("p b n -> p (b n)")
        row = lambda b: flat(b)[0:P, 0:N]
        s = {n: K.sem(name + "_" + n) for n in ("cs_ready", "als_ready", "max_done", "uv_made", "uv_ready", "bc_ready", "rows_copied", "t1_ready", "arg_ready",
                                                "e_ready", "p_ready", "pv_done", "out_free", "finish_a", "finish_b", "bias_loaded", "pair_ready"
                                                ) + tuple("gathered_%d" % b for b in range(IDX_BUFS))}
        mx, mm, u_all, v_all, s2_all = (B["small"][:, n, 0:heads, :] for n in range(5))
        junk = B["parts"][:, :, :, :].bitcast(BF16).rearrange("p i a c -> p (i a c)")[:, 0:NT * N].rearrange("p (i n) -> p i n", n=N)
        t1, arg, ex, rec = B["t1"], B["arg"], B["ex"], B["rec"]
        block = ctx.enter_context(nc.Block())
        rows = B["rows"]
        sums = [psum[0:P, 4 + b, 0:NT * (ch + 1)].rearrange("p (i c) -> p i c", c=ch + 1) for b in range(2)] if heads > 1 else None

        def of(a, h):
            return a[:, h, :] if isinstance(h, int) else a[:, bass.ds(h, 1), :].rearrange("p a i -> p (a i)")

        def column(a, h, k):
            return a[:, h, k:k + 1] if isinstance(h, int) else a[:, bass.ds(h, 1), k:k + 1].rearrange("p a i -> p (a i)")

        def turns(eng, step, tally=None, per=0):
            for b in range(pair):
                step(b, b)
            if heads > 2:
                with eng.Fori(1, heads // 2) as i:
                    if tally:
                        with tally.loop(i, per, heads // 2, 1):
                            for b in range(2):
                                step(i * 2 + b, b)
                    else:
                        for b in range(2):
                            step(i * 2 + b, b)

        def over(h, least):
            return not isinstance(h, int) or h >= least

        @block.sync
        def _(eng):
            eng.dma_start(B["bias"][:, :], finish["bias"].partition_broadcast(P)).then_inc(s["bias_loaded"], 16)
            eng.wait_ge(s["bias_loaded"], 16)

        @block.vector
        def _(eng):
            link = chain(eng, K.dve_chain)

            def maximum(h, b):
                eng.wait_ge(s["als_ready"], h + 1)
                eng.nop(nofuse=True)
                for i in range(NT):
                    last = eng.tensor_tensor_reduce(out=junk[:, i, :], in0=row(2 * b), in1=K.maskT[:, i, :], scale=1.0, scalar=-3.0e38,
                                                    op0=ALU.add, op1=ALU.max, accum_out=B["max_cur"][:, b, i:i + 1])
                link(last)
                eng.tensor_copy(of(mx, h), B["max_cur"][:, b, :]).then_inc(s["max_done"], 1)
            turns(eng, maximum, K.dve_chain, 2)
            eng.wait_ge(s["max_done"], heads)
            a_s, a_d = B["al_s"][:, 0:heads, :], B["al_d"][:, 0:heads, :]
            link(eng.tensor_scalar(s2_all, a_s, 0.2, None, ALU.mult))
            link(eng.tensor_tensor(mm, a_d, mx, ALU.add))
            link(eng.scalar_tensor_tensor(mm, mm, 0.2, mm, ALU.mult, ALU.max))
            link(eng.tensor_tensor(u_all, a_d, mm, ALU.subtract))
            eng.scalar_tensor_tensor(v_all, a_d, 0.2, mm, ALU.mult, ALU.subtract).then_inc(s["uv_made"], 1)

            def weights(h, b):
                prob = B["prob"][b]
                eng.wait_ge(s["rows_copied"], h + 1)

                def make_arg(k):
                    eng.wait_ge(s["t1_ready"], h * NT + (k + 1))
                    eng.scalar_tensor_tensor(arg[:, k % 2, :], rows[:, b, 1, :], column(s2_all, h, k), t1[:, k % 2, :], ALU.add, ALU.max
                                             ).then_inc(s["arg_ready"], 1)

                def make_prob(k):
                    eng.wait_ge(s["e_ready"], h * NT + (k + 1))
                    eng.scalar_tensor_tensor(prob[:, k, :], ex[:, k % 2, :], 1.0, K.counts[:, k, :], ALU.min, ALU.mult
                                             ).then_inc(s["p_ready"], 1)
                make_arg(0)
                for k in range(1, NT):
                    make_arg(k)
                    make_prob(k - 1)
                make_prob(NT - 1)

            def normalise(h, b):
                eng.wait_ge(s["out_free"], h + 2)
                eng.wait_ge(s["pv_done"], h + 1)
                link(eng.tensor_scalar(rec[:, :], sums[b][:, :, ch], 1e-16, None, ALU.add))
                link(eng.reciprocal(rec[:, :], rec[:, :]))
                cols = slice(h * ch, (h + 1) * ch) if isinstance(h, int) else bass.ds(h * ch, ch)
                eng.tensor_tensor(B["g"][:, :, cols], sums[b][:, :, 0:ch], bc(rec[:, :].unsqueeze(2), [P, NT, ch]), ALU.mult
                                  ).then_inc(s["out_free"], 1)

            def step(h, b):
                if over(h, 1):
                    weights(h - 1, 1 - b)
                if over(h, 2):
                    normalise(h - 2, b)
            turns(eng, step, K.dve_chain, 4)
            weights(heads - 1, pair - 1)
            if heads > 1:
                normalise(heads - 2, 0)
                normalise(heads - 1, 1)
                eng.wait_ge(s["out_free"], heads + 2)
                finish["vector"](eng, link, s)
            else:
                finish["vector"](eng, link, s, psum)

        @block.scalar
        def _(eng):
            def current(h, b):
                if over(h, 2):
                    eng.wait_ge(s["als_ready"], h - 1)
                eng.copy(B["cur"][:, b, 0, :], of(B["al_s"], h)).then_inc(s["cs_ready"], 1)
            turns(eng, current)

            def weights(h, b):
                def make_t1(k):
                    eng.activation(t1[:, k % 2, :], rows[:, b, 0, :], ACT.Identity, bias=column(B["al_s"], h, k)).then_inc(s["t1_ready"], 1)

                def make_ex(k):
                    eng.wait_ge(s["arg_ready"], h * NT + (k + 1))
                    if k >= 2:
                        eng.wait_ge(s["p_ready"], h * NT + (k - 1))
                    eng.activation(ex[:, k % 2, :], arg[:, k % 2, :], ACT.Exp).then_inc(s["e_ready"], 1)
                eng.wait_ge(s["rows_copied"], h + 1)
                make_t1(0)
                make_t1(1)
                for k in range(2, NT):
                    make_ex(k - 2)
                    make_t1(k)
                make_ex(NT - 2)
                make_ex(NT - 1)

            def step(h, b):
                if over(h, 2):
                    eng.wait_ge(s["bc_ready"], h - 1)
                eng.copy(B["cur"][:, b, 1, :], of(u_all, h))
                eng.copy(B["cur"][:, b, 2, :], of(v_all, h)).then_inc(s["uv_ready"], 1)
                if over(h, 1):
                    weights(h - 1, 1 - b)
                eng.wait_ge(s["bc_ready"], h + 1)
                eng.copy(rows[:, b, 0, :], row(0))
                eng.copy(rows[:, b, 1, :], row(2)).then_inc(s["rows_copied"], 1)
            eng.wait_ge(s["uv_made"], 1)
            turns(eng, step)
            weights(heads - 1, pair - 1)
            finish["scalar"](eng, s)

        @block.gpsimd
        def _(eng):
            if heads > 1:
                eng.sem_inc(s["out_free"], 2)
                gather_inverse_counts(K, eng, s, T_EARLY, T1)

        @block.tensor
        def _(eng):
            def spread(bank, col):
                for i in range(NT):
                    for lo, hi, off in column_pieces(i):
                        ins = eng.matmul(flat(bank)[:, lo:hi], bc(col[:, i:i + 1], [P, 128]), K.ident[0:P, off:off + hi - lo],
                                         start=True, stop=True)
                return ins

            def spread_sources(h, b):
                if over(h, 2):
                    eng.wait_ge(s["max_done"], h - 1)
                eng.wait_ge(s["cs_ready"], h + 1)
                spread(2 * b, B["cur"][:, b, 0, :]).then_inc(s["als_ready"], 1)
            turns(eng, spread_sources)

            def multiply(h, b):
                eng.wait_ge(s["p_ready"], h * NT + NT)
                if heads > 1:
                    eng.wait_ge(s["out_free"], h + 1)
                for i in range(NT):
                    if heads == 1 and i >= 2:
                        eng.wait_ge(s["out_free"], i - 1)
                    for k in range(NT):
                        w = B["prob"][b][:, k, i * P:(i + 1) * P]
                        if heads > 1:
                            v = h_sb[:, k, h, :] if isinstance(h, int) else h_sb[:, k, bass.ds(h, 1), :].rearrange("p a c -> p (a c)")
                            ins = eng.matmul(sums[b][:, i, :], w, v, start=k == 0, stop=k == NT - 1)
                        else:
                            a = (6, 4)[i % 2]
                            eng.matmul(psum[0:P, a, 0:HC], w, h_sb[:, k, 0, 0:HC], start=k == 0, stop=k == NT - 1)
                            ins = eng.matmul(psum[0:P, a + 1, 0:HC + 1], w, h_sb[:, k, 0, HC:C + 1], start=k == 0, stop=k == NT - 1)
                    if heads == 1:
                        ins.then_inc(s["pv_done"], 1)
                if heads > 1:
                    ins.then_inc(s["pv_done"], 1)

            def step(h, b):
                if over(h, 1):
                    eng.wait_ge(s["rows_copied"], h)
                eng.wait_ge(s["uv_ready"], h + 1)
                spread(0, B["cur"][:, b, 1, :])
                spread(2, B["cur"][:, b, 2, :]).then_inc(s["bc_ready"], 1)
                if over(h, 2):
                    multiply(h - 2, b)
            turns(eng, step)
            if heads > 1:
                multiply(heads - 2, 0)
            multiply(heads - 1, pair - 1)


def gat_phase(K):
    nc, ins = K.nc, K.ins
    with ExitStack() as ctx:
        sb = lambda n, s, d: K.sb(n, s, d, ctx)
        B = {
            "xT": sb("xT", [128, 2, KC, XW], FP16), "parts": sb("parts", [P, NT, 2, C], FP16),
            "stage": sb("stage", [128, KC, C], FP32), "wparts": sb("wparts", [128, 2, KC, C], FP16),
            "a_bc": sb("a_bc", [P, 2, C], FP32), "prod": sb("prod", [P, 2, C], FP32),
            "al_s": sb("al_s", [P, HEADS, NT], FP32), "al_d": sb("al_d", [P, HEADS, NT], FP32),
            "small": sb("small", [P, 5, HEADS, NT], FP32), "cur": sb("cur", [P, 2, 3, NT], FP32),
            "max_cur": sb("max_cur", [P, 2, NT], FP32), "rec": sb("rec", [P, NT], FP32), "rows": sb("spread", [P, 2, 2, N], FP32), "bias": sb("bias", [P, C], FP32), "g": sb("g", [P, NT, C], FP32),
            "t1": sb("t1", [P, 2, N], FP32), "arg": sb("arg", [P, 2, N], FP32), "ex": sb("ex", [P, 2, N], FP32),
        }
        norm = {"stats": sb("stats", [P, NT, 2, 6], FP32), "mv": sb("mv", [P, NT, 2], FP32), "sd": sb("sd", [P, NT], FP32)}
        h1 = sb("h1", [P, NT, HEADS, HD + 1], FP32)
        h2 = h1[:, :, :, :].rearrange("p i h c -> p i (h c)")[:, :, 0:C + 1].unsqueeze(2)
        B["prob"] = [a[:, 0:NT * N].rearrange("p (k n) -> p k n", n=N) for a in (
            B["stage"][0:P, :, :].rearrange("p k n -> p (k n)"), B["parts"][:, :, :, :].bitcast(FP32).rearrange("p i a c -> p (i a c)"))]

        gat_project(K, "g1", B, B["g"], norm, ins["L0_gnn_W1"], ins["L0_gnn_a_src1"], ins["L0_gnn_a_dst1"], HEADS, HD, h1)

        def elu_vector(eng, link, s):
            g, t = B["g"], h1[:, :, :, :].rearrange("p i h c -> p (i h c)")[:, 0:NT * C].rearrange("p (i c) -> p i c", c=C)
            eng.wait_ge(s["bias_loaded"], 16)
            for i in range(NT + 1):
                if i < NT:
                    link(eng.tensor_tensor(g[:, i, :], g[:, i, :], B["bias"][:, :], ALU.add))
                    eng.tensor_scalar(t[:, i, :], g[:, i, :], 0.0, None, ALU.min).then_inc(s["finish_a"], 1)
                if i:
                    eng.wait_ge(s["finish_b"], i)
                    link(eng.scalar_tensor_tensor(t[:, i - 1, :], g[:, i - 1, :], 0.0, t[:, i - 1, :], ALU.max, ALU.add))
                    eng.tensor_scalar(g[:, i - 1, :], t[:, i - 1, :], 1.0, None, ALU.subtract)

        def elu_scalar(eng, s):
            t = h1[:, :, :, :].rearrange("p i h c -> p (i h c)")
            for i in range(NT):
                eng.wait_ge(s["finish_a"], i + 1)
                eng.activation(t[:, i * C:(i + 1) * C], t[:, i * C:(i + 1) * C], ACT.Exp).then_inc(s["finish_b"], 1)

        gat_attend(K, "a1", B, HEADS, HD, h1, {"bias": ins["L0_gnn_b1"], "vector": elu_vector, "scalar": elu_scalar})
        gat_project(K, "g2", B, B["g"], None, ins["L0_gnn_W2"], ins["L0_gnn_a_src2"], ins["L0_gnn_a_dst2"], 1, C, h2)

        def residual(eng, link, s, psum):
            rec = B["rec"]
            eng.wait_ge(s["bias_loaded"], 16)
            link(eng.tensor_tensor(K.x[:, :, :], K.x[:, :, :], bc(B["bias"][:, :].unsqueeze(1), [P, NT, C]), ALU.add))
            for i in range(NT):
                b = (6, 4)[i % 2]
                eng.wait_ge(s["pv_done"], i + 1)
                link(eng.tensor_scalar(rec[:, i:i + 1], psum[0:P, b + 1, HC:HC + 1], 1e-16, None, ALU.add))
                link(eng.reciprocal(rec[:, i:i + 1], rec[:, i:i + 1]))
                for h in range(2):
                    xs = K.x[:, i, h * HC:(h + 1) * HC]
                    last = eng.scalar_tensor_tensor(xs, psum[0:P, b + h, 0:HC], rec[:, i:i + 1], xs, ALU.mult, ALU.add)
                last.then_inc(s["out_free"], 1)

        gat_attend(K, "a2", B, 1, C, h2, {"bias": ins["L0_gnn_b2"], "vector": residual, "scalar": lambda eng, s: None})


def ffn_phase(K, layer):
    nc, ins = K.nc, K.ins
    L = "L%d_ffn_" % layer
    CH, CW = KC, EXP * F
    NR = EXP if layer == 0 else EXP + 24 + 1
    PR = 24
    with ExitStack() as ctx:
        sb = lambda n, s, d: K.sb("f%d_%s" % (layer, n), s, d, ctx)
        xT = sb("xT", [128, 2, KC, XW], FP16)
        rows = sb("parts", [128, NT * 2 * C], FP16)
        parts = rows[0:P, :].rearrange("p (i a c) -> p i a c", i=NT, a=2)
        per = 1 + 2 * layer
        stage = sb("stage", [128, (4, 2)[layer] * per, CW], FP32)
        base = (2, 0)[layer]
        first_chunk = CH * layer
        w_all = sb("wparts", [128, 2, 2 * CH - first_chunk, CW], FP16)
        w_up = K.ring[:, :].rearrange("p (a k n) -> p a k n", a=2, k=CH) if layer == 1 else w_all[:, :, 0:CH, :]
        w_down = w_all[:, :, CH - first_chunk:2 * CH - first_chunk, :]
        xn = w_down[0:P, 1, CH - NT:CH, :].bitcast(FP32)
        norm = {"stats": sb("stats", [P, NT, 2, 6], FP32), "mv": sb("mv", [P, NT, 2], FP32), "sd": sb("sd", [P, NT], FP32)}
        early = sb("early", [128, FT * XW], FP16)
        rw = early[0:NR, 0:2 * C].bitcast(FP32)
        b2 = early[0:EXP, 2 * C:4 * C].bitcast(FP32)
        wTf = early[0:EXP, 4 * C:4 * C + 2 * N].bitcast(FP32)
        rT = sb("rT", [128, 2, KC, NR], FP16)
        lg = sb("lg", [P, NT, NR], FP32)
        m8 = sb("m8", [P, NT, 8], FP32)
        i8 = sb("i8", [P, NT, 8], mybir.dt.uint32)
        fidx = sb("fidx", [P, NT, 8], FP32)
        wk = sb("wk", [P, NT, 2], FP32)
        wt = sb("wt", [P, 2, NT, EXP], FP32)
        iota8 = sb("iota8", [P, EXP], FP32)
        sel = sb("sel", [EXP, CW], FP16)
        wT = sb("wT", [EXP, 2, XW], FP16)
        b1 = sb("b1", [128, FT], FP32)
        b2p = sb("b2p", [EXP, 2, C], FP16)
        if layer == 1:
            mg2 = sb("mg2", [128, FT], FP32)
            emb = sb("emb", [P, EXP, PR], FP32)
            en = sb("en", [P, EXP, 4], FP32)
            pr = sb("pr", [P, NT, EXP, PR], FP32)
            tok = sb("tok", [P, NT, 4], FP32)
            al = sb("al", [P, NT, EXP], FP32)

        psum_ctx = ExitStack()
        psum = K.pb("f%d_ps" % layer, [128, 8, 512], FP32, psum_ctx)
        pT = [psum[:, 4 + 2 * b:6 + 2 * b, :].bitcast(FP16) for b in range(2)]
        T = Transposed(K, "f%d_t" % layer, xn, xT, parts, pT, norm)
        s = {n: K.sem("f%d_%s" % (layer, n)) for n in (
            "router_loaded", "small_loaded", "pool_ready", "rt_ready", "rt_hi", "rt_lo", "logits_ready", "diff_ready", "exp_ready", "norm_ready",
            "root_ready", "gates_ready", "gates_transposed", "w_hi", "w_lo")}
        s_up = [K.sem("f%d_up_chunk%d" % (layer, c)) for c in range(4)]
        s_down = [K.sem("f%d_down_chunk%d" % (layer, c)) for c in range(2)]
        w1 = lambda n: ins[L + n].rearrange("e (k p) f -> p k e f", p=128)
        w2 = lambda n: ins[L + n].rearrange("e f c -> (e f) c").rearrange("(k t p) c -> p k t c", p=128, t=2)
        names = ("w2",) if layer == 0 else ("w_fast2", "w_slow2", "h_fast2")
        block = psum_ctx.enter_context(nc.Block())

        def load_up(eng, c):
            eng.dma_start(stage[:, c % 4, :].rearrange("p (e f) -> p e f", f=F), w1("w1")[:, c, :, :]).then_inc(s_up[c % 4], 16)

        def load_down(eng, c):
            for a, name in enumerate(names):
                st = stage[:, (base + c % 2) * per + a, :].rearrange("p (e f) -> p e f", f=C)
                eng.dma_start(st, w2(name)[:, c, :, :]).then_inc(s_down[c % 2], 16)

        @block.sync
        def _(eng):
            eng.dma_start(rw[0:EXP, :], ins[L + "router_w"]).then_inc(s["router_loaded"], 16)
            if layer == 1:
                eng.dma_start(rw[EXP:EXP + PR, :], ins[L + "probe_w"]).then_inc(s["router_loaded"], 16)
            with nc.allow_non_contiguous_dma("a bias to a column per hidden tile"):
                eng.dma_start(b1[:, :], ins[L + "b1"].rearrange("e f -> (e f)").rearrange("(t p) -> p t", p=128)).then_inc(s["small_loaded"], 16)
            eng.dma_start(b2[:, :], ins[L + "b2"]).then_inc(s["small_loaded"], 16)
            if layer == 1:
                even = ins[L + "m_gate2"].rearrange("(a b) -> a b", b=2)
                with nc.allow_non_contiguous_dma("a few gates"):
                    for p0, p1, first, which in ((0, 128, 0, 0), (0, 64, 1, 0), (64, 128, 1, 1), (0, 128, 2, 1)):
                        eng.dma_start(mg2[p0:p1, first::3], even[:, which].partition_broadcast(p1 - p0)).then_inc(s["small_loaded"], 16)
                    eng.dma_start(en[:, :, 0], ins[L + "energy"].partition_broadcast(P)).then_inc(s["small_loaded"], 16)
                    eng.dma_start(en[:, :, 1], ins[L + "fatigue"].partition_broadcast(P)).then_inc(s["small_loaded"], 16)
                eng.dma_start(emb[:, :, :], ins[L + "router_emb"].partition_broadcast(P)).then_inc(s["small_loaded"], 16)
            if layer == 0:
                for c in range(CH):
                    if c >= 4:
                        eng.wait_ge(s["w_lo"], c - 3)
                    load_up(eng, c)
                eng.wait_ge(s["w_lo"], 4)
            load_down(eng, 0), load_down(eng, 1)

        small_loads = 32 if layer == 0 else 16 * 9

        @block.gpsimd
        def _(eng):
            link = chain(eng, K.pool_chain)
            eng.iota(iota8[:, :], pattern=[[1, EXP]], base=0, channel_multiplier=0, allow_small_or_imprecise_dtypes=True
                     ).then_inc(s["pool_ready"], 1)
            if layer == 1:
                eng.wait_ge(s["pool_ready"], 1)
                eng.memset(rw[NR - 1:NR, :], 1.0).then_inc(s["pool_ready"], 1)
            eng.wait_ge(s["pool_ready"], 1 + layer)
            link(eng.memset(sel[:, :], 1.0))
            link(eng.affine_select(out=sel[:, :], in_=sel[:, :], compare_op=ALU.is_ge, fill=0.0, base=0,
                                   pattern=[[1, CW]], channel_multiplier=-F))
            eng.affine_select(out=sel[:, :], in_=sel[:, :], compare_op=ALU.is_ge, fill=0.0, base=F - 1,
                              pattern=[[-1, CW]], channel_multiplier=F).then_inc(s["pool_ready"], 1)

        pool_ready = 2 if layer == 0 else 3

        @block.vector
        def _(eng):
            link = chain(eng, K.dve_chain)

            def cut(c):
                eng.wait_ge(s["w_hi"], c + 1)
                eng.scalar_tensor_tensor(w_all[:, 1, c, :], stage[:, c % 4, :], W_SCALE, w_all[:, 0, c, :], ALU.mult, ALU.subtract
                                         ).then_inc(s["w_lo"], 1)

            T.vector(eng)
            eng.wait_ge(s["rt_hi"], 1)
            rps = psum[:, 0, 0:KC * NR].rearrange("p (k r) -> p k r", r=NR)
            eng.scalar_tensor_tensor(rT[:, 1, :, :], rps, W_SCALE, rT[:, 0, :, :], ALU.mult, ALU.subtract).then_inc(s["rt_lo"], 1)
            eng.wait_ge(s["small_loaded"], small_loads)
            link(eng.tensor_scalar(b2p[:, 0, :], b2[:, :], W_SCALE, None, ALU.mult))
            link(eng.scalar_tensor_tensor(b2p[:, 1, :], b2[:, :], W_SCALE, b2p[:, 0, :], ALU.mult, ALU.subtract))
            if layer == 1:
                link(eng.tensor_tensor(pr[:, 0, :, :], emb[:, :, :], emb[:, :, :], ALU.mult))
                eng.tensor_reduce(en[:, :, 2], pr[:, 0, :, :], AX.X, ALU.add).then_inc(s["norm_ready"], 1)
                eng.wait_ge(s["root_ready"], 1)
                link(eng.tensor_scalar(en[:, :, 3], en[:, :, 2], 1e-12, None, ALU.max))
                link(eng.reciprocal(en[:, :, 3], en[:, :, 3]))
                link(eng.tensor_tensor(emb[:, :, :], emb[:, :, :], bc(en[:, :, 3].unsqueeze(2), [P, EXP, PR]), ALU.mult))
                link(eng.tensor_scalar(en[:, :, 0:2], en[:, :, 0:2], 0.1, None, ALU.mult))
            if layer == 0:
                cut(0), cut(1)
            eng.wait_ge(s["logits_ready"], 1)
            link(eng.tensor_scalar(lg[:, :, :], psum[0:P, 1, 0:NT * NR].rearrange("p (i r) -> p i r", r=NR), 1.0 / W_SCALE, None, ALU.mult))
            eng.wait_ge(s["pool_ready"], pool_ready)
            logit = lg[:, :, 0:EXP]
            if layer == 1:
                probe = lg[:, :, EXP:EXP + PR]
                squares = pr[:, :, 0, :]
                link(eng.tensor_tensor(squares, probe, probe, ALU.mult))
                eng.tensor_reduce(tok[:, :, 1], squares, AX.X, ALU.add).then_inc(s["norm_ready"], 1)
                eng.wait_ge(s["root_ready"], 2)
                link(eng.tensor_scalar(tok[:, :, 1], tok[:, :, 1], 1e-12, None, ALU.max))
                link(eng.reciprocal(tok[:, :, 1], tok[:, :, 1]))
                link(eng.tensor_tensor(probe, probe, bc(tok[:, :, 1:2], [P, NT, PR]), ALU.mult))
                for i in range(NT):
                    last = eng.tensor_tensor(pr[:, i, :, :], emb[:, :, :], bc(lg[:, i, EXP:EXP + PR].unsqueeze(1), [P, EXP, PR]), ALU.mult)
                link(last)
                link(eng.tensor_reduce(al[:, :, :].rearrange("p i e -> p (i e)"), pr[:, :, :, :].rearrange("p i e d -> p (i e) d"), AX.X, ALU.add))
                link(eng.tensor_scalar(tok[:, :, 2], lg[:, :, NR - 1], 0.02 / C, None, ALU.mult))
                link(eng.tensor_tensor(logit, logit, bc(tok[:, :, 2:3], [P, NT, EXP]), ALU.add))
                for i in range(NT):
                    last = eng.scalar_tensor_tensor(logit[:, i, :], en[:, :, 2], tok[:, i, 2:3], logit[:, i, :], ALU.mult, ALU.add)
                link(last)
                link(eng.scalar_tensor_tensor(logit, al[:, :, :], 0.02, logit, ALU.mult, ALU.add))
                link(eng.tensor_tensor(logit, logit, bc(en[:, :, 0].unsqueeze(1), [P, NT, EXP]), ALU.add))
                link(eng.tensor_tensor(logit, logit, bc(en[:, :, 1].unsqueeze(1), [P, NT, EXP]), ALU.subtract))
            for i in range(NT):
                last = eng.max(m8[:, i, :], logit[:, i, :])
            link(last)
            for i in range(NT):
                last = eng.max_index(i8[:, i, :], m8[:, i, :], logit[:, i, :])
            link(last)
            link(eng.tensor_copy(fidx[:, :, :], i8[:, :, :]))
            eng.tensor_tensor(wk[:, :, 1], m8[:, :, 1], m8[:, :, 0], ALU.subtract).then_inc(s["diff_ready"], 1)
            eng.wait_ge(s["exp_ready"], 1)
            link(eng.tensor_scalar(wk[:, :, 0], wk[:, :, 1], 1.0, None, ALU.add))
            link(eng.reciprocal(wk[:, :, 0], wk[:, :, 0]))
            link(eng.tensor_tensor(wk[:, :, 1], wk[:, :, 1], wk[:, :, 0], ALU.mult))
            for a in range(2):
                w = wt[:, a, :, :]
                link(eng.tensor_tensor(w, bc(iota8[:, :].unsqueeze(1), [P, NT, EXP]), bc(fidx[:, :, a:a + 1], [P, NT, EXP]), ALU.is_equal))
                link(eng.tensor_tensor(w, w, bc(wk[:, :, a:a + 1], [P, NT, EXP]), ALU.mult))
            eng.tensor_tensor(wt[:, 0, :, :], wt[:, 0, :, :], wt[:, 1, :, :], ALU.add).then_inc(s["gates_ready"], 1)
            eng.wait_ge(s["gates_transposed"], 1)
            link(eng.tensor_copy(wTf[:, :], psum[0:EXP, 2:4, :].rearrange("p b n -> p (b n)")[:, 0:N]))
            link(eng.memset(wT[:, :, N:XW], 0.0))
            link(eng.tensor_copy(wT[:, 0, 0:N], wTf[:, :]))
            link(eng.tensor_tensor(wT[:, 1, 0:N], wTf[:, :], wT[:, 0, 0:N], ALU.subtract))
            if layer == 0:
                for c in range(2, CH):
                    cut(c)

        @block.scalar
        def _(eng):
            def cut(c):
                eng.wait_ge(s_up[c % 4], 16 * (c // 4 + 1))
                eng.activation(w_all[:, 0, c, :], stage[:, c % 4, :], ACT.Copy, scale=W_SCALE).then_inc(s["w_hi"], 1)

            T.scalar(eng)
            eng.wait_ge(s["rt_ready"], 1)
            rps = psum[:, 0, 0:KC * NR].rearrange("p (k r) -> p k r", r=NR)
            eng.activation(rT[:, 0, :, :], rps, ACT.Copy, scale=W_SCALE).then_inc(s["rt_hi"], 1)
            if layer == 0:
                cut(0), cut(1)
            else:
                eng.wait_ge(s["norm_ready"], 1)
                eng.activation(en[:, :, 2], en[:, :, 2], ACT.Sqrt).then_inc(s["root_ready"], 1)
                eng.wait_ge(s["norm_ready"], 2)
                eng.activation(tok[:, :, 1], tok[:, :, 1], ACT.Sqrt).then_inc(s["root_ready"], 1)
            eng.wait_ge(s["diff_ready"], 1)
            eng.activation(wk[:, :, 1], wk[:, :, 1], ACT.Exp).then_inc(s["exp_ready"], 1)
            if layer == 0:
                for c in range(2, CH):
                    cut(c)

        @block.tensor
        def _(eng):
            eng.wait_ge(s["router_loaded"], 16 * (1 + layer))
            eng.wait_ge(s["pool_ready"], pool_ready)
            for k in range(KC):
                last = eng.transpose(psum[:, 0, k * NR:(k + 1) * NR], rw[:, k * 128:(k + 1) * 128], K.ident[0:NR, 0:NR])
            last.then_inc(s["rt_ready"], 1)
            T.tensor(eng)
            T.wait_done(eng)
            eng.wait_ge(s["rt_lo"], 1)
            for i in range(NT):
                tok_ = slice(i * P, (i + 1) * P)
                out = psum[0:P, 1, i * NR:(i + 1) * NR]
                for k in range(KC):
                    last = three_products(eng, [out], xT[:, 0, k, tok_], xT[:, 1, k, tok_], rT[:, 0, k, :], rT[:, 1, k, :], k == 0, k == KC - 1)
            last.then_inc(s["logits_ready"], 1)
            eng.wait_ge(s["gates_ready"], 1)
            flat = psum[0:EXP, 2:4, :].rearrange("p b n -> p (b n)")
            for i in range(NT):
                for lo, hi, off in column_pieces(i):
                    last = eng.matmul(flat[:, lo:hi], wt[:, 0, i, :], K.ident[0:P, off:off + hi - lo], start=True, stop=True)
            last.then_inc(s["gates_transposed"], 1)

        psum_ctx.close()

        with ExitStack() as main_ctx:
            psum = K.pb("f%d_mps" % layer, [128, 8, 512], FP32, main_ctx)
            tiles_of = lambda a: a[:, 0:FT * XW].rearrange("p (f n) -> p f n", f=FT)
            yv = tiles_of(sb("y_hi", [128, FT * XW], FP16) if layer == 0 else K.graph[:, :].bitcast(FP16)), tiles_of(early[:, :])
            hy = rows[:, :].bitcast(FP32)[:, 0:4 * XW].rearrange("p (a u n) -> p a u n", a=2, u=2)
            h, y = hy[:, 0], hy[:, 1]
            s = {n: K.sem("f%dm_%s" % (layer, n)) for n in ("up_ready", "up_free", "h_ready", "y_ready", "y_hi", "down_ready", "down_free", "merged", "cut_hi", "cut_lo", "stored")}
            block = main_ctx.enter_context(nc.Block())
            up = [psum[:, 2 * b:2 * b + 2, 0:HALF] for b in range(2)]
            wbc = [psum[:, 4 + 2 * b:6 + 2 * b, 0:HALF] for b in range(2)]
            halves = lambda a: a.rearrange("p (b n) -> p b n", b=2)

            per_turn = 4

            @block.sync
            def _(eng):
                for n in range(2, CH):
                    eng.wait_ge(s["cut_lo"], n - 1)
                    load_down(eng, n)
                if layer == 1:
                    for i in range(NT):
                        eng.wait_ge(s["down_free"], i + 1)
                        eng.dma_start(K.out[i * P:(i + 1) * P, :], K.x[:, i, :]).then_inc(s["stored"], 16)
                    eng.wait_ge(s["stored"], 16 * NT)

            @block.scalar
            def _(eng):
                with eng.Fori(0, FT // per_turn) as j:
                    for v in range(per_turn):
                        u, f = v % 2, j * per_turn + v
                        if u == 1:
                            slot = v // 2
                            c = j * 2 + slot
                            if layer == 1:
                                eng.wait_ge(s["merged"], c + 1)
                            else:
                                eng.wait_ge(s_down[slot], j * 16 + 16)
                            eng.activation(w_down[:, 0, bass.ds(c, 1), :].rearrange("p a n -> p (a n)"), stage[:, (base + slot) * per, :], ACT.Copy,
                                           scale=W_SCALE).then_inc(s["cut_hi"], 1)
                        eng.wait_ge(s["up_ready"], f + 1)
                        eng.activation(halves(h[:, u, :]), up[u], ACT.Gelu if layer == 0 else ACT.Relu,
                                       bias=b1[:, bass.ds(f, 1)], scale=1.0 / W_SCALE).then_inc(s["h_ready"], 1)
                        eng.wait_ge(s["y_ready"], f + 1)
                        eng.activation(yv[0][:, bass.ds(f, 1), :].rearrange("p a n -> p (a n)"), y[:, u, :], ACT.Copy).then_inc(s["y_hi"], 1)

            @block.vector
            def _(eng):
                link = chain(eng, K.dve_chain)

                def merge(c, slot):
                    eng.wait_ge(s_down[slot], (c - slot) * (8 * per) + 16 * per)
                    a, b, h_ = (stage[:, slot * per + n, :] for n in range(3))
                    for t in range(2):
                        cols = slice(t * C, (t + 1) * C)
                        last = eng.scalar_tensor_tensor(a[:, cols], b[:, cols], mg2[:, bass.ds(c * 2 + t, 1)], a[:, cols], ALU.mult, ALU.add)
                    link(last)
                    eng.tensor_tensor(a, a, h_, ALU.add).then_inc(s["merged"], 1)

                def cut_lo(c, slot):
                    part = [w_down[:, a, bass.ds(c, 1), :].rearrange("p a n -> p (a n)") for a in range(2)]
                    eng.wait_ge(s["cut_hi"], c + 1)
                    eng.scalar_tensor_tensor(part[1], stage[:, (base + slot) * per, :], W_SCALE, part[0], ALU.mult, ALU.subtract).then_inc(s["cut_lo"], 1)

                with eng.Fori(0, FT // per_turn) as j:
                    with K.dve_chain.loop(j, 6 if layer else 0, FT // per_turn):
                        for v in range(per_turn):
                            u, f = v % 2, j * per_turn + v
                            if u == 1:
                                cut_lo(j * 2 + v // 2, v // 2)
                            elif layer == 1:
                                merge(j * 2 + v // 2, v // 2)
                            eng.wait_ge(s["h_ready"], f + 1)
                            if layer == 1:
                                link(eng.tensor_tensor(h[:, u, :], h[:, u, :], h[:, u, :], ALU.mult))
                            eng.tensor_tensor(halves(y[:, u, :]), halves(h[:, u, :]), wbc[u], ALU.mult).then_inc(s["y_ready"], 1)
                            eng.wait_ge(s["y_hi"], f + 1)
                            eng.tensor_tensor(yv[1][:, bass.ds(f, 1), :].rearrange("p a n -> p (a n)"), y[:, u, :],
                                              yv[0][:, bass.ds(f, 1), :].rearrange("p a n -> p (a n)"), ALU.subtract).then_inc(s["up_free"], 1)
                for i in range(NT):
                    eng.wait_ge(s["down_ready"], i + 1)
                    for hh in range(2):
                        xs = K.x[:, i, hh * HC:(hh + 1) * HC]
                        last = eng.scalar_tensor_tensor(xs, psum[0:P, 2 * (i % 2) + hh, 0:HC], 1.0 / W_SCALE, xs, ALU.mult, ALU.add)
                    last.then_inc(s["down_free"], 1)

            @block.gpsimd
            def _(eng):
                eng.sem_inc(s["up_free"], 2)

            @block.tensor
            def _(eng):
                with eng.Fori(0, FT // 2) as j:
                    for u in range(2):
                        f = j * 2 + u
                        eng.wait_ge(s["up_free"], f + 1)
                        for a in range(2):
                            for hh in range(2):
                                eng.matmul(wbc[u][:, hh, :], sel[:, bass.ds(f * 128, 128)], wT[:, a, hh * HALF:(hh + 1) * HALF],
                                           start=a == 0, stop=a == 1)
                        for k in range(KC):
                            for wa, xs in ((0, (0, 1)), (1, (0,))):
                                w = w_up[:, wa, k, bass.ds(f * 128, 128)]
                                for xa in xs:
                                    for hh in range(2):
                                        last = eng.matmul(up[u][:, hh, :], w, xT[:, xa, k, hh * HALF:(hh + 1) * HALF],
                                                          start=k == 0 and wa == 0 and xa == 0, stop=k == KC - 1 and wa == 1)
                        last.then_inc(s["up_ready"], 1)
                eng.wait_ge(s["up_free"], FT + 2)
                eng.wait_ge(s["cut_lo"], CH)
                for i in range(NT):
                    if i >= 2:
                        eng.wait_ge(s["down_free"], i - 1)
                    tok_ = slice(i * P, (i + 1) * P)
                    outs = [psum[0:P, 2 * (i % 2) + hh, 0:HC] for hh in range(2)]
                    three_products(eng, outs, wT[:, 0, tok_], wT[:, 1, tok_], b2p[:, 0, :], b2p[:, 1, :], True, False)
                    for f in range(FT):
                        c, o = f // 2, (f % 2) * C
                        last = three_products(eng, outs, yv[0][:, f, tok_], yv[1][:, f, tok_], w_down[:, 0, c, o:o + C], w_down[:, 1, c, o:o + C],
                                              False, f == FT - 1)
                    last.then_inc(s["down_ready"], 1)


def ffn0_phase(K):
    ffn_phase(K, 0)


def ffn1_phase(K):
    ffn_phase(K, 1)


def project_block(K, name, src, norm, xT, parts, W, out, sync=None, vector=None, merged=None, beside=None):
    with ExitStack() as ctx:
        psum = K.pb(name + "_ps", [128, 8, 512], FP32, ctx)
        pT = [psum[:, 4 + 2 * b:6 + 2 * b, :].bitcast(FP16) for b in range(2)]
        pO = [psum[:, 2 * b:2 * b + 2, :] for b in range(2)]
        T = Transposed(K, name + "_t", src, xT, parts, pT, norm)
        s = {n: K.sem(name + "_" + n) for n in ("projected", "out_ready", "extra")}
        block = ctx.enter_context(K.nc.Block())

        @block.sync
        def _(eng):
            if merged:
                merged.sync(eng)
            else:
                W.sync(eng)
                beside.sync(eng)
            if sync:
                sync(eng, T, s)

        if merged:
            @block.gpsimd
            def _(eng):
                merged.gpsimd(eng, 0, MERGE_EARLY)

        @block.vector
        def _(eng):
            link = chain(eng, K.dve_chain)
            T.vector(eng)
            if merged:
                for c in range(MERGE_EARLY):
                    merged.add(eng, link, c)
                    merged.cut_lo(eng, c)
            else:
                W.vector(eng)
                beside.vector(eng)
            if vector:
                vector(eng, link, s)

        @block.scalar
        def _(eng):
            T.scalar(eng)
            if not merged:
                W.scalar(eng)
                beside.scalar(eng)
            for i in range(NT):
                if merged:
                    for c in range(i * MERGE_EARLY // NT, (i + 1) * MERGE_EARLY // NT):
                        merged.scalar(eng, c)
                eng.wait_ge(s["projected"], i + 1)
                for b in range(2):
                    last = eng.activation(out[:, i, b * HC:(b + 1) * HC], pO[i % 2][0:P, b, 0:HC], ACT.Copy, scale=1.0 / W_SCALE)
                last.then_inc(s["out_ready"], 1)

        @block.tensor
        def _(eng):
            T.tensor(eng)
            T.wait_done(eng)
            project_tiles(eng, pO, xT, W, lambda i: None, s["projected"], s["out_ready"])


MERGE_CHUNKS = KC
MERGE_EARLY = MERGE_CHUNKS - 2


class MergedFirst:

    def __init__(self, K, stage):
        self.K, self.stage = K, stage
        self.parts = K.ring[:, :].rearrange("p (a k n) -> p a k n", a=2, k=MERGE_CHUNKS)
        self.s_loaded = [K.sem("m_loaded%d" % u) for u in range(2)]
        self.s_gate, self.s_scaled, self.s_merged, self.s_hi, self.s_lo = (K.sem("m_" + n) for n in ("gate", "scaled", "merged", "hi", "lo"))

    def load(self, eng, c):
        for a, name in enumerate(("w_fast1", "w_slow1", "h_fast1")):
            src = self.K.ins["L1_ffn_" + name].rearrange("e (k p) f -> p k e f", p=128)[:, c, :, :]
            eng.dma_start(self.slot(c)[:, a, :].rearrange("p (e f) -> p e f", f=F), src).then_inc(self.s_loaded[c % 2], 16)

    def slot(self, c):
        return self.stage[:, (c + 1) % 2, :, :]

    def early(self, eng, W):
        eng.dma_start(self.K.gate1[:, :], self.K.ins["L1_ffn_m_gate1"].partition_broadcast(128)).then_inc(self.s_gate, 16)
        self.load(eng, 0)
        W.ready(eng, KC - 1)
        self.load(eng, 1)

    def sync(self, eng):
        for c in range(2, MERGE_CHUNKS):
            eng.wait_ge(self.s_lo, c - 1)
            self.load(eng, c)

    def gpsimd(self, eng, start, end):
        eng.wait_ge(self.s_gate, 16)
        for c in range(start, end):
            slow = self.slot(c)[:, 1, :].rearrange("p (e f) -> p e f", f=F)
            eng.wait_ge(self.s_loaded[c % 2], 48 * (c // 2 + 1))
            eng.tensor_tensor(slow, slow, bc(self.K.gate1[:, :].unsqueeze(2), [128, EXP, F]), ALU.mult).then_inc(self.s_scaled, 1)

    def add(self, eng, link, c):
        w, slow, fast2 = (self.slot(c)[:, a, :] for a in range(3))
        eng.wait_ge(self.s_loaded[c % 2], 48 * (c // 2 + 1))
        link(eng.tensor_tensor(w, w, fast2, ALU.add))
        eng.wait_ge(self.s_scaled, c + 1)
        eng.tensor_tensor(w, w, slow, ALU.add).then_inc(self.s_merged, 1)

    def cut_lo(self, eng, c):
        eng.wait_ge(self.s_hi, c + 1)
        eng.scalar_tensor_tensor(self.parts[:, 1, c, :], self.slot(c)[:, 0, :], W_SCALE, self.parts[:, 0, c, :], ALU.mult, ALU.subtract
                                 ).then_inc(self.s_lo, 1)

    def scalar(self, eng, c):
        eng.wait_ge(self.s_merged, c + 1)
        eng.activation(self.parts[:, 0, c, :], self.slot(c)[:, 0, :], ACT.Copy, scale=W_SCALE).then_inc(self.s_hi, 1)


def relation_phase(K, wstage, wring):
    nc, ins = K.nc, K.ins
    w_rel = ins["L1_gnn_W_rel"]
    with ExitStack() as ctx:
        sb = lambda n, s, d: K.sb(n, s, d, ctx)
        rows = sb("r_rows", [128, UN, 2 * C], FP16)
        rowsT = sb("r_rowsT", [128, 2, 2, KC, 128], FP16)
        msg = sb("r_msg", [128, UN, 2, C], FP16)
        gcol = sb("r_gcol", [128, UN], I32)
        scol = sb("r_scol", [128, UN], I32)
        pT = [K.pb("r_pT%d" % b, [128, 2, 1024], FP16, ctx) for b in range(2)]
        pO = [K.pb("r_pO%d" % b, [128, 2, 512], FP32, ctx) for b in range(2)]
        s = {n: K.sem("r_" + n) for n in ("staged_0", "staged_1", "w_hi", "w_lo", "col_ready", "scol_ready", "transposed", "copied", "multiplied",
                                          "msg_hi", "msg_ready")}
        gathered = [K.sem("r_gathered%d" % u) for u in range(UN)]
        scattered = [K.sem("r_scattered%d" % u) for u in range(UN)]
        block = ctx.enter_context(nc.Block())

        def load_w(eng, r, u):
            eng.dma_start(wstage[:, u, :, :], w_rel[r].rearrange("(k p) n -> p k n", p=128) if isinstance(r, int) else
                          w_rel[bass.ds(r, 1), :, :].rearrange("a (k p) n -> p (a k) n", p=128)).then_inc(s["staged_%d" % u], 16)

        @block.sync
        def _(eng):
            for b in range(AHEAD):
                eng.wait_ge(gathered[b], 16)
            load_w(eng, 1, 1)
            with eng.Fori(1, REL // 2) as i:
                for u in range(2):
                    eng.wait_ge(s["w_lo"], i * 2 + (u - 1))
                    load_w(eng, i * 2 + u, u)

        def live_turns(eng, step):
            with eng.Fori(1, TURNS) as i:
                live = eng.value_load(K.live_row[0:1, bass.ds(i, 1)], min_val=0, max_val=1)
                with eng.If(live == 1):
                    for u in range(UN):
                        step(i * UN + u, u, False)

        def col(a, t):
            return a[:, t:t + 1] if isinstance(t, int) else a[:, bass.ds(t, 1)]

        @block.gpsimd
        def _(eng):
            def gather(t, b):
                eng.tensor_copy(gcol[:, b:b + 1], col(K.slot_src, t)).then_inc(s["col_ready"], 1)
                eng.wait_ge(s["col_ready"], t + 1)
                eng.nop(nofuse=True)
                eng.indirect_dma_start(out=rows[:, b, :], out_offset=None, in_=K.xn_dram,
                                       in_offset=bass.IndirectOffsetOnAxis(ap=gcol[:, b:b + 1], axis=0)).then_inc(gathered[b], 16)

            def step(t, u, first):
                b = (u + AHEAD) % UN
                if not (first and u < UN - AHEAD):
                    eng.wait_ge(s["transposed"], t + (AHEAD - UN + 1))
                gather(t + AHEAD, b)
                if not first:
                    eng.wait_ge(scattered[u], (t - u) * (16 // UN))
                eng.tensor_copy(scol[:, u:u + 1], col(K.slot_row, t)).then_inc(s["scol_ready"], 1)
                eng.wait_ge(s["scol_ready"], t + 1)
                eng.nop(nofuse=True)
                eng.wait_ge(s["msg_ready"], t + 1)
                eng.nop(nofuse=True)
                eng.indirect_dma_start(out=K.msg_dram, out_offset=bass.IndirectOffsetOnAxis(ap=scol[:, u:u + 1], axis=0),
                                       in_=msg[:, u, :, :].rearrange("p a c -> p (a c)"), in_offset=None,
                                       bounds_check=E_EDGES - 1, oob_is_err=False).then_inc(scattered[u], 16)
            eng.sem_inc(s["w_hi"], KC)
            eng.sem_inc(s["w_lo"], 1)
            for b in range(AHEAD):
                gather(b, b)
            for u in range(UN):
                step(u, u, True)
            live_turns(eng, step)
            turns = eng.value_load(K.live_row[0:1, TURNS:TURNS + 1], min_val=1, max_val=TURNS)
            for u in range(UN):
                eng.wait_ge(scattered[u], turns * 16)
            for u in range(AHEAD):
                eng.wait_ge(gathered[u], turns * 16 + 16)
            eng.nop(nofuse=True)

        @block.scalar
        def _(eng):
            def cut(r, base, slot):
                for k in range(KC):
                    eng.activation(wring[:, slot, 0, k, :], wstage[:, slot, k, :], ACT.Copy, scale=W_SCALE).then_inc(s["w_hi"], 1)

            def step(t, u, first):
                flag = eng.value_load(K.first_row[0:1, t:t + 1] if isinstance(t, int) else K.first_row[0:1, bass.ds(t, 1)], min_val=0, max_val=2)
                for slot in range(2):
                    with eng.If(flag == slot + 1):
                        rel = eng.value_load(K.rel_row[0:1, t:t + 1] if isinstance(t, int) else K.rel_row[0:1, bass.ds(t, 1)], min_val=0, max_val=REL - 1)
                        eng.wait_ge(s["staged_%d" % slot], (rel + (1 + slot)) * 8)
                        eng.nop(nofuse=True)
                        if not (first and u == 0):
                            eng.wait_ge(s["multiplied"], t)
                            eng.nop(nofuse=True)
                        cut(None, None, slot)
                eng.wait_ge(s["multiplied"], t + 1)
                if not first:
                    eng.wait_ge(scattered[u], (t - u) * (16 // UN))
                for h in range(2):
                    last = eng.activation(msg[:, u, 0, h * HC:(h + 1) * HC], pO[u % 2][:, h, 0:HC], ACT.Copy,
                                          scale=col(K.slot_inv, t + IDX_BUFS))
                last.then_inc(s["msg_hi"], 1)
            for u in range(UN):
                step(u, u, True)
            live_turns(eng, step)

        @block.vector
        def _(eng):
            def cut(slot, hi_from):
                for k in range(KC):
                    eng.wait_ge(s["w_hi"], hi_from + (k + 1))
                    ins_ = eng.scalar_tensor_tensor(wring[:, slot, 1, k, :], wstage[:, slot, k, :], W_SCALE, wring[:, slot, 0, k, :],
                                                    ALU.mult, ALU.subtract)
                ins_.then_inc(s["w_lo"], 1)

            def copy_rows(t, b, free):
                eng.wait_ge(s["transposed"], t + 1)
                if free:
                    eng.wait_ge(s["multiplied"], t - 1)
                    eng.nop(nofuse=True)
                    eng.wait_ge(s["transposed"], t + 1)
                eng.tensor_copy(rowsT[:, b, :, :, :].rearrange("p a k n -> p a (k n)"), pT[b][:, :, 0:C]).then_inc(s["copied"], 1)

            copy_rows(0, 0, False)

            def step(t, u, first):
                copy_rows(t + 1, (u + 1) % 2, not (first and u == 0))
                flag = eng.value_load(K.first_row[0:1, t:t + 1] if isinstance(t, int) else K.first_row[0:1, bass.ds(t, 1)], min_val=0, max_val=2)
                for slot in range(2):
                    with eng.If(flag == slot + 1):
                        rel = eng.value_load(K.rel_row[0:1, t:t + 1] if isinstance(t, int) else K.rel_row[0:1, bass.ds(t, 1)], min_val=0, max_val=REL - 1)
                        cut(slot, rel * KC + KC)
                eng.wait_ge(s["msg_hi"], t + 1)
                for h in range(2):
                    last = eng.scalar_tensor_tensor(msg[:, u, 1, h * HC:(h + 1) * HC], pO[u % 2][:, h, 0:HC], col(K.slot_inv, t + IDX_BUFS),
                                                    msg[:, u, 0, h * HC:(h + 1) * HC], ALU.mult, ALU.subtract)
                last.then_inc(s["msg_ready"], 1)
            for u in range(UN):
                step(u, u, True)
            live_turns(eng, step)

        @block.tensor
        def _(eng):
            def transposes(t, b, turn, free):
                eng.wait_ge(gathered[b], turn)
                eng.nop(nofuse=True)
                if free:
                    eng.wait_ge(s["copied"], t - 1)
                for a in range(2):
                    for k in range(KC):
                        last = eng.transpose(pT[b % 2][:, a, k * 128:(k + 1) * 128], rows[:, b, a * C + k * 128:a * C + (k + 1) * 128], K.ident16[:, :])
                last.then_inc(s["transposed"], 1)

            transposes(0, 0, 16, False)

            def step(t, u, first):
                b = (u + 1) % UN
                turn = 16 * (t // UN + 1 + (u + 1) // UN) if first else (t - u) * (16 // UN) + 16 * (1 + (u + 1) // UN)
                transposes(t + 1, b, turn, not (first and u == 0))
                rel = eng.value_load(K.rel_row[0:1, t:t + 1] if isinstance(t, int) else K.rel_row[0:1, bass.ds(t, 1)], min_val=0, max_val=REL - 1)
                slot = rel % 2
                eng.wait_ge(s["w_lo"], rel + 1)
                eng.nop(nofuse=True)
                if not (first and u < 2):
                    eng.wait_ge(s["msg_ready"], t - 1)
                    eng.nop(nofuse=True)
                eng.wait_ge(s["copied"], t + 1)
                for k in range(KC):
                    w = [wring[:, bass.ds(slot, 1), a, k, :].rearrange("p s n -> p (s n)") for a in range(2)]
                    last = three_products(eng, [pO[u % 2][:, h, 0:HC] for h in range(2)], rowsT[:, u % 2, 0, k, :], rowsT[:, u % 2, 1, k, :],
                                          w[0], w[1], k == 0, k == KC - 1)
                last.then_inc(s["multiplied"], 1)
            for u in range(UN):
                step(u, u, True)
            live_turns(eng, step)


def collect_phase(K, h1, rows, W, merged):
    nc = K.nc
    with ExitStack() as ctx:
        sb = lambda n, s, d: K.sb(n, s, d, ctx)
        onehot = sb("c_onehot", [128, 2, P], FP16)
        iota_p = sb("c_iota", [128, P], FP16)
        pO = [K.pb("c_pO%d" % b, [128, 2, 512], FP32, ctx) for b in range(2)]
        s = {n: K.sem("c_" + n) for n in ("iota_ready", "onehot_ready", "multiplied", "added")}
        loaded = [K.sem("c_loaded%d" % u) for u in range(UC)]
        block = ctx.enter_context(nc.Block())

        def val(eng, table, t, top):
            return eng.value_load(table[0:1, t:t + 1] if isinstance(t, int) else table[0:1, bass.ds(t, 1)], min_val=0, max_val=top)

        @block.gpsimd
        def _(eng):
            eng.iota(iota_p[:, :], pattern=[[1, P]], base=0, channel_multiplier=0, allow_small_or_imprecise_dtypes=True).then_inc(s["iota_ready"], 1)

        @block.scalar
        def _(eng):
            W.scalar(eng)

        @block.sync
        def _(eng):
            def step(t, u, first):
                at = val(eng, K.start_row, t, E_EDGES)
                if not first:
                    eng.wait_ge(s["multiplied"], t - (UC - 1))
                eng.dma_start(rows[:, u, :, :].rearrange("p a c -> p (a c)"), K.msg_dram[bass.ds(at, 128), :]).then_inc(loaded[u], 16)
            for u in range(UC):
                step(u, u, True)
            W.sync(eng)
            with eng.Fori(1, T2 // UC) as i:
                for u in range(UC):
                    step(i * UC + u, u, False)
            merged.early(eng, W)

        @block.vector
        def _(eng):
            eng.wait_ge(s["iota_ready"], 1)

            def make(t, b, first):
                if not first:
                    eng.wait_ge(s["multiplied"], t - 1)
                c = K.slot_dst[:, t:t + 1] if isinstance(t, int) else K.slot_dst[:, bass.ds(t, 1)]
                eng.tensor_scalar(onehot[:, b, :], iota_p[:, :], c, None, ALU.is_equal).then_inc(s["onehot_ready"], 1)

            def step(t, u, first):
                bucket = val(eng, K.bucket_row, t, NT - 1)
                make(t + 1, (u + 1) % 2, first and u == 0)
                if not (first and u == 0):
                    eng.wait_ge(s["added"], t)
                    eng.nop(nofuse=True)
                eng.wait_ge(s["multiplied"], t + 1)
                eng.nop(nofuse=True)
                acc = h1[:, bass.ds(bucket, 1), :].rearrange("p a c -> p (a c)").rearrange("p (b n) -> p b n", b=2)
                eng.tensor_tensor(acc, pO[u % 2][0:P, :, 0:HC], acc, ALU.add).then_inc(s["added"], 1)
            make(0, 0, True)
            for u in range(UC):
                step(u, u, True)
            W.vector(eng)
            with eng.Fori(1, T2 // UC) as i:
                for u in range(UC):
                    step(i * UC + u, u, False)

        @block.tensor
        def _(eng):
            def step(t, u, first, turn=0):
                eng.wait_ge(loaded[u], turn * 16 + 16)
                eng.nop(nofuse=True)
                if not (first and u < 2):
                    eng.wait_ge(s["added"], t - 1)
                    eng.nop(nofuse=True)
                eng.wait_ge(s["onehot_ready"], t + 1)
                for a in range(2):
                    for h in range(2):
                        last = eng.matmul(pO[u % 2][0:P, h, 0:HC], onehot[:, u % 2, :], rows[:, u, a, h * HC:(h + 1) * HC], start=a == 0, stop=a == 1)
                last.then_inc(s["multiplied"], 1)
            for u in range(UC):
                step(u, u, True)
            with eng.Fori(1, T2 // UC) as i:
                for u in range(UC):
                    step(i * UC + u, u, False, i)


def gcn_phase(K, z, dinv, bias, merged):
    with ExitStack() as ctx:
        pO = [K.pb("n_pO%d" % b, [128, 2, 512], FP32, ctx) for b in range(2)]
        s = {n: K.sem("n_" + n) for n in ("bias_loaded", "multiplied", "added")}
        block = ctx.enter_context(K.nc.Block())

        @block.sync
        def _(eng):
            eng.dma_start(bias[:, :], K.ins["L1_gnn_b_gcn"].partition_broadcast(P)).then_inc(s["bias_loaded"], 16)

        @block.gpsimd
        def _(eng):
            merged.gpsimd(eng, MERGE_EARLY, MERGE_CHUNKS)

        @block.scalar
        def _(eng):
            for c in range(MERGE_EARLY, MERGE_CHUNKS):
                merged.scalar(eng, c)

        @block.tensor
        def _(eng):
            for i in range(NT):
                if i >= 2:
                    eng.wait_ge(s["added"], i - 1)
                for k in range(NT):
                    for h in range(2):
                        last = eng.matmul(pO[i % 2][0:P, h, 0:HC], K.counts[:, k, i * P:(i + 1) * P], z[:, k, h * HC:(h + 1) * HC],
                                          start=k == 0, stop=k == NT - 1)
                last.then_inc(s["multiplied"], 1)

        @block.vector
        def _(eng):
            link = chain(eng, K.dve_chain)
            eng.wait_ge(s["bias_loaded"], 16)
            link(eng.tensor_tensor(K.x[:, :, :], K.x[:, :, :], bc(bias[:, :].unsqueeze(1), [P, NT, C]), ALU.add))
            for i in range(NT):
                link(eng.scalar_tensor_tensor(K.x[:, i, :], z[:, i, :], dinv[:, i:i + 1], K.x[:, i, :], ALU.mult, ALU.add))
                eng.wait_ge(s["multiplied"], i + 1)
                xs = K.x[:, i, :].rearrange("p (b n) -> p b n", b=2)
                eng.scalar_tensor_tensor(xs, pO[i % 2][0:P, :, 0:HC], dinv[:, i:i + 1], xs, ALU.mult, ALU.add).then_inc(s["added"], 1)
                if i % 2 == 0 and MERGE_EARLY + i // 2 < MERGE_CHUNKS:
                    merged.add(eng, link, MERGE_EARLY + i // 2)
                    merged.cut_lo(eng, MERGE_EARLY + i // 2)


def rgcn_phase(K):
    nc, ins = K.nc, K.ins
    with ExitStack() as ctx:
        sb = lambda n, s, d: K.sb("q_" + n, s, d, ctx)
        rows = sb("parts", [128, 2 * KC * XW + NT * 2 * C], FP16)
        xT = rows[:, 0:2 * KC * XW].rearrange("p (a k n) -> p a k n", a=2, k=KC)
        parts = rows[0:P, 2 * KC * XW:].rearrange("p (i a c) -> p i a c", i=NT, a=2)
        wstage = sb("wstage", [128, 2, KC, C], FP32)
        wring = K.ring[:, :].rearrange("p (s a k n) -> p s a k n", s=2, a=2, k=KC)
        xn = sb("xn", [P, NT, C], FP32)
        h1 = sb("h1", [P, NT, C], FP32)
        bias = sb("bias", [P, C], FP32)
        dinv = sb("dinv", [P, NT], FP32)
        norm = {"stats": sb("stats", [P, NT, 2, 6], FP32), "mv": sb("mv", [P, NT, 2], FP32), "sd": sb("sd", [P, NT], FP32)}

        def store_rows(eng, T, s):
            eng.dma_start(bias[:, :], ins["L1_gnn_b_rgcn"].partition_broadcast(P)).then_inc(s["extra"], 16)
            eng.wait_ge(T.s["lo_ready"], NT)
            eng.dma_start(K.xn_dram.rearrange("(i p) c -> p i c", p=P), parts[:, :, :, :].rearrange("p i a c -> p i (a c)")).then_inc(s["extra"], 16)
            eng.wait_ge(s["extra"], 32)

        def add_bias(eng, link, s):
            eng.wait_ge(s["extra"], 32)
            for i in range(NT):
                eng.wait_ge(s["out_ready"], i + 1)
                eng.tensor_tensor(h1[:, i, :], h1[:, i, :], bias[:, :], ALU.add)

        w_root = Weights(K, "q1_w", rows_view(ins["L1_gnn_W_root"]), wstage[:, 1], wring[:, 1])
        w_first = Weights(K, "q1_r", rows_view(ins["L1_gnn_W_rel"][0]), wstage[:, 0], wring[:, 0])
        project_block(K, "q1", xn, norm, xT, parts, w_root, h1, store_rows, add_bias, beside=w_first)
        relation_phase(K, wstage, wring)
        gcn_parts = sb("gcn_parts", [128, 2, KC, C], FP16)
        w_gcn = Weights(K, "q2_w", rows_view(ins["L1_gnn_W_gcn"]), wstage[:, 0], gcn_parts)
        merged = MergedFirst(K, wstage[:, :, :, :].rearrange("p s k n -> p s (k n)").rearrange("p s (a n) -> p s a n", a=3))
        collect_phase(K, h1, rows[:, 0:UC * 2 * C].rearrange("p (u a c) -> p u a c", u=UC, a=2), w_gcn, merged)

        def degrees(eng, link, s):
            link(eng.tensor_scalar(dinv[:, :], K.deg[:, :], 1.0, None, ALU.add))
            eng.wait_ge(s["out_ready"], NT)

        project_block(K, "q2", h1, None, xT, parts, w_gcn, xn, None, degrees, merged)
        scale_phase(K, xn, dinv)
        gcn_phase(K, xn, dinv, bias, merged)


def scale_phase(K, z, dinv):
    with ExitStack() as ctx:
        s = {n: K.sem("z_" + n) for n in ("root",)}
        block = ctx.enter_context(K.nc.Block())

        @block.scalar
        def _(eng):
            eng.activation(dinv[:, :], dinv[:, :], ACT.Sqrt).then_inc(s["root"], 1)

        @block.vector
        def _(eng):
            link = chain(eng, K.dve_chain)
            eng.wait_ge(s["root"], 1)
            link(eng.reciprocal(dinv[:, :], dinv[:, :]))
            for i in range(NT):
                last = eng.tensor_scalar(z[:, i, :], z[:, i, :], dinv[:, i:i + 1], None, ALU.mult)
            link(last)


_OUTS = [((N, C), "float32")]
_INS = ["x", "src", "dst", "edge_type_34",
        "L0_gnn_W1", "L0_gnn_a_src1", "L0_gnn_a_dst1", "L0_gnn_b1", "L0_gnn_W2", "L0_gnn_a_src2", "L0_gnn_a_dst2", "L0_gnn_b2",
        "L0_ffn_router_w", "L0_ffn_w1", "L0_ffn_b1", "L0_ffn_w2", "L0_ffn_b2",
        "L1_gnn_W_rel", "L1_gnn_W_root", "L1_gnn_b_rgcn", "L1_gnn_W_gcn", "L1_gnn_b_gcn",
        "L1_ffn_router_w", "L1_ffn_probe_w", "L1_ffn_router_emb", "L1_ffn_fatigue", "L1_ffn_energy",
        "L1_ffn_w_fast1", "L1_ffn_w_slow1", "L1_ffn_h_fast1", "L1_ffn_m_gate1", "L1_ffn_b1",
        "L1_ffn_w_fast2", "L1_ffn_w_slow2", "L1_ffn_h_fast2", "L1_ffn_m_gate2", "L1_ffn_b2"]


def build(nc, ins, out):
    with ExitStack() as ctx:
        K = Core(nc, ctx, ins, out)
        K.x = K.sb("x", [P, NT, C], FP32)
        K.ident = K.sb("ident", [128, 128], FP32)
        K.ident16 = K.sb("ident16", [128, 128], FP16)
        K.zrow = K.sb("zrow", [128, 512], FP16)
        K.graph = K.sb("graph", [128, 3 * NT * N + 1], BF16)
        K.counts = K.graph[0:P, 0:2 * NT * N].bitcast(FP32).rearrange("p (i n) -> p i n", n=N)
        K.maskT = K.graph[0:P, 2 * NT * N:3 * NT * N].rearrange("p (i n) -> p i n", n=N)
        K.deg = K.sb("deg", [P, NT], FP32)
        K.slot_src = K.sb("slot_src", [128, T1 + AHEAD], I32)
        K.slot_row = K.sb("slot_row", [128, T1], I32)
        K.slot_inv = K.sb("slot_inv", [128, IDX_BUFS + T1], FP32)
        K.slot_pair = K.sb("slot_pair", [128, T1], I32)
        K.pair_col = K.sb("pair_col", [128, IDX_BUFS], I32)
        K.inv_col = K.sb("inv_col", [128, IDX_BUFS], FP32)
        K.slot_dst = K.sb("slot_dst", [128, T2 + 1], FP32)
        K.rel_row = K.sb("rel_row", [1, T1], I32)
        K.live_row = K.sb("live_row", [1, T1 // UN + 1], I32)
        K.first_row = K.sb("first_row", [1, T1], I32)
        K.bucket_row = K.sb("bucket_row", [1, T2], I32)
        K.start_row = K.sb("start_row", [1, T2], I32)
        K.qinv_dram = nc.dram_tensor("qinv_dram", (REL * N, 1), FP32).ap()
        K.msg_dram = nc.dram_tensor("msg_dram", (E_EDGES + 128, 2 * C), FP16).ap()
        K.xn_dram = nc.dram_tensor("xn_dram", (N, 2 * C), FP16).ap()
        edge_phase(K)
        K.end_phase()
        gat_phase(K)
        K.end_phase()
        ffn0_phase(K)
        K.end_phase()
        with ExitStack() as late:
            K.ring = K.sb("ring", [128, 4 * KC * C], FP16, late)
            K.gate1 = K.sb("gate1", [128, EXP], FP32, late)
            rgcn_phase(K)
            K.end_phase()
            ffn1_phase(K)
            K.end_phase()


def kernel(**inputs):
    import numpy as _np
    import concourse.bacc as _bacc
    from concourse import mybir as _mybir
    from concourse.bass_utils import run_bass_kernel_spmd as _run

    nc = _bacc.Bacc("TRN2", target_bir_lowering=False, num_devices=1)
    arrays, ins = {}, {}
    for name in _INS:
        a = _np.ascontiguousarray(inputs[name])
        arrays[f"in_{name}_dram"] = a
        ins[name] = nc.dram_tensor(f"in_{name}_dram", a.shape, _mybir.dt.from_np(a.dtype), kind="ExternalInput").ap()
    outs = []
    for i, (shape, dtype) in enumerate(_OUTS):
        dt = _mybir.dt.from_np(_np.dtype(dtype))
        outs.append(nc.dram_tensor(f"out_{i}_dram", shape, dt, kind="ExternalOutput").ap())
    build(nc, ins, outs[0])
    r = _run(nc, [arrays], core_ids=[0])
    return r.results[0]["out_0_dram"]
```
